# Optimizing a Trainium2 kernel written in Bass

```python
import numpy as np
import jax
import jax.numpy as jnp

def _softmax(x, axis=-1):
    return jax.nn.softmax(x, axis=axis)

def _gelu(x):
    return jax.nn.gelu(x, approximate=True)

def _silu(x):
    return jax.nn.silu(x)

def _sigmoid(x):
    return jax.nn.sigmoid(x)

def _layernorm(x, axis=-1, eps=1e-05):
    m = jnp.mean(x, axis=axis, keepdims=True)
    v = jnp.var(x, axis=axis, keepdims=True)
    return (x - m) / jnp.sqrt(v + eps)

def _scatter_add(tgt, idx, src, axis=0):
    return tgt.at[idx].add(src)

def _segment_sum(src, seg, n):
    return jax.ops.segment_sum(src, seg, n)
kernel_name = 'mk_decoder_preln_d2_seqx_r8_547cac'

def setup_inputs(seed: int=0):
    np.random.seed(seed)
    _w = jnp.asarray

    def _rec_inputs():
        import jax
        import jax.numpy as jnp
        _rk = jax.random.key(seed)
        x = -0.000125 + 0.9999 * jax.random.normal(jax.random.fold_in(_rk, 1), (8, 256, 256), jnp.float32)
        _lenS = 256 - jax.random.randint(jax.random.fold_in(_rk, 7), (8,), 0, max(1, 256 // 4) + 1, jnp.int32)
        _lenS2 = 64 - jax.random.randint(jax.random.fold_in(_rk, 8), (8,), 0, max(1, 64 // 4) + 1, jnp.int32)
        _ctx_2048P = jax.random.normal(jax.random.fold_in(_rk, 11), (8, 16, 256), jnp.float32)
        _ctx_2048c = jax.random.dirichlet(jax.random.fold_in(_rk, 511), 0.3 * jnp.ones((16,), jnp.float32), (8, 64))
        _ctx_2048t = jnp.einsum('bsk,bkd->bsd', _ctx_2048c, _ctx_2048P)
        _ctx_2048t = _ctx_2048t * jax.lax.rsqrt(jnp.mean(jnp.square(_ctx_2048t)) + 1e-12) * 0.953939
        ctx_2048 = 0.00222621 + 0.99962 * (_ctx_2048t + 0.3 * jax.random.normal(jax.random.fold_in(_rk, 611), (8, 64, 256), jnp.float32))
        itok_Sx4_0_63 = jax.random.randint(jax.random.fold_in(_rk, 12), (256, 4), 0, 64, jnp.int32)
        pos_BxS2 = jnp.broadcast_to(jnp.arange(64, dtype=jnp.int32), (8, 64))
        itok_BxS_4096_4607 = jax.random.randint(jax.random.fold_in(_rk, 14), (8, 256), 512, 576, jnp.int32)
        return (x, ctx_2048, itok_Sx4_0_63, pos_BxS2, itok_BxS_4096_4607)
    x, ctx_2048, itok_Sx4_0_63, pos_BxS2, itok_BxS_4096_4607 = _rec_inputs()

    def _L0_attn_setup():
        import jax, jax.numpy as jnp
        import numpy as np
        H = 16
        KVH = 4
        G = H // KVH
        HD = 128
        D = 256
        BASE = 10000.0

        def _rope(x, cos, sin):
            half = HD // 2
            x1, x2 = (x[..., :half], x[..., half:])
            return jnp.concatenate([x1 * cos - x2 * sin, x1 * sin + x2 * cos], axis=-1)
        key = jax.random.key(seed)
        ks = jax.random.split(key, 5)
        B, S = (2, 256)
        x = jax.random.normal(ks[0], (B, S, D), dtype=jnp.float32)
        Wq = jax.random.normal(ks[1], (D, H * HD), dtype=jnp.float32) * 0.02
        Wk = jax.random.normal(ks[2], (D, KVH * HD), dtype=jnp.float32) * 0.02
        Wv = jax.random.normal(ks[3], (D, KVH * HD), dtype=jnp.float32) * 0.02
        Wo = jax.random.normal(ks[4], (H * HD, D), dtype=jnp.float32) * 0.02
        return {'x': x, 'Wq': Wq, 'Wk': Wk, 'Wv': Wv, 'Wo': Wo}
    _L0_attn_all = _L0_attn_setup()
    _L0_attn_in = {k: v for k, v in _L0_attn_all.items() if k in ('Wq', 'Wk', 'Wv', 'Wo')}
    del _L0_attn_all

    def _L0_xattn_setup():
        import math
        import jax, jax.numpy as jnp
        import numpy as np
        B, S, D, N, K, TOPK = (4, 512, 256, 64, 4, 2)
        key = jax.random.key(seed)
        k0, k1, k2, k3, k4 = jax.random.split(key, 5)
        token_states = jax.random.normal(k0, (B, S, D), dtype=jnp.float32)
        set_states = jax.random.normal(k1, (B, N, D), dtype=jnp.float32)
        desc_router = jax.random.normal(k2, (N, D), dtype=jnp.float32)
        token_to_sets = jax.random.randint(k3, (S, K), 0, N)
        bound = 1.0 / math.sqrt(D)
        W_q = jax.random.uniform(k4, (D, D), jnp.float32, -bound, bound)
        b_q = jnp.zeros((D,), jnp.float32)
        return {'token_states': token_states, 'set_states': set_states, 'desc_router': desc_router, 'W_q': W_q, 'b_q': b_q, 'token_to_sets': token_to_sets}
    _L0_xattn_all = _L0_xattn_setup()
    _L0_xattn_in = {k: v for k, v in _L0_xattn_all.items() if k in ('desc_router', 'W_q', 'b_q')}
    del _L0_xattn_all

    def _L0_ffn_setup():
        import jax, jax.numpy as jnp
        import numpy as np
        TOP_K = 4
        NUM_EXPERTS = 16
        key = jax.random.key(seed)
        ks = jax.random.split(key, 6)
        B, S, H, I, E = (2, 128, 256, 224, NUM_EXPERTS)
        return {'x': jax.random.normal(ks[0], (B, S, H), dtype=jnp.float32), 'router_w': jax.random.normal(ks[1], (E, H), dtype=jnp.float32) * 0.02, 'expert_bias': jnp.zeros((E,), dtype=jnp.float32), 'gate_proj': jax.random.normal(ks[2], (E, H, I), dtype=jnp.float32) * 0.02, 'up_proj': jax.random.normal(ks[3], (E, H, I), dtype=jnp.float32) * 0.02, 'down_proj': jax.random.normal(ks[4], (E, I, H), dtype=jnp.float32) * 0.02}
    _L0_ffn_all = _L0_ffn_setup()
    _L0_ffn_in = {k: v for k, v in _L0_ffn_all.items() if k in ('router_w', 'expert_bias', 'gate_proj', 'up_proj', 'down_proj')}
    del _L0_ffn_all

    def _L1_attn_setup():
        import jax, jax.numpy as jnp
        import numpy as np
        H = 256
        HK = 16
        HV = 32
        DK = 128
        DV = 128
        KC = 4
        VE = HV // HK * DV
        B, T = (1, 64)

        def _causal_conv_silu(x, w, b):
            t = x.shape[1]
            kk = w.shape[1]
            xp = jnp.pad(x, ((0, 0), (kk - 1, 0), (0, 0)))
            y = b
            for j in range(kk):
                y = y + w[:, j] * xp[:, j:j + t, :]
            return jax.nn.silu(y)

        def _l2norm(x):
            return x / jnp.maximum(jnp.linalg.norm(x, axis=-1, keepdims=True), 1e-12)

        def _reference_tuple_inner(x, Wq, Wk, Wv, Wo, Wa, Wb, qcw, qcb, kcw, kcb, vcw, vcb):
            b, t, _ = x.shape
            q = _causal_conv_silu(x @ Wq, qcw, qcb).reshape(b, t, HK, DK)
            k = _causal_conv_silu(x @ Wk, kcw, kcb).reshape(b, t, HK, DK)
            v = _causal_conv_silu(x @ Wv, vcw, vcb).reshape(b, t, HK, VE)
            q = _l2norm(q)
            k = _l2norm(k)
            alpha = jax.nn.sigmoid(x @ Wa)
            beta = jax.nn.sigmoid(x @ Wb)
            state0 = jnp.zeros((b, HK, DK, VE), x.dtype)

            def step(state, inp):
                qt, kt, vt, at, bt = inp
                state = state * at[:, :, None, None]
                err = vt - jnp.einsum('bhkv,bhk->bhv', state, kt)
                state = state + bt[:, :, None, None] * jnp.einsum('bhk,bhv->bhkv', kt, err)
                ot = jnp.einsum('bhkv,bhk->bhv', state, qt)
                return (state, ot)
            xs = (q.transpose(1, 0, 2, 3), k.transpose(1, 0, 2, 3), v.transpose(1, 0, 2, 3), alpha.transpose(1, 0, 2), beta.transpose(1, 0, 2))
            state, outs = jax.lax.scan(step, state0, xs)
            out = outs.transpose(1, 0, 2, 3).reshape(b, t, HV * DV) @ Wo
            return (out, state)
        key = jax.random.key(seed)
        ks = jax.random.split(key, 13)
        s = 0.02

        def p(k, shape):
            return jax.random.normal(k, shape, jnp.float32) * s
        return {'x': jax.random.normal(ks[0], (B, T, H), jnp.float32), 'Wq': p(ks[1], (H, HK * DK)), 'Wk': p(ks[2], (H, HK * DK)), 'Wv': p(ks[3], (H, HV * DV)), 'Wo': p(ks[4], (HV * DV, H)), 'Wa': p(ks[5], (H, HK)), 'Wb': p(ks[6], (H, HK)), 'qcw': p(ks[7], (HK * DK, KC)), 'qcb': p(ks[8], (HK * DK,)), 'kcw': p(ks[9], (HK * DK, KC)), 'kcb': p(ks[10], (HK * DK,)), 'vcw': p(ks[11], (HV * DV, KC)), 'vcb': p(ks[12], (HV * DV,))}
    _L1_attn_all = _L1_attn_setup()
    _L1_attn_in = {k: v for k, v in _L1_attn_all.items() if k in ('Wq', 'Wk', 'Wv', 'Wo', 'Wa', 'Wb', 'qcw', 'qcb', 'kcw', 'kcb', 'vcw', 'vcb')}
    del _L1_attn_all

    def _L1_xattn_setup():
        import jax, jax.numpy as jnp
        import numpy as np
        B, CTX, DRAFT, D = (2, 512, 64, 256)
        H, KVH, HD = (16, 4, 128)
        N_REP = H // KVH
        EPS = 1e-06
        THETA = 10000.0
        SCALE = 1.0 / np.sqrt(HD).astype(np.float32)

        def _rms_norm(x, w):
            v = jnp.mean(jnp.square(x.astype(jnp.float32)), axis=-1, keepdims=True)
            return (w * (x.astype(jnp.float32) * jax.lax.rsqrt(v + EPS))).astype(x.dtype)

        def _rotate_half(x):
            x1, x2 = jnp.split(x, 2, axis=-1)
            return jnp.concatenate((-x2, x1), axis=-1)

        def _rope(x, pos):
            inv_freq = 1.0 / THETA ** (jnp.arange(0, HD, 2, dtype=jnp.float32) / HD)
            freqs = pos.astype(jnp.float32)[:, None, :, None] * inv_freq
            emb = jnp.concatenate((freqs, freqs), axis=-1)
            return x * jnp.cos(emb) + _rotate_half(x) * jnp.sin(emb)
        key = jax.random.key(seed)
        ks = jax.random.split(key, 6)
        return {'draft_hidden': jax.random.normal(ks[0], (B, DRAFT, D), jnp.float32), 'context_hidden': jax.random.normal(ks[1], (B, CTX, D), jnp.float32), 'Wq': jax.random.normal(ks[2], (H * HD, D), jnp.float32) * 0.02, 'Wk': jax.random.normal(ks[3], (KVH * HD, D), jnp.float32) * 0.02, 'Wv': jax.random.normal(ks[4], (KVH * HD, D), jnp.float32) * 0.02, 'Wo': jax.random.normal(ks[5], (D, H * HD), jnp.float32) * 0.02, 'q_norm_w': jnp.ones((HD,), jnp.float32), 'k_norm_w': jnp.ones((HD,), jnp.float32), 'context_position_ids': jnp.broadcast_to(jnp.arange(CTX, dtype=jnp.int32), (B, CTX)), 'draft_position_ids': jnp.broadcast_to(CTX + jnp.arange(DRAFT, dtype=jnp.int32), (B, DRAFT))}
    _L1_xattn_all = _L1_xattn_setup()
    _L1_xattn_in = {k: v for k, v in _L1_xattn_all.items() if k in ('Wq', 'Wk', 'Wv', 'Wo', 'q_norm_w', 'k_norm_w')}
    del _L1_xattn_all

    def _L1_ffn_setup():
        import jax, jax.numpy as jnp
        import numpy as np
        NUM_EXPERTS = 128
        NUM_KEPT = 48
        TOP_K = 8
        HIDDEN = 256
        INTER = 96
        CAP = 96
        BATCH, SEQ = (2, 128)
        key = jax.random.key(seed)
        k1, k2, k3, k4 = jax.random.split(key, 4)
        hidden_states = jax.random.normal(k1, (BATCH, SEQ, HIDDEN), jnp.float32)
        gate_weight = jax.random.normal(k2, (NUM_EXPERTS, HIDDEN), jnp.float32) * 0.02
        gate_up_proj = jax.random.normal(k3, (NUM_KEPT, 2 * INTER, HIDDEN), jnp.float32) * 0.02
        down_proj = jax.random.normal(k4, (NUM_KEPT, HIDDEN, INTER), jnp.float32) * 0.02
        o2n = -np.ones(NUM_EXPERTS, np.int32)
        o2n[np.arange(NUM_KEPT) * 2] = np.arange(NUM_KEPT, dtype=np.int32)
        old_to_new = jnp.asarray(o2n)
        return {'hidden_states': hidden_states, 'gate_weight': gate_weight, 'gate_up_proj': gate_up_proj, 'down_proj': down_proj, 'old_to_new': old_to_new}
    _L1_ffn_all = _L1_ffn_setup()
    _L1_ffn_in = {k: v for k, v in _L1_ffn_all.items() if k in ('gate_weight', 'gate_up_proj', 'down_proj', 'old_to_new')}
    del _L1_ffn_all
    return {'x': x, 'ctx_2048': ctx_2048, 'itok_Sx4_0_63': itok_Sx4_0_63, 'pos_BxS2': pos_BxS2, 'itok_BxS_4096_4607': itok_BxS_4096_4607, 'L0_attn_Wq': _L0_attn_in['Wq'], 'L0_attn_Wk': _L0_attn_in['Wk'], 'L0_attn_Wv': _L0_attn_in['Wv'], 'L0_attn_Wo': _L0_attn_in['Wo'], 'L0_xattn_desc_router': _L0_xattn_in['desc_router'], 'L0_xattn_W_q': _L0_xattn_in['W_q'], 'L0_xattn_b_q': _L0_xattn_in['b_q'], 'L0_ffn_router_w': _L0_ffn_in['router_w'], 'L0_ffn_expert_bias': _L0_ffn_in['expert_bias'], 'L0_ffn_gate_proj': _L0_ffn_in['gate_proj'], 'L0_ffn_up_proj': _L0_ffn_in['up_proj'], 'L0_ffn_down_proj': _L0_ffn_in['down_proj'], 'L1_attn_Wq': _L1_attn_in['Wq'], 'L1_attn_Wk': _L1_attn_in['Wk'], 'L1_attn_Wv': _L1_attn_in['Wv'], 'L1_attn_Wo': _L1_attn_in['Wo'], 'L1_attn_Wa': _L1_attn_in['Wa'], 'L1_attn_Wb': _L1_attn_in['Wb'], 'L1_attn_qcw': _L1_attn_in['qcw'], 'L1_attn_qcb': _L1_attn_in['qcb'], 'L1_attn_kcw': _L1_attn_in['kcw'], 'L1_attn_kcb': _L1_attn_in['kcb'], 'L1_attn_vcw': _L1_attn_in['vcw'], 'L1_attn_vcb': _L1_attn_in['vcb'], 'L1_xattn_Wq': _L1_xattn_in['Wq'], 'L1_xattn_Wk': _L1_xattn_in['Wk'], 'L1_xattn_Wv': _L1_xattn_in['Wv'], 'L1_xattn_Wo': _L1_xattn_in['Wo'], 'L1_xattn_q_norm_w': _L1_xattn_in['q_norm_w'], 'L1_xattn_k_norm_w': _L1_xattn_in['k_norm_w'], 'L1_ffn_gate_weight': _L1_ffn_in['gate_weight'], 'L1_ffn_gate_up_proj': _L1_ffn_in['gate_up_proj'], 'L1_ffn_down_proj': _L1_ffn_in['down_proj'], 'L1_ffn_old_to_new': _L1_ffn_in['old_to_new']}

def reference(x, ctx_2048, itok_Sx4_0_63, pos_BxS2, itok_BxS_4096_4607, L0_attn_Wq, L0_attn_Wk, L0_attn_Wv, L0_attn_Wo, L0_xattn_desc_router, L0_xattn_W_q, L0_xattn_b_q, L0_ffn_router_w, L0_ffn_expert_bias, L0_ffn_gate_proj, L0_ffn_up_proj, L0_ffn_down_proj, L1_attn_Wq, L1_attn_Wk, L1_attn_Wv, L1_attn_Wo, L1_attn_Wa, L1_attn_Wb, L1_attn_qcw, L1_attn_qcb, L1_attn_kcw, L1_attn_kcb, L1_attn_vcw, L1_attn_vcb, L1_xattn_Wq, L1_xattn_Wk, L1_xattn_Wv, L1_xattn_Wo, L1_xattn_q_norm_w, L1_xattn_k_norm_w, L1_ffn_gate_weight, L1_ffn_gate_up_proj, L1_ffn_down_proj, L1_ffn_old_to_new):
    import jax
    import jax.numpy as jnp

    def _L0_attn_ref(x, Wq, Wk, Wv, Wo):
        import jax, jax.numpy as jnp
        import numpy as np
        H = 16
        KVH = 4
        G = H // KVH
        HD = 128
        D = 256
        BASE = 10000.0

        def _rope(x, cos, sin):
            half = HD // 2
            x1, x2 = (x[..., :half], x[..., half:])
            return jnp.concatenate([x1 * cos - x2 * sin, x1 * sin + x2 * cos], axis=-1)
        B, S, _ = x.shape
        scale = HD ** (-0.5)
        q = (x @ Wq).reshape(B, S, H, HD).transpose(0, 2, 1, 3)
        k = (x @ Wk).reshape(B, S, KVH, HD).transpose(0, 2, 1, 3)
        v = (x @ Wv).reshape(B, S, KVH, HD).transpose(0, 2, 1, 3)
        t = jnp.arange(S, dtype=x.dtype)
        inv_freq = 1.0 / BASE ** (jnp.arange(0, HD, 2, dtype=x.dtype) / HD)
        freqs = t[:, None] * inv_freq[None, :]
        cos, sin = (jnp.cos(freqs), jnp.sin(freqs))
        q = _rope(q, cos, sin)
        k = _rope(k, cos, sin)
        qg = q.reshape(B, KVH, G, S, HD)
        scores = jnp.einsum('bkgqd,bksd->bkgqs', qg, k) * scale
        causal = jnp.triu(jnp.full((S, S), -jnp.inf, dtype=x.dtype), k=1)
        scores = scores + causal
        attn = jax.nn.softmax(scores, axis=-1)
        out = jnp.einsum('bkgqs,bksd->bkgqd', attn, v)
        out = out.reshape(B, H, S, HD).transpose(0, 2, 1, 3).reshape(B, S, H * HD)
        return out @ Wo

    def _L0_xattn_ref(token_states, set_states, desc_router, W_q, b_q, token_to_sets):
        import math
        import jax, jax.numpy as jnp
        import numpy as np
        B, S, D, N, K, TOPK = (4, 512, 256, 64, 4, 2)
        batch, seq_len, d = token_states.shape
        num_sets = set_states.shape[1]
        scale = 1.0 / math.sqrt(d)
        q = jnp.einsum('bsd,ed->bse', token_states, W_q) + b_q
        scores = jnp.einsum('bse,ne->bsn', q, desc_router) * scale
        valid = token_to_sets >= 0
        mask = ((token_to_sets[:, :, None] == jnp.arange(num_sets)[None, None, :]) & valid[:, :, None]).any(axis=1)
        neg_inf = jnp.array(-jnp.inf, scores.dtype)
        scores = jnp.where(mask[None, :, :], scores, neg_inf)
        topk_vals, topk_idx = jax.lax.top_k(scores, TOPK)
        b_i = jnp.arange(batch)[:, None, None]
        s_i = jnp.arange(seq_len)[None, :, None]
        scores = jnp.full_like(scores, neg_inf).at[b_i, s_i, topk_idx].set(topk_vals)
        weights = jax.nn.softmax(scores, axis=-1)
        return jnp.einsum('bsn,bnd->bsd', weights, set_states)

    def _L0_ffn_ref(x, router_w, expert_bias, gate_proj, up_proj, down_proj):
        import jax, jax.numpy as jnp
        import numpy as np
        TOP_K = 4
        NUM_EXPERTS = 16
        logits = jnp.einsum('bsh,eh->bse', x, router_w) + expert_bias
        scores = jax.nn.softmax(logits, axis=-1)
        top_w, top_idx = jax.lax.top_k(scores, TOP_K)
        top_w = top_w / jnp.sum(top_w, axis=-1, keepdims=True)
        g = jnp.einsum('bsh,khe->bske', x, gate_proj)
        u = jnp.einsum('bsh,khe->bske', x, up_proj)
        act = jax.nn.silu(g) * u
        out = jnp.einsum('bske,keh->bskh', act, down_proj)
        sel = jnp.take_along_axis(out, top_idx[..., None], axis=2)
        return jnp.sum(sel * top_w[..., None], axis=2)

    def _L1_attn_ref(x, Wq, Wk, Wv, Wo, Wa, Wb, qcw, qcb, kcw, kcb, vcw, vcb):
        import jax, jax.numpy as jnp
        import numpy as np
        H = 256
        HK = 16
        HV = 32
        DK = 128
        DV = 128
        KC = 4
        VE = HV // HK * DV
        B, T = (1, 64)

        def _causal_conv_silu(x, w, b):
            t = x.shape[1]
            kk = w.shape[1]
            xp = jnp.pad(x, ((0, 0), (kk - 1, 0), (0, 0)))
            y = b
            for j in range(kk):
                y = y + w[:, j] * xp[:, j:j + t, :]
            return jax.nn.silu(y)

        def _l2norm(x):
            return x / jnp.maximum(jnp.linalg.norm(x, axis=-1, keepdims=True), 1e-12)

        def _reference_tuple_inner(x, Wq, Wk, Wv, Wo, Wa, Wb, qcw, qcb, kcw, kcb, vcw, vcb):
            b, t, _ = x.shape
            q = _causal_conv_silu(x @ Wq, qcw, qcb).reshape(b, t, HK, DK)
            k = _causal_conv_silu(x @ Wk, kcw, kcb).reshape(b, t, HK, DK)
            v = _causal_conv_silu(x @ Wv, vcw, vcb).reshape(b, t, HK, VE)
            q = _l2norm(q)
            k = _l2norm(k)
            alpha = jax.nn.sigmoid(x @ Wa)
            beta = jax.nn.sigmoid(x @ Wb)
            state0 = jnp.zeros((b, HK, DK, VE), x.dtype)

            def step(state, inp):
                qt, kt, vt, at, bt = inp
                state = state * at[:, :, None, None]
                err = vt - jnp.einsum('bhkv,bhk->bhv', state, kt)
                state = state + bt[:, :, None, None] * jnp.einsum('bhk,bhv->bhkv', kt, err)
                ot = jnp.einsum('bhkv,bhk->bhv', state, qt)
                return (state, ot)
            xs = (q.transpose(1, 0, 2, 3), k.transpose(1, 0, 2, 3), v.transpose(1, 0, 2, 3), alpha.transpose(1, 0, 2), beta.transpose(1, 0, 2))
            state, outs = jax.lax.scan(step, state0, xs)
            out = outs.transpose(1, 0, 2, 3).reshape(b, t, HV * DV) @ Wo
            return (out, state)
        return _reference_tuple_inner(x, Wq, Wk, Wv, Wo, Wa, Wb, qcw, qcb, kcw, kcb, vcw, vcb)[0]

    def _L1_xattn_ref(draft_hidden, context_hidden, Wq, Wk, Wv, Wo, q_norm_w, k_norm_w, context_position_ids, draft_position_ids):
        import jax, jax.numpy as jnp
        import numpy as np
        B, CTX, DRAFT, D = (2, 512, 64, 256)
        H, KVH, HD = (16, 4, 128)
        N_REP = H // KVH
        EPS = 1e-06
        THETA = 10000.0
        SCALE = 1.0 / np.sqrt(HD).astype(np.float32)

        def _rms_norm(x, w):
            v = jnp.mean(jnp.square(x.astype(jnp.float32)), axis=-1, keepdims=True)
            return (w * (x.astype(jnp.float32) * jax.lax.rsqrt(v + EPS))).astype(x.dtype)

        def _rotate_half(x):
            x1, x2 = jnp.split(x, 2, axis=-1)
            return jnp.concatenate((-x2, x1), axis=-1)

        def _rope(x, pos):
            inv_freq = 1.0 / THETA ** (jnp.arange(0, HD, 2, dtype=jnp.float32) / HD)
            freqs = pos.astype(jnp.float32)[:, None, :, None] * inv_freq
            emb = jnp.concatenate((freqs, freqs), axis=-1)
            return x * jnp.cos(emb) + _rotate_half(x) * jnp.sin(emb)
        bsz, draft_len, _ = draft_hidden.shape
        ctx_len = context_hidden.shape[1]
        total_len = ctx_len + draft_len
        q = (draft_hidden @ Wq.T).reshape(bsz, draft_len, H, HD)
        q = _rms_norm(q, q_norm_w).transpose(0, 2, 1, 3)
        kv_in = jnp.concatenate([context_hidden, draft_hidden], axis=1)
        k = (kv_in @ Wk.T).reshape(bsz, total_len, KVH, HD)
        v = (kv_in @ Wv.T).reshape(bsz, total_len, KVH, HD).transpose(0, 2, 1, 3)
        k = _rms_norm(k, k_norm_w).transpose(0, 2, 1, 3)
        full_position_ids = jnp.concatenate([context_position_ids, draft_position_ids], axis=1)
        q = _rope(q, draft_position_ids)
        k = _rope(k, full_position_ids)
        k = jnp.repeat(k, N_REP, axis=1)
        v = jnp.repeat(v, N_REP, axis=1)
        scores = jnp.einsum('bhqd,bhkd->bhqk', q, k) * SCALE
        probs = jax.nn.softmax(scores, axis=-1)
        attn = jnp.einsum('bhqk,bhkd->bhqd', probs, v)
        attn = attn.transpose(0, 2, 1, 3).reshape(bsz, draft_len, H * HD)
        return attn @ Wo.T

    def _L1_ffn_ref(hidden_states, gate_weight, gate_up_proj, down_proj, old_to_new):
        import jax, jax.numpy as jnp
        import numpy as np
        NUM_EXPERTS = 128
        NUM_KEPT = 48
        TOP_K = 8
        HIDDEN = 256
        INTER = 96
        CAP = 96
        BATCH, SEQ = (2, 128)
        B, S, H = hidden_states.shape
        x = hidden_states.reshape(-1, H)
        T = x.shape[0]
        logits = x @ gate_weight.T
        logits = jnp.where(old_to_new[None, :] == -1, -jnp.inf, logits)
        probs = jax.nn.softmax(logits.astype(jnp.float32), axis=-1).astype(logits.dtype)
        top_v, top_i = jax.lax.top_k(probs, TOP_K)
        top_v = top_v / jnp.sum(top_v, axis=-1, keepdims=True)
        sel_new = old_to_new[top_i]
        E = gate_up_proj.shape[0]
        flat_e = sel_new.reshape(-1)
        flat_w = top_v.reshape(-1)
        tok = jnp.repeat(jnp.arange(T), TOP_K)
        oh = (flat_e[:, None] == jnp.arange(E)[None, :]).astype(jnp.int32)
        pos = jnp.sum(jnp.cumsum(oh, axis=0) * oh, axis=-1) - 1
        valid = pos < CAP
        pos_c = jnp.where(valid, pos, CAP)
        xb = jnp.zeros((E, CAP + 1, H), x.dtype).at[flat_e, pos_c].set(x[tok])
        xb = xb[:, :CAP]
        gu = jnp.einsum('ech,eoh->eco', xb, gate_up_proj)
        g, u = jnp.split(gu, 2, axis=-1)
        h = jax.nn.silu(g) * u
        out = jnp.einsum('eci,ehi->ech', h, down_proj)
        y = out[flat_e, jnp.minimum(pos_c, CAP - 1)]
        w = flat_w * valid.astype(flat_w.dtype)
        final = jnp.zeros_like(x).at[tok].add(y * w[:, None])
        return final.reshape(B, S, H)
    x = x + _L0_attn_ref(_layernorm(x, axis=-1), L0_attn_Wq, L0_attn_Wk, L0_attn_Wv, L0_attn_Wo)
    x = x + _L0_xattn_ref(_layernorm(x, axis=-1), ctx_2048, L0_xattn_desc_router, L0_xattn_W_q, L0_xattn_b_q, itok_Sx4_0_63)
    x = x + _L0_ffn_ref(_layernorm(x, axis=-1), L0_ffn_router_w, L0_ffn_expert_bias, L0_ffn_gate_proj, L0_ffn_up_proj, L0_ffn_down_proj)
    x = x + _L1_attn_ref(_layernorm(x, axis=-1), L1_attn_Wq, L1_attn_Wk, L1_attn_Wv, L1_attn_Wo, L1_attn_Wa, L1_attn_Wb, L1_attn_qcw, L1_attn_qcb, L1_attn_kcw, L1_attn_kcb, L1_attn_vcw, L1_attn_vcb)
    x = x + _L1_xattn_ref(_layernorm(x, axis=-1), ctx_2048, L1_xattn_Wq, L1_xattn_Wk, L1_xattn_Wv, L1_xattn_Wo, L1_xattn_q_norm_w, L1_xattn_k_norm_w, pos_BxS2, itok_BxS_4096_4607)
    x = x + _L1_ffn_ref(_layernorm(x, axis=-1), L1_ffn_gate_weight, L1_ffn_gate_up_proj, L1_ffn_down_proj, L1_ffn_old_to_new)
    return x

_drawn_inputs = setup_inputs


def setup_inputs(seed=0):
    import zlib

    import numpy as np

    out = dict(_drawn_inputs(seed))
    spreads = {'L0_xattn_b_q': (0.0, 0.1),
     'L0_ffn_expert_bias': (0.0, 0.8),
     'L1_xattn_q_norm_w': (1.0, 0.6),
     'L1_xattn_k_norm_w': (1.0, 0.6)}
    factors = {'L0_attn_Wk': 3.346,
     'L0_ffn_router_w': 8.0,
     'L0_ffn_gate_proj': 8.0,
     'L0_ffn_up_proj': 8.0,
     'L0_ffn_down_proj': 8.0,
     'L1_attn_Wq': 8.0,
     'L1_attn_Wk': 8.0,
     'L1_attn_Wv': 8.0,
     'L1_attn_Wo': 8.0,
     'L1_attn_Wa': 8.0,
     'L1_attn_Wb': 8.0,
     'L1_attn_qcw': 8.0,
     'L1_attn_qcb': 8.0,
     'L1_attn_kcw': 8.0,
     'L1_attn_kcb': 8.0,
     'L1_attn_vcw': 8.0,
     'L1_attn_vcb': 8.0,
     'L1_ffn_gate_weight': 8.0,
     'L1_ffn_gate_up_proj': 8.0,
     'L1_ffn_down_proj': 8.0}
    for name, (base, spread) in spreads.items():
        noise = np.random.default_rng([zlib.crc32(name.encode()), seed]).standard_normal(out[name].shape)
        drawn = base * np.exp(spread * noise) if base else spread * noise
        out[name] = jnp.asarray(drawn.astype(out[name].dtype))
    for name, factor in factors.items():
        out[name] = (out[name] * factor).astype(out[name].dtype)
    return out
```

```python
from contextlib import ExitStack, contextmanager

import numpy as np

import concourse.bass as bass
from concourse import mybir

F32 = mybir.dt.float32
BF16 = mybir.dt.bfloat16
I32 = mybir.dt.int32
U32 = mybir.dt.uint32
ALU = mybir.AluOpType
ACT = mybir.ActivationFunctionType
AX_X = mybir.AxisListType.X
ds = bass.ds

P = 128
B, S, D = 8, 256, 256
T = B * S
NT = T // P
DC = D // P
TB = S // P
NEG = -1.0e30
LN_EPS = 1e-5
LN_TILES = 4
CTX = 64
HD = 128
H, KVH = 16, 4
G = H // KVH
HALF = HD // 2


class Chain:

    def __init__(self, eng, sem, first):
        self.eng, self.sem, self.first, self.count = eng, sem, first, 0

    def link(self, ins):
        self.count += 1
        ins.then_inc(self.sem, 1)
        self.eng.wait_ge(self.sem, self.first + self.count)


class Core:

    def __init__(self, nc, ins, out, stack):
        self.nc, self.ins, self.out, self.stack = nc, ins, out, stack
        self.ln_calls = 0
        self.attn_calls = 0
        self.phase, self.suffix = None, ""

    def sb(self, name, shape, dt=F32, stack=None):
        return (stack or self.stack).enter_context(self.nc.sbuf_tensor(name, shape, dt))

    def sem(self, name):
        handle = (self.phase or self.stack).enter_context(self.nc.semaphore(name + self.suffix))
        if self.phase:
            self.phase_sems.append(handle)
        return handle

    def sems(self, name):
        return [self.sem(f"{name}{h}") for h in range(2)]

    @contextmanager
    def own_semaphores(self, suffix):
        self.phase, self.phase_sems, self.suffix = ExitStack(), [], suffix
        with self.phase:
            yield
            numbers = sorted(s.num for s in self.phase_sems)
            runs = []
            for n in numbers:
                if runs and runs[-1][-1] == n - 1:
                    runs[-1].append(n)
                else:
                    runs.append([n])
            with self.nc.Block() as block:

                @block.gpsimd
                def _(pool):
                    for r in runs:
                        pool.sem_clear(range(r[0], r[-1] + 1))
        self.phase, self.suffix = None, ""


def load_constants(k):
    nc, ins = k.nc, k.ins
    k.x = k.sb("x", [P, NT, D])
    k.xnT = k.sb("xnT", [P, DC, T])
    k.ident = k.sb("ident", [P, P])
    k.identb = k.sb("identb", [P, P], BF16)
    k.causb = k.sb("causb", [P, P], BF16)
    k.mhalf = k.sb("mhalf", [P, 16])
    k.ps = [k.stack.enter_context(nc.psum_tensor(f"ps{h}", [P, 4, 512], F32)) for h in range(2)]
    k.ln_stats = k.sb("ln_stats", [P, LN_TILES, 6])
    k.ln_mv = k.sb("ln_mv", [P, LN_TILES, 2])
    k.ln_ve = k.sb("ln_ve", [P, LN_TILES])
    k.ln_rstd = k.sb("ln_rstd", [P, LN_TILES])
    k.ln_xn = [k.sb(f"ln_xn{q}", [P, D]) for q in range(LN_TILES)]
    k.ln_chain = k.sem("ln_chain")
    k.ln_var = k.sem("ln_var")
    k.ln_pow = k.sem("ln_pow")
    k.ln_normed = k.sem("ln_normed")
    k.ln_turned = k.sem("ln_turned")
    k.ln_stored = k.sem("ln_stored")
    loaded = k.sem("const_loaded")
    made = k.sem("const_made")
    with nc.Block() as block:

        @block.sync
        def _(sp):
            for b in range(B):
                sp.dma_start(k.x[:, TB * b:TB * b + TB, :],
                             ins["x"][b].rearrange("(t p) d -> p t d", p=P)).then_inc(loaded, 16)
            sp.dma_start(k.ident[:, :], ins["c_ident"]).then_inc(loaded, 16)
            sp.dma_start(k.identb[:, :], ins["c_identb"]).then_inc(loaded, 16)
            sp.dma_start(k.causb[:, :], ins["c_causb"]).then_inc(loaded, 16)
            sp.wait_ge(loaded, 16 * (B + 3))

        @block.gpsimd
        def _(pool):
            nc.gpsimd.memset(k.mhalf[:, :], -0.5).then_inc(made, 1)
            pool.wait_ge(made, 1)


def layernorm(k, rows=None):
    nc = k.nc
    Q = LN_TILES
    turns = NT // Q

    def xn(i, q):
        return k.ln_xn[q][:, :] if rows is None else rows[:, i * Q + q, :]

    base = k.ln_calls * turns
    k.ln_calls += 1
    first = base == 0
    with nc.Block() as block:

        @block.vector
        def _(dve):
            for i in range(turns):
                for q in range(Q):
                    nc.vector.bn_stats(k.ln_stats[:, q, :], k.x[:, i * Q + q, :]).then_inc(k.ln_chain, 1)
                dve.wait_ge(k.ln_chain, (i + base) * (2 * Q) + Q)
                for q in range(Q):
                    nc.vector.bn_aggr(k.ln_mv[:, q, :], k.ln_stats[:, q, :]).then_inc(k.ln_chain, 1)
                dve.wait_ge(k.ln_chain, (i + base) * (2 * Q) + 2 * Q)
                nc.vector.tensor_scalar(k.ln_ve[:, :], k.ln_mv[:, :, 1], LN_EPS, None, ALU.add).then_inc(k.ln_var, 1)
                dve.wait_ge(k.ln_turned, i + base + 1)
                dve.wait_ge(k.ln_pow, i + base + 1)
                for q in range(Q):
                    last = nc.vector.tensor_scalar(xn(i, q), k.x[:, i * Q + q, :],
                                                   k.ln_mv[:, q, 0:1], k.ln_rstd[:, q:q + 1],
                                                   ALU.subtract, ALU.mult)
                last.then_inc(k.ln_normed, 1)

        @block.gpsimd
        def _(pool):
            for i in range(turns):
                pool.wait_ge(k.ln_var, i + base + 1)
                nc.gpsimd.tensor_tensor(k.ln_rstd[:, :], k.ln_ve[:, :], k.mhalf[:, 0:Q], ALU.pow).then_inc(k.ln_pow, 1)

        @block.tensor
        def _(pe):
            if first:
                pe.sem_inc(k.ln_turned, 1)
            for i in range(turns):
                pe.wait_ge(k.ln_normed, i + base + 1)
                pe.wait_ge(k.ln_stored, i + base + 1)
                for q in range(Q):
                    for c in range(DC):
                        last = nc.tensor.transpose(k.ps[0][:, c, q * P:(q + 1) * P],
                                                   xn(i, q)[:, c * P:(c + 1) * P], k.ident[:, :])
                last.then_inc(k.ln_turned, 1)

        @block.scalar
        def _(act):
            if first:
                act.sem_inc(k.ln_stored, 1)
            for i in range(turns):
                act.wait_ge(k.ln_turned, i + base + 2)
                nc.scalar.copy(k.xnT[:, :, i * Q * P:(i + 1) * Q * P], k.ps[0][:, 0:DC, :]).then_inc(k.ln_stored, 1)


class AttentionSemaphores:

    def __init__(self, k):
        self.xb_ready = k.sems("xb_ready")
        self.projected = k.sems("projected")
        self.v_kept = k.sems("v_kept")
        self.projected_sq = k.sems("projected_sq")
        self.rotated = k.sems("rotated")
        self.summed = k.sems("summed")
        self.sq_done = k.sems("sq_done")
        self.rms_ready = k.sems("rms_ready")
        self.turned_in = k.sems("turned_in")
        self.qk_turned = k.sems("qk_turned")
        self.qk_kept = k.sems("qk_kept")
        self.scored = k.sems("scored")
        self.max_ready = k.sems("max_ready")
        self.exp_done = k.sems("exp_done")
        self.probs_ready = k.sems("probs_ready")
        self.probs_turned = k.sems("probs_turned")
        self.probs_kept_a = k.sems("probs_kept_a")
        self.probs_kept_d = k.sems("probs_kept_d")
        self.mixed = k.sems("mixed")
        self.mix_kept = k.sems("mix_kept")
        self.out_ready = k.sems("out_ready")
        self.out_added = k.sems("out_added")


def attention(k, weights, rope, ctx):
    nc, ins = k.nc, k.ins
    cross = ctx is not None
    scale = float(HD) ** -0.5
    KT = TB + 1 if cross else TB
    NK = S + (CTX if cross else 0)
    krows = [P] * TB + [CTX]
    s = AttentionSemaphores(k)
    chains, loaded = k.sems("at_chain"), k.sem("at_loaded")
    with ExitStack() as st:
        def sb(name, shape, dt=F32):
            return k.sb(f"at{k.attn_calls}_{name}", shape, dt, st)

        wq = sb("wq", [P, DC, H * HD])
        wkv = sb("wkv", [P, DC, KVH * 2 * HD])
        wo = sb("wo", [P, H, D])
        xb = [sb(f"xb{h}", [P, DC, NK]) for h in range(2)]
        t1 = [sb(f"t1{h}", [P, KT, G + 1, HD]) for h in range(2)]
        t2 = [sb(f"t2{h}", [P, KT, G + 1, HD]) for h in range(2)]
        qT = [sb(f"qT{h}", [P, G, S]) for h in range(2)]
        kT = [sb(f"kT{h}", [P, NK]) for h in range(2)]
        v = [sb(f"v{h}", [P, KT, HD]) for h in range(2)]
        mx = [sb(f"mx{h}", [P, 4]) for h in range(2)]
        nb = [sb(f"nb{h}", [P, 4]) for h in range(2)]
        den = [sb(f"den{h}", [P, 4]) for h in range(2)]
        rden = [sb(f"rden{h}", [P, 4]) for h in range(2)]
        probs = [sb(f"probs{h}", [P, 4, NK]) for h in range(2)]
        shared = [sb(f"shared{h}", [P, max(2 * KT * S, KT * (G + 1) * HD)]) for h in range(2)]
        pT = [b[:, 0:2 * KT * S].rearrange("p (m s) -> p m s", s=S) for b in shared]
        sqs = [b[:, 0:KT * (G + 1) * HD].rearrange("p (t g d) -> p t g d", t=KT, g=G + 1) for b in shared]
        oT = [sb(f"oT{h}", [P, G, S]) for h in range(2)]
        if cross:
            ss = [sb(f"ss{h}", [P, KT, G + 1]) for h in range(2)]
            rs = [sb(f"rs{h}", [P, KT, G + 1]) for h in range(2)]
            esc = [sb(f"esc{h}", [P, TB, G]) for h in range(2)]
        loads = 3

        def q_ps(h):
            return k.ps[h][:, 0:TB, :].rearrange("p t (g d) -> p t g d", g=G)

        def kv_ps(h, part):
            return k.ps[h][:, 2, :].rearrange("p (t s d) -> p t s d", t=TB, s=2)[:, :, part, :]

        def ckv_ps(h, part):
            return k.ps[h][0:CTX, 3, part * HD:(part + 1) * HD]

        def slot(h, m):
            return k.ps[h][:, m // 2, (m % 2) * S:(m % 2) * S + S]

        with nc.Block() as block:

            @block.sync
            def _(sp):
                sp.dma_start(wq[:, :, :], ins[weights[0]].rearrange("(c p) n -> p c n", p=P)).then_inc(loaded, 16)
                sp.dma_start(wkv[:, :, :], ins[weights[1]].rearrange("(c p) n -> p c n", p=P)).then_inc(loaded, 16)
                sp.dma_start(wo[:, :, :], ins[weights[2]].rearrange("(h p) n -> p h n", p=P)).then_inc(loaded, 16)

            @block.gpsimd
            def _(pool):
                with pool.Fori(0, KVH) as g:
                    with pool.Fori(0, B // 2) as p:
                        n = g * (B // 2) + p + 1
                        for h in range(2):
                            pool.wait_ge(s.projected[h], n)
                            xc = nc.gpsimd.tensor_copy(xb[h][:, :, 0:S], k.xnT[:, :, ds(p * (2 * S) + h * S, S)])
                            if cross:
                                xc = nc.gpsimd.tensor_copy(xb[h][:, :, S:NK], ctx.ctxT[:, :, ds(p * (2 * CTX) + h * CTX, CTX)])
                            xc.then_inc(s.xb_ready[h], 1)
                        for h in range(2):
                            pool.wait_ge(s.rotated[h], n)
                            ad = nc.gpsimd.tensor_tensor(t1[h][:, 0:TB], t1[h][:, 0:TB], t2[h][:, 0:TB], ALU.add)
                            if cross:
                                ad = nc.gpsimd.tensor_tensor(t1[h][0:CTX, TB, G, :], t1[h][0:CTX, TB, G, :],
                                                             t2[h][0:CTX, TB, G, :], ALU.add)
                            ad.then_inc(s.summed[h], 1)
                            if cross:
                                pool.wait_ge(s.sq_done[h], n)
                                nc.gpsimd.tensor_tensor(rs[h][:, 0:TB, :], ss[h][:, 0:TB, :],
                                                        k.mhalf[:, 0:TB * (G + 1)].rearrange("p (t g) -> p t g", t=TB),
                                                        ALU.pow)
                                nc.gpsimd.tensor_tensor(rs[h][0:CTX, TB, G:G + 1], ss[h][0:CTX, TB, G:G + 1],
                                                        k.mhalf[0:CTX, 0:1], ALU.pow).then_inc(s.rms_ready[h], 1)

            @block.tensor
            def _(pe):
                pe.wait_ge(loaded, 16 * loads)
                for h in range(2):
                    pe.sem_inc(s.projected[h], 1)
                    pe.sem_inc(s.mixed[h], 1)
                with pe.Fori(0, KVH) as g:
                    with pe.Fori(0, B // 2) as p:
                        n = g * (B // 2) + p + 1

                        def project(h):
                            pe.wait_ge(s.xb_ready[h], n)
                            pe.wait_ge(s.out_added[h], n)
                            for t in range(TB):
                                for c in range(DC):
                                    nc.tensor.matmul(k.ps[h][:, t, :], xb[h][:, c, t * P:(t + 1) * P],
                                                     wq[:, c, ds(g * (G * HD), G * HD)], start=c == 0, stop=c == DC - 1)
                            for t in range(KT):
                                o = k.ps[h][0:krows[t], 2 + t // 2, (t % 2) * 2 * HD:(t % 2 + 1) * 2 * HD]
                                for c in range(DC):
                                    last = nc.tensor.matmul(o, xb[h][:, c, t * P:t * P + krows[t]],
                                                            wkv[:, c, ds(g * (2 * HD), 2 * HD)],
                                                            start=c == 0, stop=c == DC - 1)
                            last.then_inc(s.projected[h], 1)

                        def turn_qk(h):
                            pe.wait_ge(s.turned_in[h] if cross else s.summed[h], n)
                            pe.wait_ge(s.v_kept[h], n)
                            for hh in range(G):
                                for t in range(TB):
                                    nc.tensor.transpose(slot(h, hh)[:, t * P:(t + 1) * P], t1[h][:, t, hh, :], k.ident[:, :])
                            for t in range(KT):
                                r = krows[t]
                                last = nc.tensor.transpose(k.ps[h][:, 2, t * P:t * P + r], t1[h][0:r, t, G, :],
                                                           k.ident[0:r, 0:r])
                            last.then_inc(s.qk_turned[h], 1)

                        def score(h, r):
                            if r == 0:
                                pe.wait_ge(s.qk_kept[h], n)
                            else:
                                pe.wait_ge(s.mix_kept[h], 2 * n - 1)
                            for hh in range(2):
                                for t in range(TB):
                                    nk = NK if cross else (t + 1) * P
                                    last = nc.tensor.matmul(k.ps[h][:, hh * TB + t, 0:nk],
                                                            qT[h][:, 2 * r + hh, t * P:(t + 1) * P],
                                                            kT[h][:, 0:nk], start=True, stop=cross)
                                    if not cross:
                                        last = nc.tensor.matmul(k.ps[h][:, hh * TB + t, t * P:nk], k.identb[:, :],
                                                                k.causb[:, :], start=False, stop=True)
                            last.then_inc(s.scored[h], 1)

                        def turn_probs(h, r):
                            pe.wait_ge(s.probs_ready[h], 2 * n - 1 + r)
                            for hh in range(2):
                                for j in range(KT):
                                    w = krows[j]
                                    for t in range(TB):
                                        if cross or j <= t:
                                            last = nc.tensor.transpose(slot(h, hh * KT + j)[0:w, t * P:(t + 1) * P],
                                                                       probs[h][:, hh * TB + t, j * P:j * P + w], k.ident[:, :])
                            last.then_inc(s.probs_turned[h], 1)

                        def mix(h, r):
                            pe.wait_ge(s.probs_kept_a[h], 2 * n - 1 + r)
                            pe.wait_ge(s.probs_kept_d[h], 2 * n - 1 + r)
                            for hh in range(2):
                                for j in range(KT):
                                    w = krows[j]
                                    c0 = 0 if cross else j * P
                                    last = nc.tensor.matmul(k.ps[h][:, 3, hh * S + c0:(hh + 1) * S], v[h][0:w, j, :],
                                                            pT[h][0:w, hh * KT + j, c0:S], start=j == 0, stop=j == KT - 1)
                            last.then_inc(s.mixed[h], 1)

                        def give(h):
                            pe.wait_ge(s.mix_kept[h], 2 * n)
                            for t in range(TB):
                                for hh in range(G):
                                    last = nc.tensor.matmul(slot(h, t), oT[h][:, hh, t * P:(t + 1) * P],
                                                            wo[:, ds(g * G + hh, 1), :], start=hh == 0, stop=hh == G - 1)
                            last.then_inc(s.out_ready[h], 1)

                        for h in range(2):
                            project(h)
                        for h in range(2):
                            turn_qk(h)
                        for r in range(2):
                            for h in range(2):
                                score(h, r)
                            for h in range(2):
                                turn_probs(h, r)
                            for h in range(2):
                                mix(h, r)
                        for h in range(2):
                            give(h)

            @block.vector
            def _(dve):
                for h in range(2):
                    dve.sem_inc(s.out_added[h], 1)
                LINKS = 5 if cross else 4
                with dve.Fori(0, KVH) as g:
                    with dve.Fori(0, B // 2) as p:
                        n = g * (B // 2) + p + 1
                        chain = [Chain(dve, chains[h], (n - 1) * LINKS) for h in range(2)]

                        def rotate(h):
                            dve.wait_ge(s.projected[h], n + 1)
                            cq, sq = rope.q(p, h)
                            ck, sk = rope.k(p, h)
                            q, kk = q_ps(h), kv_ps(h, 0)

                            def each(o1, o2, x, c, sn):
                                nc.vector.tensor_tensor(o1, x, c, ALU.mult)
                                nc.vector.tensor_tensor(o2[..., 0:HALF], x[..., HALF:HD], sn[..., 0:HALF], ALU.mult)
                                return nc.vector.tensor_tensor(o2[..., HALF:HD], x[..., 0:HALF], sn[..., HALF:HD], ALU.mult)

                            for t in range(TB):
                                each(t1[h][:, t, 0:G, :], t2[h][:, t, 0:G, :], q[:, t],
                                     cq[:, t:t + 1, :].to_broadcast([P, G, HD]), sq[:, t:t + 1, :].to_broadcast([P, G, HD]))
                            last = each(t1[h][:, 0:TB, G, :], t2[h][:, 0:TB, G, :], kk, ck, sk)
                            if cross:
                                cc, sc = rope.c(p, h)
                                last = each(t1[h][0:CTX, TB, G, :], t2[h][0:CTX, TB, G, :], ckv_ps(h, 0), cc, sc)
                            last.then_inc(s.rotated[h], 1)

                        def rms(h):
                            dve.wait_ge(s.projected_sq[h], n)
                            sq = sqs[h]
                            nc.vector.tensor_reduce(ss[h][:, 0:TB, :], sq[:, 0:TB], AX_X, ALU.add)
                            chain[h].link(nc.vector.tensor_reduce(ss[h][0:CTX, TB, G:G + 1], sq[0:CTX, TB, G:G + 1, :], AX_X, ALU.add))
                            nc.vector.tensor_scalar(ss[h][:, 0:TB, :], ss[h][:, 0:TB, :], 1.0 / HD, 1e-6, ALU.mult, ALU.add)
                            nc.vector.tensor_scalar(ss[h][0:CTX, TB, G:G + 1], ss[h][0:CTX, TB, G:G + 1], 1.0 / HD, 1e-6,
                                                    ALU.mult, ALU.add).then_inc(s.sq_done[h], 1)

                        def rms_keys(h):
                            dve.wait_ge(s.rms_ready[h], n)
                            nc.vector.tensor_scalar(esc[h][:, :, :], rs[h][:, 0:TB, 0:G], scale, None, ALU.mult)
                            dve.wait_ge(s.summed[h], n)
                            for t in range(KT):
                                r = krows[t]
                                last = nc.vector.tensor_scalar(t1[h][0:r, t, G, :], t1[h][0:r, t, G, :],
                                                               rs[h][0:r, t, G:G + 1], None, ALU.mult)
                            last.then_inc(s.turned_in[h], 1)

                        def row_max(h, r):
                            dve.wait_ge(s.scored[h], 2 * n - 1 + r)
                            if cross:
                                chain[h].link(nc.vector.tensor_reduce(mx[h][:, :], k.ps[h][:, :, 0:NK], AX_X, ALU.max))
                                nc.vector.scalar_tensor_tensor(nb[h][:, :].rearrange("p (g t) -> p g t", g=2),
                                                               mx[h][:, :].rearrange("p (g t) -> p g t", g=2), -1.0,
                                                               esc[h][:, :, 2 * r:2 * r + 2].rearrange("p t g -> p g t"),
                                                               ALU.mult, ALU.mult).then_inc(s.max_ready[h], 1)
                            else:
                                for t in range(TB):
                                    last = nc.vector.tensor_reduce(mx[h][:, :].rearrange("p (g t) -> p g t", g=2)[:, :, t],
                                                                   k.ps[h][:, t:4:TB, 0:(t + 1) * P], AX_X, ALU.max)
                                chain[h].link(last)
                                nc.vector.tensor_scalar(nb[h][:, :], mx[h][:, :], -scale, None, ALU.mult).then_inc(s.max_ready[h], 1)

                        def norm_probs(h, r):
                            dve.wait_ge(s.exp_done[h], 2 * n - 1 + r)
                            chain[h].link(nc.vector.reciprocal(rden[h][:, :], den[h][:, :]))
                            for m in range(4):
                                nk = NK if cross else (m % TB + 1) * P
                                last = nc.vector.tensor_scalar(probs[h][:, m, 0:nk], probs[h][:, m, 0:nk],
                                                               rden[h][:, m:m + 1], None, ALU.mult)
                            last.then_inc(s.probs_ready[h], 1)

                        def keep_probs(h, r):
                            dve.wait_ge(s.probs_turned[h], 2 * n - 1 + r)
                            dve.wait_ge(s.mixed[h], 2 * n - 1 + r)
                            if cross:
                                nc.vector.tensor_copy(pT[h][0:CTX, 2, :], slot(h, 2)[0:CTX, :])
                                last = nc.vector.tensor_copy(pT[h][:, 3, :], slot(h, 3))
                            else:
                                nc.vector.tensor_copy(pT[h][:, 2, :], slot(h, 2))
                                last = nc.vector.tensor_copy(pT[h][:, 3, P:S], slot(h, 3)[:, P:S])
                            last.then_inc(s.probs_kept_d[h], 1)

                        def add_out(h):
                            dve.wait_ge(s.out_ready[h], n)
                            xt = k.x[:, ds(p * (2 * TB) + h * TB, TB), :]
                            nc.vector.tensor_tensor(xt, xt, k.ps[h][:, 0, :].rearrange("p (t d) -> p t d", t=TB),
                                                    ALU.add).then_inc(s.out_added[h], 1)

                        for h in range(2):
                            rotate(h)
                        if cross:
                            for h in range(2):
                                rms(h)
                            for h in range(2):
                                rms_keys(h)
                        for r in range(2):
                            for h in range(2):
                                row_max(h, r)
                            for h in range(2):
                                norm_probs(h, r)
                            for h in range(2):
                                keep_probs(h, r)
                        for h in range(2):
                            add_out(h)
                        assert chain[0].count == LINKS

            @block.scalar
            def _(act):
                with act.Fori(0, KVH) as g:
                    with act.Fori(0, B // 2) as p:
                        n = g * (B // 2) + p + 1

                        def keep_v(h):
                            act.wait_ge(s.rotated[h], n)
                            if cross:
                                nc.scalar.activation(sqs[h][:, 0:TB, 0:G, :], q_ps(h), ACT.Square)
                                nc.scalar.activation(sqs[h][:, 0:TB, G, :], kv_ps(h, 0), ACT.Square)
                                nc.scalar.activation(sqs[h][0:CTX, TB, G, :], ckv_ps(h, 0), ACT.Square)\
                                    .then_inc(s.projected_sq[h], 1)
                                nc.scalar.copy(v[h][0:CTX, TB, :], ckv_ps(h, 1))
                            nc.scalar.copy(v[h][:, 0:TB, :], kv_ps(h, 1)).then_inc(s.v_kept[h], 1)

                        def keep_qk(h):
                            act.wait_ge(s.qk_turned[h], n)
                            nc.scalar.copy(qT[h][:, :, :], k.ps[h][:, 0:2, :].rearrange("p a (b s) -> p (a b) s", b=2))
                            nc.scalar.copy(kT[h][:, :], k.ps[h][:, 2, 0:NK]).then_inc(s.qk_kept[h], 1)

                        def exps(h, r):
                            act.wait_ge(s.max_ready[h], 2 * n - 1 + r)
                            for m in range(4):
                                nk = NK if cross else (m % TB + 1) * P
                                sc = esc[h][:, m % TB, 2 * r + m // TB:2 * r + m // TB + 1] if cross else scale
                                last = nc.scalar.activation(probs[h][:, m, 0:nk], k.ps[h][:, m, 0:nk], ACT.Exp,
                                                            bias=nb[h][:, m:m + 1], scale=sc, accum_out=den[h][:, m:m + 1])
                            last.then_inc(s.exp_done[h], 1)

                        def keep_probs(h, r):
                            act.wait_ge(s.probs_turned[h], 2 * n - 1 + r)
                            act.wait_ge(s.mixed[h], 2 * n - 1 + r)
                            if cross:
                                nc.scalar.copy(pT[h][:, 0:2, :], k.ps[h][:, 0, :].rearrange("p (a s) -> p a s", a=2))
                                nc.scalar.copy(pT[h][:, 4, :], slot(h, 4))
                                last = nc.scalar.copy(pT[h][0:CTX, 5, :], slot(h, 5)[0:CTX, :])
                            else:
                                nc.scalar.copy(pT[h][:, 0, :], slot(h, 0))
                                last = nc.scalar.copy(pT[h][:, 1, P:S], slot(h, 1)[:, P:S])
                            last.then_inc(s.probs_kept_a[h], 1)

                        def keep_mix(h, r):
                            act.wait_ge(s.mixed[h], 2 * n + r)
                            nc.scalar.copy(oT[h][:, 2 * r:2 * r + 2, :], k.ps[h][:, 3, :].rearrange("p (a s) -> p a s", a=2))\
                                .then_inc(s.mix_kept[h], 1)

                        for h in range(2):
                            keep_v(h)
                        for h in range(2):
                            keep_qk(h)
                        for r in range(2):
                            for h in range(2):
                                exps(h, r)
                            for h in range(2):
                                keep_probs(h, r)
                            for h in range(2):
                                keep_mix(h, r)

    k.attn_calls += 1


TOPK_SETS = 2
E0, TOPK0, I0 = 16, 4, 224
IC = I0 // 2


def set_attention(k):
    nc, ins = k.nc, k.ins
    scale = float(D) ** -0.5
    turns = B // 2
    loaded, chain = k.sem("set_loaded"), k.sem("set_chain")
    q_ready, q_kept = k.sems("set_q_ready"), k.sems("set_q_kept")
    scored, gap_ready, gap_exp = k.sems("set_scored"), k.sems("set_gap_ready"), k.sems("set_gap_exp")
    w_ready, w_turned, w_kept = k.sems("set_w_ready"), k.sems("set_w_turned"), k.sems("set_w_kept")
    mixed, added = k.sems("set_mixed"), k.sems("set_added")
    with ExitStack() as st:
        def sb(name, shape, dt=F32):
            return k.sb(f"set_{name}", shape, dt, st)

        wq, bq, desc = sb("wq", [P, DC, D]), sb("bq", [P, DC]), sb("desc", [P, DC, CTX])
        rows = sb("rows", [CTX, B, D])
        iota = sb("iota", [P, CTX])
        tok_i, tok = sb("tok_i", [P, TB, 4], I32), sb("tok", [P, TB, 4])
        mask = sb("mask", [P, TB, CTX])
        qT = [sb(f"qT{h}", [P, DC, S]) for h in range(2)]
        sc = [sb(f"sc{h}", [P, TB, CTX]) for h in range(2)]
        best = [sb(f"best{h}", [P, TB, 8]) for h in range(2)]
        at = [sb(f"at{h}", [P, TB, 8], U32) for h in range(2)]
        atf = [sb(f"atf{h}", [P, TB, 8]) for h in range(2)]
        gap = [sb(f"gap{h}", [P, TB]) for h in range(2)]
        w2 = [sb(f"w2{h}", [P, TB]) for h in range(2)]
        w1 = [sb(f"w1{h}", [P, TB]) for h in range(2)]
        wa = [sb(f"wa{h}", [P, TB, CTX]) for h in range(2)]
        wb = [sb(f"wb{h}", [P, TB, CTX]) for h in range(2)]
        wT = [sb(f"wT{h}", [CTX, S]) for h in range(2)]
        with nc.Block() as block:

            @block.sync
            def _(sp):
                sp.dma_start(wq[:, :, :], ins["w0xq"].rearrange("(c p) n -> p c n", p=P)).then_inc(loaded, 16)
                sp.dma_start(bq[:, :], ins["w0xb"]).then_inc(loaded, 16)
                sp.dma_start(desc[:, :, :], ins["w0xd"].rearrange("(c p) n -> p c n", p=P)).then_inc(loaded, 16)
                sp.dma_start(rows[:, :, :], ins["ctx"].rearrange("b n d -> n b d")).then_inc(loaded, 16)
                sp.dma_start(iota[:, :], ins["c_iota"][:, 0:CTX]).then_inc(loaded, 16)
                sp.dma_start(tok_i[:, :, :], ins["sets"].rearrange("(t p) k -> p t k", p=P)).then_inc(loaded, 16)

            @block.tensor
            def _(pe):
                pe.wait_ge(loaded, 96)
                for n in range(1, turns + 1):
                    for h in range(2):
                        b = 2 * (n - 1) + h
                        if n > 1:
                            pe.wait_ge(added[h], n - 1)
                        for e in range(DC):
                            for c in range(DC):
                                last = nc.tensor.matmul(k.ps[h][:, 0, e * S:(e + 1) * S], wq[:, c, e * P:(e + 1) * P],
                                                        k.xnT[:, c, b * S:(b + 1) * S], start=c == 0, stop=c == DC - 1)
                        last.then_inc(q_ready[h], 1)
                    for h in range(2):
                        pe.wait_ge(q_kept[h], n)
                        for t in range(TB):
                            for e in range(DC):
                                last = nc.tensor.matmul(k.ps[h][:, 1, t * CTX:(t + 1) * CTX], qT[h][:, e, t * P:(t + 1) * P],
                                                        desc[:, e, :], start=e == 0, stop=e == DC - 1)
                        last.then_inc(scored[h], 1)
                    for h in range(2):
                        pe.wait_ge(w_ready[h], n)
                        for t in range(TB):
                            last = nc.tensor.transpose(k.ps[h][0:CTX, 2, t * P:(t + 1) * P], wa[h][:, t, :], k.ident[:, :])
                        last.then_inc(w_turned[h], 1)
                    for h in range(2):
                        b = 2 * (n - 1) + h
                        pe.wait_ge(w_kept[h], n)
                        for t in range(TB):
                            last = nc.tensor.matmul(k.ps[h][:, 3, t * D:(t + 1) * D], wT[h][:, t * P:(t + 1) * P],
                                                    rows[:, b, :], start=True, stop=True)
                        last.then_inc(mixed[h], 1)

            @block.scalar
            def _(act):
                for n in range(1, turns + 1):
                    for h in range(2):
                        act.wait_ge(q_ready[h], n)
                        for e in range(DC):
                            last = nc.scalar.activation(qT[h][:, e, :], k.ps[h][:, 0, e * S:(e + 1) * S], ACT.Identity,
                                                        bias=bq[:, e:e + 1], scale=1.0)
                        last.then_inc(q_kept[h], 1)
                    for h in range(2):
                        act.wait_ge(gap_ready[h], n)
                        nc.scalar.activation(w2[h][:, :], gap[h][:, :], ACT.Exp).then_inc(gap_exp[h], 1)
                    for h in range(2):
                        act.wait_ge(w_turned[h], n)
                        nc.scalar.copy(wT[h][:, :], k.ps[h][0:CTX, 2, 0:S]).then_inc(w_kept[h], 1)

            @block.vector
            def _(dve):
                ch = Chain(dve, chain, 0)
                dve.wait_ge(loaded, 96)
                ch.link(nc.vector.tensor_copy(tok[:, :, :], tok_i[:, :, :]))
                for t in range(TB):
                    ch.link(nc.vector.tensor_scalar(mask[:, t, :], iota[:, :], tok[:, t, 0:1], None, ALU.is_equal))
                    for j in range(1, 4):
                        ch.link(nc.vector.scalar_tensor_tensor(mask[:, t, :], iota[:, :], tok[:, t, j:j + 1], mask[:, t, :],
                                                               ALU.is_equal, ALU.add))
                ch.link(nc.vector.tensor_scalar(mask[:, :, :], mask[:, :, :], 0.5, NEG, ALU.is_lt, ALU.mult))
                for n in range(1, turns + 1):
                    for h in range(2):
                        dve.wait_ge(scored[h], n)
                        ch.link(nc.vector.scalar_tensor_tensor(
                            sc[h][:, :, :], k.ps[h][:, 1, 0:TB * CTX].rearrange("p (t n) -> p t n", t=TB), scale,
                            mask[:, :, :], ALU.mult, ALU.add))
                        for t in range(TB):
                            last = nc.vector.max(best[h][:, t, :], sc[h][:, t, :])
                        ch.link(last)
                        for t in range(TB):
                            last = nc.vector.max_index(at[h][:, t, :], best[h][:, t, :], sc[h][:, t, :])
                        ch.link(last)
                        nc.vector.tensor_copy(atf[h][:, :, :], at[h][:, :, :])
                        nc.vector.tensor_tensor(gap[h][:, :], best[h][:, :, 1], best[h][:, :, 0], ALU.subtract)\
                            .then_inc(gap_ready[h], 1)
                    for h in range(2):
                        dve.wait_ge(gap_exp[h], n)
                        ch.link(nc.vector.tensor_scalar(w1[h][:, :], w2[h][:, :], 1.0, None, ALU.add))
                        ch.link(nc.vector.reciprocal(w1[h][:, :], w1[h][:, :]))
                        ch.link(nc.vector.tensor_tensor(w2[h][:, :], w2[h][:, :], w1[h][:, :], ALU.mult))
                        for t in range(TB):
                            nc.vector.tensor_scalar(wa[h][:, t, :], iota[:, :], atf[h][:, t, 0:1], w1[h][:, t:t + 1],
                                                    ALU.is_equal, ALU.mult)
                            last = nc.vector.tensor_scalar(wb[h][:, t, :], iota[:, :], atf[h][:, t, 1:2], w2[h][:, t:t + 1],
                                                           ALU.is_equal, ALU.mult)
                        ch.link(last)
                        nc.vector.tensor_tensor(wa[h][:, :, :], wa[h][:, :, :], wb[h][:, :, :], ALU.add).then_inc(w_ready[h], 1)
                    for h in range(2):
                        b = 2 * (n - 1) + h
                        dve.wait_ge(mixed[h], n)
                        xt = k.x[:, b * TB:(b + 1) * TB, :]
                        nc.vector.tensor_tensor(xt, xt, k.ps[h][:, 3, :].rearrange("p (t d) -> p t d", t=TB),
                                                ALU.add).then_inc(added[h], 1)


def experts(k):
    nc, ins = k.nc, k.ins
    GT = 4
    groups = NT // GT
    loaded, chain = k.sem("moe_loaded"), k.sem("moe_chain")
    routed, shifted, exps_done, w_made = k.sem("moe_routed"), k.sem("moe_shifted"), k.sem("moe_exps"), k.sem("moe_w_made")
    w_loaded = [k.sem(f"moe_w_loaded{q}") for q in range(2)]
    up_ready, silu_done, act_ready = k.sems("moe_up_ready"), k.sems("moe_silu_done"), k.sems("moe_act_ready")
    down_ready, added = k.sems("moe_down_ready"), k.sems("moe_added")
    with ExitStack() as st:
        def sb(name, shape, dt=F32):
            return k.sb(f"moe_{name}", shape, dt, st)

        router, bias, iota = sb("router", [P, DC, E0]), sb("bias", [P, E0]), sb("iota", [P, E0])
        lg = sb("lg", [P, NT, E0])
        best, at, atf = sb("best", [P, NT, 8]), sb("at", [P, NT, 8], U32), sb("atf", [P, NT, 8])
        ex, tot, rtot = sb("ex", [P, NT, TOPK0]), sb("tot", [P, NT]), sb("rtot", [P, NT])
        w = sb("w", [P, NT, E0])
        eq = [sb(f"eq{j}", [P, NT, E0]) for j in range(TOPK0)]
        wgu = [[sb(f"wgu{q}{h}", [P, DC, 2 * I0]) for h in range(2)] for q in range(2)]
        wd = [[sb(f"wd{q}{h}", [IC, 2, D]) for h in range(2)] for q in range(2)]
        sg = [sb(f"sg{h}", [IC, 2, GT * P]) for h in range(2)]
        hT = [sb(f"hT{h}", [IC, 2, GT * P]) for h in range(2)]

        def load_expert(sp, q, h, e):
            sp.dma_start(wgu[q][h][:, :, :], ins["w0gu"][ds(e, 1)].rearrange("e (c p) n -> p (e c) n", p=P))\
                .then_inc(w_loaded[q], 16)
            sp.dma_start(wd[q][h][:, :, :], ins["w0d"][ds(e, 1)].rearrange("e (c p) n -> p (e c) n", p=IC))\
                .then_inc(w_loaded[q], 16)

        with nc.Block() as block:

            @block.sync
            def _(sp):
                sp.dma_start(router[:, :, :], ins["w0r"].rearrange("(c p) n -> p c n", p=P)).then_inc(loaded, 16)
                sp.dma_start(bias[:, :], ins["w0rb"].partition_broadcast(P)).then_inc(loaded, 16)
                sp.dma_start(iota[:, :], ins["c_iota"][:, 0:E0]).then_inc(loaded, 16)
                for q in range(2):
                    for h in range(2):
                        load_expert(sp, q, h, 2 * q + h)
                with sp.Fori(1, E0 // 4) as j:
                    for q in range(2):
                        for h in range(2):
                            sp.wait_ge(added[h], j * (2 * groups) + (q - 1) * groups + 1)
                            load_expert(sp, q, h, j * 4 + (2 * q + h))

            @block.tensor
            def _(pe):
                pe.wait_ge(loaded, 48)
                for i in range(NT):
                    for c in range(DC):
                        last = nc.tensor.matmul(k.ps[0][:, 0, i * E0:(i + 1) * E0], k.xnT[:, c, i * P:(i + 1) * P],
                                                router[:, c, :], start=c == 0, stop=c == DC - 1)
                last.then_inc(routed, 1)
                pe.wait_ge(shifted, 1)
                with pe.Fori(0, E0 // 4) as j:
                    for q in range(2):
                        with pe.Fori(0, groups) as g:
                            n = j * (2 * groups) + g + (q * groups + 1)
                            for h in range(2):
                                pe.wait_ge(w_loaded[q], (j + 1) * 64)
                                pe.wait_ge(added[h], n)
                                for m in range(4):
                                    for c in range(DC):
                                        last = nc.tensor.matmul(k.ps[h][0:IC, m, :], wgu[q][h][:, c, m * IC:(m + 1) * IC],
                                                                k.xnT[:, c, ds(g * (GT * P), GT * P)],
                                                                start=c == 0, stop=c == DC - 1)
                                last.then_inc(up_ready[h], 1)
                            for h in range(2):
                                pe.wait_ge(act_ready[h], n)
                                for t in range(GT):
                                    for c in range(2):
                                        last = nc.tensor.matmul(k.ps[h][:, t // 2, (t % 2) * D:(t % 2 + 1) * D],
                                                                hT[h][:, c, t * P:(t + 1) * P], wd[q][h][:, c, :],
                                                                start=c == 0, stop=c == 1)
                                last.then_inc(down_ready[h], 1)

            @block.scalar
            def _(act):
                act.wait_ge(shifted, 1)
                nc.scalar.activation(ex[:, :, :], ex[:, :, :], ACT.Exp).then_inc(exps_done, 1)
                with act.Fori(0, E0 // 4) as j:
                    for q in range(2):
                        with act.Fori(0, groups) as g:
                            n = j * (2 * groups) + g + (q * groups + 1)
                            for h in range(2):
                                act.wait_ge(up_ready[h], n)
                                nc.scalar.activation(sg[h][:, :, :], k.ps[h][0:IC, 0:2, :], ACT.Silu).then_inc(silu_done[h], 1)

            @block.vector
            def _(dve):
                for h in range(2):
                    dve.sem_inc(added[h], 1)
                ch = Chain(dve, chain, 0)
                dve.wait_ge(routed, 1)
                ch.link(nc.vector.tensor_tensor(lg[:, :, :], k.ps[0][:, 0, 0:NT * E0].rearrange("p (t e) -> p t e", e=E0),
                                                bias[:, :].unsqueeze(1).to_broadcast([P, NT, E0]), ALU.add))
                for i in range(NT):
                    last = nc.vector.max(best[:, i, :], lg[:, i, :])
                ch.link(last)
                for i in range(NT):
                    last = nc.vector.max_index(at[:, i, :], best[:, i, :], lg[:, i, :])
                ch.link(last)
                nc.vector.tensor_tensor(ex[:, :, :], best[:, :, 0:TOPK0],
                                        best[:, :, 0:1].to_broadcast([P, NT, TOPK0]), ALU.subtract).then_inc(shifted, 1)
                ch.link(nc.vector.tensor_copy(atf[:, :, :], at[:, :, :]))
                dve.wait_ge(exps_done, 1)
                ch.link(nc.vector.tensor_reduce(tot[:, :], ex[:, :, :], AX_X, ALU.add))
                ch.link(nc.vector.reciprocal(rtot[:, :], tot[:, :]))
                ch.link(nc.vector.tensor_tensor(ex[:, :, :], ex[:, :, :],
                                                rtot[:, :].unsqueeze(2).to_broadcast([P, NT, TOPK0]), ALU.mult))
                for j in range(TOPK0):
                    last = nc.vector.tensor_tensor(eq[j][:, :, :], iota[:, :].unsqueeze(1).to_broadcast([P, NT, E0]),
                                                   atf[:, :, j:j + 1].to_broadcast([P, NT, E0]), ALU.is_equal)
                ch.link(last)
                for j in range(TOPK0):
                    last = nc.vector.tensor_tensor(eq[j][:, :, :], eq[j][:, :, :],
                                                   ex[:, :, j:j + 1].to_broadcast([P, NT, E0]), ALU.mult)
                ch.link(last)
                nc.vector.tensor_tensor(eq[0][:, :, :], eq[0][:, :, :], eq[1][:, :, :], ALU.add)
                ch.link(nc.vector.tensor_tensor(eq[2][:, :, :], eq[2][:, :, :], eq[3][:, :, :], ALU.add))
                ch.link(nc.vector.tensor_tensor(w[:, :, :], eq[0][:, :, :], eq[2][:, :, :], ALU.add))
                with dve.Fori(0, E0 // 4) as j:
                    for q in range(2):
                        with dve.Fori(0, groups) as g:
                            n = j * (2 * groups) + g + (q * groups + 1)
                            for h in range(2):
                                dve.wait_ge(silu_done[h], n)
                                nc.vector.tensor_tensor(hT[h][:, :, :], sg[h][:, :, :], k.ps[h][0:IC, 2:4, :], ALU.mult)\
                                    .then_inc(act_ready[h], 1)
                            for h in range(2):
                                dve.wait_ge(down_ready[h], n)
                                if h == 1:
                                    dve.wait_ge(added[0], n + 1)
                                for t in range(GT):
                                    xt = k.x[:, ds(g * GT + t, 1), :].rearrange("p a d -> p (a d)")
                                    sc = w[:, ds(g * GT + t, 1), ds(j * 4 + (2 * q + h), 1)].rearrange("p a e -> p (a e)")
                                    last = nc.vector.scalar_tensor_tensor(xt, k.ps[h][:, t // 2, (t % 2) * D:(t % 2 + 1) * D],
                                                                          sc, xt, ALU.mult, ALU.add)
                                last.then_inc(added[h], 1)


HK, VE, KC = 16, 256, 4


def delta_attention(k):
    nc, ins = k.nc, k.ins
    loaded, made = k.sem("dl_loaded"), k.sem("dl_made")
    gates_ready, gates_abs, gates_exp, gates_log = k.sem("dl_gates"), k.sem("dl_gabs"), k.sem("dl_gexp"), k.sem("dl_glog")
    loga_ready, cum_ready, cum_kept, cum_turned = k.sem("dl_loga"), k.sem("dl_cum"), k.sem("dl_cum_kept"), k.sem("dl_cumT")
    rows_kept, rows_stored, chain0 = k.sem("dl_rows_kept"), k.sem("dl_rows_stored"), k.sem("dl_setup_chain")
    w_loaded = [k.sem(f"dl_w_loaded{q}") for q in range(2)]
    projected = k.sems("dl_projected")
    tapped = k.sems("dl_tapped")
    convolved = k.sems("dl_convolved")
    tanh_done = k.sems("dl_tanh_done")
    silu_done = k.sems("dl_silu_done")
    squared = k.sems("dl_squared")
    lengths = k.sems("dl_lengths")
    lengths_kept = k.sems("dl_len_kept")
    inverse_len = k.sems("dl_inv_len")
    scales_ready = k.sems("dl_scales")
    masked = k.sems("dl_masked")
    decayed = k.sems("dl_decayed")
    v_turned = k.sems("dl_v_turned")
    v_scaled = k.sems("dl_v_scaled")
    products = k.sems("dl_products")
    lp_ready = k.sems("dl_lp_ready")
    nt_ready = k.sems("dl_nt_ready")
    t_turned = k.sems("dl_t_turned")
    t_kept = k.sems("dl_t_kept")
    off_ready = k.sems("dl_off_ready")
    off_kept = k.sems("dl_off_kept")
    solved = k.sems("dl_solved")
    w_kept = k.sems("dl_w_kept")
    rest_kept = k.sems("dl_rest_kept")
    mixed = k.sems("dl_mixed")
    mix_kept = k.sems("dl_mix_kept")
    out_ready = k.sems("dl_out_ready")
    added = k.sems("dl_added")
    chain = k.sems("dl_chain")
    levels = [1 << i for i in range(1, 7)]
    NL = len(levels)
    scratch = nc.dram_tensor("decay_rows", (HK, T), F32, kind="Internal").ap()
    with ExitStack() as st:
        def sb(name, shape, dt=F32):
            return k.sb(f"dl_{name}", shape, dt, st)

        wab = sb("wab", [P, DC, 2 * HK])
        taps = [sb(f"taps{q}", [P, 4, KC + 1]) for q in range(2)]
        tri, ones = sb("tri", [P, P]), sb("ones", [P, P])
        negstrict, maskadd = sb("negstrict", [P, P]), sb("maskadd", [P, P])
        lvl, lvl1T = sb("lvl", [P, NL, P]), sb("lvl1T", [P, P])
        za, zabs = sb("za", [P, NT, HK]), sb("zabs", [P, NT, 2 * HK])
        loga, beta = sb("loga", [P, NT, HK]), sb("beta", [P, NT, HK])
        cum, negcum = sb("cum", [P, NT, HK]), sb("negcum", [P, NT, HK])
        rows = sb("rows", [HK, T])
        wkqv = [sb(f"wkqv{q}", [P, DC, 4 * P]) for q in range(2)]
        wo = [sb(f"wo{q}", [P, 2, D]) for q in range(2)]
        grow = [sb(f"grow{q}", [P, T]) for q in range(2)]
        y = [sb(f"y{h}", [P, 4, S]) for h in range(2)]
        e = [sb(f"e{h}", [P, 4, S]) for h in range(2)]
        z = [sb(f"z{h}", [P, 4, S]) for h in range(2)]
        sq = [sb(f"sq{h}", [P, 2, S]) for h in range(2)]
        n2 = [sb(f"n2{h}", [P, 4]) for h in range(2)]
        rn = [sb(f"rn{h}", [P, 4]) for h in range(2)]
        nk = [sb(f"nk{h}", [P, TB]) for h in range(2)]
        cj = [sb(f"cj{h}", [P, TB]) for h in range(2)]
        gm = [sb(f"gm{h}", [P, 3 * P]) for h in range(2)]
        ng = [sb(f"ng{h}", [P, TB]) for h in range(2)]
        dec = [sb(f"dec{h}", [P, 3 * P]) for h in range(2)]
        vs = [sb(f"vs{h}", [P, TB, VE]) for h in range(2)]
        lp0 = [sb(f"lp0{h}", [P, 2, S]) for h in range(2)]
        lp1 = [sb(f"lp1{h}", [P, 2, P]) for h in range(2)]
        ntm = [sb(f"ntm{h}", [P, 2, P]) for h in range(2)]
        nt = [sb(f"nt{h}", [P, 2, P]) for h in range(2)]
        tt = [sb(f"tt{h}", [P, 2, 2, P]) for h in range(2)]
        off = [sb(f"off{h}", [P, 2, P]) for h in range(2)]
        wv = [sb(f"wv{h}", [P, 2, VE]) for h in range(2)]
        rest = [sb(f"rest{h}", [P, VE]) for h in range(2)]
        oT = [sb(f"oT{h}", [P, 2, S]) for h in range(2)]

        def load_head(sp, q, hd):
            sp.dma_start(wkqv[q][:, :, :], ins["w1kqv"][ds(hd, 1)].rearrange("e (c p) n -> p (e c) n", p=P))\
                .then_inc(w_loaded[q], 16)
            sp.dma_start(wo[q][:, :, :], ins["w1o"][ds(hd, 1)].rearrange("e (c p) n -> p (e c) n", p=P))\
                .then_inc(w_loaded[q], 16)
            sp.dma_start(taps[q][:, :, :], ins["w1t"][ds(hd, 1)].rearrange("e p m n -> p (e m) n")).then_inc(w_loaded[q], 16)
            sp.dma_start(grow[q][:, :], scratch[ds(hd, 1), :].rearrange("e t -> (e t)").partition_broadcast(P))\
                .then_inc(w_loaded[q], 16)

        UH = B // 2
        HP = HK // 2

        with nc.Block() as block:

            @block.sync
            def _(sp):
                for dst, name in ((tri[:, :], "c_tri"), (ones[:, :], "c_ones"), (negstrict[:, :], "c_negstrict"), (maskadd[:, :], "c_maskadd"),
                                  (lvl[:, :, :], "c_levels"), (lvl1T[:, :], "c_level1T")):
                    sp.dma_start(dst, ins[name]).then_inc(loaded, 16)
                sp.dma_start(wab[:, :, :], ins["w1ab"].rearrange("(c p) n -> p c n", p=P)).then_inc(loaded, 16)
                sp.wait_ge(rows_kept, 4)
                sp.dma_start(scratch, rows[:, :]).then_inc(rows_stored, 16)
                sp.wait_ge(rows_stored, 16)
                for q in range(2):
                    load_head(sp, q, q)
                with sp.Fori(1, HP) as j:
                    for q in range(2):
                        for h in range(2):
                            sp.wait_ge(added[h], j * (2 * UH) + (q - 1) * UH + 1)
                        load_head(sp, q, j * 2 + q)

            @block.gpsimd
            def _(pool):
                pool.wait_ge(loaded, 16 * 7)
                pool.wait_ge(cum_kept, 1)
                with pool.Fori(0, HP) as j:
                    for q in range(2):
                        with pool.Fori(0, UH) as p:
                            n = j * (2 * UH) + p + (q * UH + 1)
                            for h in range(2):
                                pool.wait_ge(w_loaded[q], (j + 1) * 64)
                                pool.wait_ge(decayed[h], n)
                                for blk, (c0, w) in enumerate(((0, S), (S, P))):
                                    t0 = p * (2 * S) + (h * S + blk * P)
                                    nc.gpsimd.tensor_tensor(gm[h][:, c0:c0 + P], grow[q][:, ds(t0, P)], maskadd[:, :], ALU.add)
                                nc.gpsimd.tensor_copy(ng[h][:, :], negcum[:, ds(p * (2 * TB) + h * TB, TB), ds(j * 2 + q, 1)]
                                                      .rearrange("p t a -> p (t a)"))
                                nc.gpsimd.tensor_copy(gm[h][:, P:S], grow[q][:, ds(p * (2 * S) + (h * S + P), P)])\
                                    .then_inc(masked[h], 1)
                            for h in range(2):
                                pool.wait_ge(silu_done[h], n)
                                nc.gpsimd.tensor_tensor(sq[h][:, :, :], z[h][:, 0:2, :], z[h][:, 0:2, :], ALU.mult)\
                                    .then_inc(squared[h], 1)
                            for h in range(2):
                                pool.wait_ge(lengths_kept[h], n)
                                nc.gpsimd.tensor_tensor(rn[h][:, :], n2[h][:, :], k.mhalf[:, 0:4], ALU.pow)\
                                    .then_inc(inverse_len[h], 1)
                            for h in range(2):
                                pool.wait_ge(lp_ready[h], n)
                                nc.gpsimd.tensor_tensor(ntm[h][:, 0, :], lp0[h][:, 0, 0:P], negstrict[:, :], ALU.mult)
                                nc.gpsimd.tensor_tensor(ntm[h][:, 1, :], lp1[h][:, 0, :], negstrict[:, :], ALU.mult)\
                                    .then_inc(made, 1)
                                pool.wait_ge(made, (n * 4) + (2 * h - 3))
                                nc.gpsimd.tensor_tensor(nt[h][:, :, :], ntm[h][:, :, :],
                                                        k.ident[:, :].unsqueeze(1).to_broadcast([P, 2, P]), ALU.add)\
                                    .then_inc(made, 1)
                                pool.wait_ge(made, (n * 4) + (2 * h - 2))
                                nc.gpsimd.tensor_tensor(tt[h][:, 1], nt[h][:, :, :],
                                                        lvl1T[:, :].unsqueeze(1).to_broadcast([P, 2, P]), ALU.mult)\
                                    .then_inc(nt_ready[h], 1)

            @block.tensor
            def _(pe):
                pe.wait_ge(loaded, 16 * 7)
                for i in range(NT):
                    for c in range(DC):
                        last = nc.tensor.matmul(k.ps[0][:, 0, i * 2 * HK:(i + 1) * 2 * HK], k.xnT[:, c, i * P:(i + 1) * P],
                                                wab[:, c, :], start=c == 0, stop=c == DC - 1)
                last.then_inc(gates_ready, 1)
                pe.wait_ge(loga_ready, 1)
                for i in range(NT):
                    o = k.ps[0][:, 1, i * HK:(i + 1) * HK]
                    last = nc.tensor.matmul(o, tri[:, :], loga[:, i, :], start=True, stop=i % TB == 0)
                    if i % TB:
                        last = nc.tensor.matmul(o, ones[:, :], loga[:, i - 1, :], start=False, stop=True)
                last.then_inc(cum_ready, 1)
                pe.wait_ge(cum_kept, 1)
                for i in range(NT):
                    last = nc.tensor.transpose(k.ps[1][0:HK, i // 4, (i % 4) * P:(i % 4 + 1) * P], cum[:, i, :], k.ident[:, :])
                last.then_inc(cum_turned, 1)
                pe.wait_ge(rows_kept, 4)
                with pe.Fori(0, HP) as j:
                    for q in range(2):
                        with pe.Fori(0, UH) as p:
                            n = j * (2 * UH) + p + (q * UH + 1)

                            def project(h):
                                pe.wait_ge(w_loaded[q], (j + 1) * 64)
                                pe.wait_ge(added[h], n)
                                for m in range(4):
                                    for c in range(DC):
                                        last = nc.tensor.matmul(k.ps[h][:, m // 2, (m % 2) * S:(m % 2 + 1) * S],
                                                                wkqv[q][:, c, m * P:(m + 1) * P],
                                                                k.xnT[:, c, ds(p * (2 * S) + h * S, S)],
                                                                start=c == 0, stop=c == DC - 1)
                                last.then_inc(projected[h], 1)

                            def products_of(h):
                                pe.wait_ge(silu_done[h], n)
                                nc.tensor.matmul(k.ps[h][:, 0, :].rearrange("p (a s) -> p a s", a=2), z[h][:, 0, 0:P],
                                                 z[h][:, 0:2, :], start=True, stop=True)
                                nc.tensor.matmul(k.ps[h][:, 1, 0:S].rearrange("p (a s) -> p a s", a=2), z[h][:, 0, P:S],
                                                 z[h][:, 0:2, P:S], start=True, stop=True).then_inc(products[h], 1)
                                for t in range(TB):
                                    for m in range(2):
                                        last = nc.tensor.transpose(k.ps[h][:, 3, (2 * t + m) * P:(2 * t + m + 1) * P],
                                                                   z[h][:, 2 + m, t * P:(t + 1) * P], k.ident[:, :])
                                last.then_inc(v_turned[h], 1)

                            def lengths_of(h):
                                pe.wait_ge(squared[h], n)
                                for m in range(2):
                                    for t in range(TB):
                                        last = nc.tensor.matmul(k.ps[h][:, 2, m * TB + t:m * TB + t + 1],
                                                                sq[h][:, m, t * P:(t + 1) * P], ones[:, 0:1],
                                                                start=True, stop=True)
                                last.then_inc(lengths[h], 1)

                            def turn_first(h):
                                pe.wait_ge(nt_ready[h], n)
                                for blk in range(2):
                                    last = nc.tensor.transpose(k.ps[h][:, 2, blk * P:(blk + 1) * P], tt[h][:, 1, blk, :],
                                                               k.ident[:, :])
                                last.then_inc(t_turned[h], 1)

                            def grow_off(h, i):
                                pe.wait_ge(t_kept[h], (n - 1) * (NL + 1) + (i + 1))
                                for blk in range(2):
                                    last = nc.tensor.matmul(k.ps[h][:, 2, blk * P:(blk + 1) * P], nt[h][:, blk, :],
                                                            tt[h][:, 0, blk, :], start=True, stop=True)
                                last.then_inc(off_ready[h], 1)

                            def grow_t(h, i):
                                pe.wait_ge(off_kept[h], (n - 1) * NL + (i + 1))
                                for blk in range(2):
                                    if i < NL - 1:
                                        nc.tensor.matmul(k.ps[h][:, 3, blk * P:(blk + 1) * P], tt[h][:, 1, blk, :],
                                                         off[h][:, blk, :], start=True, stop=True)
                                    last = nc.tensor.matmul(k.ps[h][:, 3, (2 + blk) * P:(3 + blk) * P], off[h][:, blk, :],
                                                            tt[h][:, 1, blk, :], start=True, stop=True)
                                last.then_inc(t_turned[h], 1)

                            def solve_first(h):
                                pe.wait_ge(t_kept[h], n * (NL + 1))
                                nc.tensor.matmul(k.ps[h][:, 0, 0:VE], tt[h][:, 1, 0, :], vs[h][:, 0, :],
                                                 start=True, stop=True).then_inc(solved[h], 1)

                            def solve_cross(h):
                                pe.wait_ge(w_kept[h], 2 * n - 1)
                                nc.tensor.matmul(k.ps[h][:, 0, VE:2 * VE], lp0[h][:, 0, P:S], wv[h][:, 0, :],
                                                 start=True, stop=True).then_inc(solved[h], 1)

                            def solve_second(h):
                                pe.wait_ge(rest_kept[h], n)
                                nc.tensor.matmul(k.ps[h][:, 1, 0:VE], tt[h][:, 1, 1, :], rest[h][:, :],
                                                 start=True, stop=True).then_inc(solved[h], 1)

                            def mix(h):
                                pe.wait_ge(w_kept[h], 2 * n)
                                for m in range(2):
                                    nc.tensor.matmul(k.ps[h][:, 2, m * S:(m + 1) * S], wv[h][:, 0, m * P:(m + 1) * P],
                                                     lp0[h][:, 1, :], start=True, stop=False)
                                    last = nc.tensor.matmul(k.ps[h][:, 2, m * S + P:(m + 1) * S], wv[h][:, 1, m * P:(m + 1) * P],
                                                            lp1[h][:, 1, :], start=False, stop=True)
                                last.then_inc(mixed[h], 1)

                            def give(h):
                                pe.wait_ge(mix_kept[h], n)
                                for t in range(TB):
                                    for m in range(2):
                                        last = nc.tensor.matmul(k.ps[h][:, 3, t * D:(t + 1) * D], oT[h][:, m, t * P:(t + 1) * P],
                                                                wo[q][:, m, :], start=m == 0, stop=m == 1)
                                last.then_inc(out_ready[h], 1)

                            for step in (project, products_of, lengths_of, turn_first):
                                for h in range(2):
                                    step(h)
                            for i in range(NL):
                                for h in range(2):
                                    grow_off(h, i)
                                for h in range(2):
                                    grow_t(h, i)
                            for step in (solve_first, solve_cross, solve_second, mix, give):
                                for h in range(2):
                                    step(h)

            @block.scalar
            def _(act):
                act.wait_ge(gates_abs, 1)
                nc.scalar.activation(zabs[:, :, :], zabs[:, :, :], ACT.Exp, scale=-1.0).then_inc(gates_exp, 1)
                act.wait_ge(gates_exp, 1)
                nc.scalar.activation(loga[:, :, :], zabs[:, :, 0:HK], ACT.Ln, bias=1.0, scale=1.0).then_inc(gates_log, 1)
                act.wait_ge(cum_turned, 1)
                for i in range(4):
                    nc.scalar.copy(rows[:, i * 512:(i + 1) * 512], k.ps[1][0:HK, i, :]).then_inc(rows_kept, 1)
                for h in range(2):
                    act.sem_inc(decayed[h], 1)
                with act.Fori(0, HP) as j:
                    for q in range(2):
                        with act.Fori(0, UH) as p:
                            n = j * (2 * UH) + p + (q * UH + 1)

                            def tap(h):
                                act.wait_ge(projected[h], n)
                                for m in range(4):
                                    last = nc.scalar.activation(y[h][:, m, :], k.ps[h][:, m // 2, (m % 2) * S:(m % 2 + 1) * S],
                                                                ACT.Identity,
                                                                bias=taps[q][:, m, KC:KC + 1], scale=taps[q][:, m, KC - 1:KC])
                                last.then_inc(tapped[h], 1)

                            def tanh_of(h):
                                act.wait_ge(convolved[h], n)
                                nc.scalar.activation(e[h][:, :, :], y[h][:, :, :], ACT.Tanh, scale=0.5).then_inc(tanh_done[h], 1)

                            def decay(h):
                                act.wait_ge(masked[h], n)
                                for blk, (c0, w) in enumerate(((0, S), (S, P))):
                                    last = nc.scalar.activation(dec[h][:, c0:c0 + w], gm[h][:, c0:c0 + w], ACT.Exp,
                                                                bias=ng[h][:, blk:blk + 1], scale=1.0)
                                last.then_inc(decayed[h], 1)

                            def scale_v(h):
                                act.wait_ge(v_turned[h], n)
                                act.wait_ge(scales_ready[h], n)
                                for t in range(TB):
                                    last = nc.scalar.activation(vs[h][:, t, :], k.ps[h][:, 3, t * VE:(t + 1) * VE], ACT.Copy,
                                                                scale=nk[h][:, t:t + 1])
                                last.then_inc(v_scaled[h], 1)

                            def keep_first(h):
                                act.wait_ge(t_turned[h], (n - 1) * (NL + 1) + 1)
                                nc.scalar.copy(tt[h][:, 0, :, :], k.ps[h][:, 2, 0:S].rearrange("p (b s) -> p b s", b=2))\
                                    .then_inc(t_kept[h], 1)

                            def keep_t(h, i):
                                act.wait_ge(t_turned[h], (n - 1) * (NL + 1) + (i + 2))
                                if i < NL - 1:
                                    ins_ = nc.scalar.copy(tt[h][:, :, :, :],
                                                          k.ps[h][:, 3, :].rearrange("p (a b s) -> p a b s", a=2, b=2))
                                else:
                                    ins_ = nc.scalar.copy(tt[h][:, 1, :, :], k.ps[h][:, 3, S:2 * S].rearrange("p (b s) -> p b s", b=2))
                                ins_.then_inc(t_kept[h], 1)

                            def keep_w(h, blk):
                                act.wait_ge(solved[h], 3 * n - 2 + 2 * blk)
                                nc.scalar.copy(wv[h][:, blk, :], k.ps[h][:, blk, 0:VE]).then_inc(w_kept[h], 1)

                            def keep_mix(h):
                                act.wait_ge(mixed[h], n)
                                nc.scalar.copy(oT[h][:, :, :], k.ps[h][:, 2, :].rearrange("p (m s) -> p m s", m=2))\
                                    .then_inc(mix_kept[h], 1)

                            for step in (tap, decay, tanh_of, scale_v, keep_first):
                                for h in range(2):
                                    step(h)
                            for i in range(NL):
                                for h in range(2):
                                    keep_t(h, i)
                            for h in range(2):
                                keep_w(h, 0)
                            for h in range(2):
                                keep_w(h, 1)
                            for h in range(2):
                                keep_mix(h)

            @block.vector
            def _(dve):
                for h in range(2):
                    dve.sem_inc(added[h], 1)
                ch = Chain(dve, chain0, 0)
                dve.wait_ge(gates_ready, 1)
                zz = k.ps[0][:, 0, :].rearrange("p (t e) -> p t e", t=NT)
                ch.link(nc.vector.tensor_copy(za[:, :, :], zz[:, :, 0:HK]))
                nc.vector.scalar_tensor_tensor(zabs[:, :, 0:HK], zz[:, :, 0:HK], -1.0, za[:, :, :], ALU.mult, ALU.max)
                nc.vector.tensor_copy(zabs[:, :, HK:2 * HK], zz[:, :, HK:2 * HK]).then_inc(gates_abs, 1)
                dve.wait_ge(gates_exp, 1)
                ch.link(nc.vector.tensor_scalar(beta[:, :, :], zabs[:, :, HK:2 * HK], 1.0, None, ALU.add))
                ch.link(nc.vector.reciprocal(beta[:, :, :], beta[:, :, :]))
                dve.wait_ge(gates_log, 1)
                nc.vector.scalar_tensor_tensor(loga[:, :, :], za[:, :, :], 0.0, loga[:, :, :], ALU.min, ALU.subtract)\
                    .then_inc(loga_ready, 1)
                dve.wait_ge(cum_ready, 1)
                cp = k.ps[0][:, 1, 0:NT * HK].rearrange("p (t e) -> p t e", t=NT)
                nc.vector.tensor_scalar(negcum[:, :, :], cp, -1.0, None, ALU.mult)
                nc.vector.tensor_copy(cum[:, :, :], cp).then_inc(cum_kept, 1)
                dve.wait_ge(cum_kept, 1)
                with dve.Fori(0, HP) as j:
                    for q in range(2):
                        with dve.Fori(0, UH) as p:
                            n = j * (2 * UH) + p + (q * UH + 1)
                            head = j * 2 + q
                            LK = 3
                            chains = [Chain(dve, chain[h], (n - 1) * LK) for h in range(2)]

                            def convolve(h):
                                dve.wait_ge(tapped[h], n)
                                for back in range(1, KC):
                                    for m in range(4):
                                        last = nc.vector.scalar_tensor_tensor(
                                            y[h][:, m, back:S], k.ps[h][:, m // 2, (m % 2) * S:(m % 2 + 1) * S - back],
                                            taps[q][:, m, KC - 1 - back:KC - back],
                                            y[h][:, m, back:S], ALU.mult, ALU.add)
                                    if back < KC - 1:
                                        chains[h].link(last)
                                last.then_inc(convolved[h], 1)

                            def silu(h):
                                dve.wait_ge(tanh_done[h], n)
                                nc.vector.scalar_tensor_tensor(z[h][:, :, :], e[h][:, :, :], 1.0, y[h][:, :, :], ALU.add,
                                                               ALU.mult).then_inc(silu_done[h], 1)

                            def keep_lengths(h):
                                dve.wait_ge(lengths[h], n)
                                nc.vector.tensor_scalar(n2[h][:, :], k.ps[h][:, 2, 0:4], 4e-24, None, ALU.max)\
                                    .then_inc(lengths_kept[h], 1)

                            def scales(h):
                                dve.wait_ge(inverse_len[h], n)
                                nc.vector.scalar_tensor_tensor(nk[h][:, :], n2[h][:, 0:TB], 0.5, rn[h][:, 0:TB], ALU.mult, ALU.mult)
                                bt = beta[:, ds(p * (2 * TB) + h * TB, TB), ds(head, 1)].rearrange("p t a -> p (t a)")
                                chains[h].link(nc.vector.tensor_tensor(cj[h][:, :], bt, rn[h][:, 0:TB], ALU.mult))
                                nc.vector.tensor_tensor(cj[h][:, :], cj[h][:, :], rn[h][:, 0:TB], ALU.mult)\
                                    .then_inc(scales_ready[h], 1)

                            def lp(h):
                                dve.wait_ge(scales_ready[h], n)
                                dve.wait_ge(products[h], n)
                                dve.wait_ge(decayed[h], n + 1)
                                nc.vector.scalar_tensor_tensor(lp0[h][:, :, :], k.ps[h][:, 0, :].rearrange("p (a s) -> p a s", a=2),
                                                               cj[h][:, 0:1],
                                                               dec[h][:, 0:S].unsqueeze(1).to_broadcast([P, 2, S]),
                                                               ALU.mult, ALU.mult)
                                nc.vector.scalar_tensor_tensor(lp1[h][:, :, :], k.ps[h][:, 1, 0:S].rearrange("p (a s) -> p a s", a=2),
                                                               cj[h][:, 1:2],
                                                               dec[h][:, S:S + P].unsqueeze(1).to_broadcast([P, 2, P]),
                                                               ALU.mult, ALU.mult).then_inc(lp_ready[h], 1)

                            def keep_off(h, i):
                                dve.wait_ge(off_ready[h], (n - 1) * NL + (i + 1))
                                nc.vector.tensor_tensor(off[h][:, :, :], k.ps[h][:, 2, 0:S].rearrange("p (b s) -> p b s", b=2),
                                                        lvl[:, i:i + 1, :].to_broadcast([P, 2, P]), ALU.mult)\
                                    .then_inc(off_kept[h], 1)

                            def keep_rest(h):
                                dve.wait_ge(solved[h], 3 * n - 1)
                                dve.wait_ge(v_scaled[h], n)
                                nc.vector.tensor_tensor(rest[h][:, :], vs[h][:, 1, :], k.ps[h][:, 0, VE:2 * VE], ALU.subtract)\
                                    .then_inc(rest_kept[h], 1)

                            def add_out(h):
                                dve.wait_ge(out_ready[h], n)
                                for t in range(TB):
                                    xt = k.x[:, ds(p * (2 * TB) + (h * TB + t), 1), :].rearrange("p a d -> p (a d)")
                                    last = nc.vector.scalar_tensor_tensor(xt, k.ps[h][:, 3, t * D:(t + 1) * D],
                                                                          rn[h][:, TB + t:TB + t + 1], xt, ALU.mult, ALU.add)
                                last.then_inc(added[h], 1)

                            for step in (convolve, silu, keep_lengths, scales, lp):
                                for h in range(2):
                                    step(h)
                            for i in range(NL):
                                for h in range(2):
                                    keep_off(h, i)
                            for h in range(2):
                                keep_rest(h)
                            for h in range(2):
                                add_out(h)
                            assert chains[0].count == 3


class CrossRope:

    TWO_PI = (6.28125, 0.0019350051879882812, 3.019915981956753e-07)
    ROUND = 12582912.0

    def __init__(self, k, stack):
        nc, ins = k.nc, k.ins
        loaded, chain = k.sem("rope_loaded"), k.sem("rope_chain")
        reduced, sines = k.sem("rope_reduced"), k.sem("rope_sines")
        self.cq, self.sq_, self.ck, self.sk = [k.sb(f"rope_{n}", [P, NT, HD], F32, stack) for n in ("cq", "sq", "ck", "sk")]
        self.cc, self.sc = [k.sb(f"rope_{n}", [CTX, B, HD], F32, stack) for n in ("cc", "sc")]
        self.ctxT = k.sb("rope_ctxT", [P, DC, B * CTX], F32, stack)
        with ExitStack() as st:
            pos_i, cpos_i = k.sb("pos_i", [P, NT], I32, st), k.sb("cpos_i", [CTX, B], I32, st)
            pos, cpos = k.sb("pos", [P, NT], F32, st), k.sb("cpos", [CTX, B], F32, st)
            inv = k.sb("inv", [P, HALF], F32, st)
            wn = k.sb("wn", [P, 2, HD], F32, st)
            ang, turns, r, r2 = [k.sb(f"rope_t{i}", [P, NT, HALF], F32, st) for i in range(4)]
            cang, cturns, cr, cr2 = [k.sb(f"rope_u{i}", [CTX, B, HALF], F32, st) for i in range(4)]
            with nc.Block() as block:

                @block.sync
                def _(sp):
                    for dst, name in ((pos_i[:, :], "pos"), (cpos_i[:, :], "cpos")):
                        sp.dma_start(dst, ins[name]).then_inc(loaded, 16)
                    sp.dma_start(inv[:, :], ins["c_inv"]).then_inc(loaded, 16)
                    for i, name in enumerate(("w1xqn", "w1xkn")):
                        sp.dma_start(wn[:, i, :], ins[name].partition_broadcast(P)).then_inc(loaded, 16)
                    sp.dma_start(self.ctxT[:, :, :], ins["ctxT"].rearrange("(c p) n -> p c n", p=P)).then_inc(loaded, 16)
                    sp.wait_ge(loaded, 96)

                @block.scalar
                def _(act):
                    act.wait_ge(reduced, 1)
                    for a in (r, r2, cr, cr2):
                        last = nc.scalar.activation(a[:, :, :], a[:, :, :], ACT.Sin)
                    last.then_inc(sines, 1)

                @block.vector
                def _(dve):
                    ch = Chain(dve, chain, 0)
                    dve.wait_ge(loaded, 96)
                    for p_i, p_f, a, tu, rr, rh, m, rows in ((pos_i, pos, ang, turns, r, r2, NT, P),
                                                             (cpos_i, cpos, cang, cturns, cr, cr2, B, CTX)):
                        ch.link(nc.vector.tensor_copy(p_f[:, :], p_i[:, :]))
                        ch.link(nc.vector.tensor_tensor(a[:, :, :], inv[0:rows, :].unsqueeze(1).to_broadcast([rows, m, HALF]),
                                                        p_f[:, :].unsqueeze(2).to_broadcast([rows, m, HALF]), ALU.mult))
                        ch.link(nc.vector.tensor_scalar(tu[:, :, :], a[:, :, :], float(1 / (2 * np.pi)), self.ROUND,
                                                        ALU.mult, ALU.add))
                        ch.link(nc.vector.tensor_scalar(tu[:, :, :], tu[:, :, :], self.ROUND, None, ALU.subtract))
                        for part in self.TWO_PI:
                            ch.link(nc.vector.scalar_tensor_tensor(a[:, :, :], tu[:, :, :], -part, a[:, :, :], ALU.mult, ALU.add))
                        ch.link(nc.vector.tensor_scalar(rr[:, :, :], a[:, :, :], float(-np.float32(np.pi)),
                                                        3.1415925, ALU.max, ALU.min))
                        last = nc.vector.tensor_scalar(rh[:, :, :], rr[:, :, :], 0.5, None, ALU.mult)
                        ch.link(last)
                    dve.sem_inc(reduced, 1)
                    dve.wait_ge(sines, 1)
                    for rr, rh, m, rows, outs in ((r, r2, NT, P, ((self.cq, self.sq_, 0), (self.ck, self.sk, 1))),
                                                  (cr, cr2, B, CTX, ((self.cc, self.sc, 1),))):
                        ch.link(nc.vector.tensor_tensor(rh[:, :, :], rh[:, :, :], rh[:, :, :], ALU.mult))
                        ch.link(nc.vector.tensor_scalar(rh[:, :, :], rh[:, :, :], -2.0, 1.0, ALU.mult, ALU.add))
                        for co, si, i in outs:
                            for a0, b0, sign in ((0, HALF, -1.0), (HALF, 0, 1.0)):
                                wa = wn[0:rows, i:i + 1, a0:a0 + HALF].to_broadcast([rows, m, HALF])
                                wb = wn[0:rows, i:i + 1, b0:b0 + HALF].to_broadcast([rows, m, HALF])
                                nc.vector.tensor_tensor(co[:, :, a0:a0 + HALF], rh[:, :, :], wa, ALU.mult)
                                last = nc.vector.scalar_tensor_tensor(si[:, :, a0:a0 + HALF], rr[:, :, :], sign, wb,
                                                                      ALU.mult, ALU.mult)
                    ch.link(last)

    def q(self, p, h):
        return (t[:, ds(p * (2 * TB) + h * TB, TB), :] for t in (self.cq, self.sq_))

    def k(self, p, h):
        return (t[:, ds(p * (2 * TB) + h * TB, TB), :] for t in (self.ck, self.sk))

    def c(self, p, h):
        return (t[:, ds(p * 2 + h, 1), :].rearrange("p a d -> p (a d)") for t in (self.cc, self.sc))


E1, EK, TOPK1, I1, CAP = 128, 48, 8, 96, 96
SLOTS = EK * CAP
FAR = float(1 << 20)


def sparse_experts(k):
    nc, ins = k.nc, k.ins
    ZN = 4
    EU = 4
    loaded, chain = k.sem("sp_loaded"), k.sem("sp_chain")
    logits_ready, shifted, exps_done = k.sem("sp_logits"), k.sem("sp_shifted"), k.sem("sp_exps")
    chosen, before_ready, slots_ready = k.sem("sp_chosen"), k.sem("sp_before"), k.sem("sp_slots")
    zero_made, zeroed, scattered = k.sem("sp_zero_made"), k.sem("sp_zeroed"), k.sem("sp_scattered")
    in_loaded = [[k.sem(f"sp_in{q}{h}") for h in range(2)] for q in range(2)]
    turned, x_kept, up_ready = k.sems("sp_turned"), k.sems("sp_x_kept"), k.sems("sp_up_ready")
    silu_done, act_ready, down_ready = k.sems("sp_silu"), k.sems("sp_act"), k.sems("sp_down")
    y_kept, y_stored = k.sems("sp_y_kept"), k.sems("sp_y_stored")
    gathered = [k.sem(f"sp_gathered{h}") for h in range(2)]
    combined, out_stored = k.sem("sp_combined"), k.sem("sp_out_stored")
    add_chain = k.sem("sp_add_chain")
    xrows = nc.dram_tensor("slot_rows", (SLOTS, D), F32, kind="Internal").ap()
    yrows = nc.dram_tensor("slot_results", (SLOTS, D), F32, kind="Internal").ap()
    with ExitStack() as st:
        def sb(name, shape, dt=F32, stack=st):
            return k.sb(f"sp_{name}", shape, dt, stack)

        w = sb("w", [P, NT, TOPK1])
        slot_i = sb("slot_i", [P, NT, TOPK1], U32)
        zero = sb("zero", [P, SLOTS * D // P // ZN])
        wgu = [[sb(f"wgu{q}{h}", [P, EU * DC, 2 * I1]) for h in range(2)] for q in range(2)]
        wd = [[sb(f"wd{q}{h}", [I1, EU, D]) for h in range(2)] for q in range(2)]
        xs = [[sb(f"xs{q}{h}", [CAP, EU, D]) for h in range(2)] for q in range(2)]

        with ExitStack() as st1:
            def sb1(name, shape, dt=F32):
                return sb(name, shape, dt, st1)

            gate = sb1("gate", [P, DC, E1])
            o2n_i, o2n = sb1("o2n_i", [P, E1], I32), sb1("o2n", [P, E1])
            neg, base = sb1("neg", [P, E1]), sb1("base", [P, E1])
            iota = sb1("iota", [P, E1])
            trib, onesb = sb1("trib", [P, P], BF16), sb1("onesb", [P, P], BF16)
            lg, left = sb1("lg", [P, NT, E1]), sb1("left", [P, NT, E1])
            best, at, atf = sb1("best", [P, NT, 8]), sb1("at", [P, NT, 8], U32), sb1("atf", [P, NT, 8])
            tot, rtot = sb1("tot", [P, NT]), sb1("rtot", [P, NT])
            m = sb1("m", [P, NT, E1], BF16)
            mc = sb1("mc", [P, NT, E1], BF16)
            far = sb1("far", [P, NT, E1])
            table = sb1("table", [P, NT, E1])
            junk = [sb1(f"junk{i}", [P, E1]) for i in range(TOPK1)]
            slot_f = sb1("slot_f", [P, NT, TOPK1])
            ok = sb1("ok", [P, NT, TOPK1])
            NB = NT * E1 // 512
            with nc.Block() as block:

                @block.sync
                def _(sp):
                    sp.dma_start(gate[:, :, :], ins["w1r"].rearrange("(c p) n -> p c n", p=P)).then_inc(loaded, 16)
                    sp.dma_start(o2n_i[:, :], ins["o2n"].partition_broadcast(P)).then_inc(loaded, 16)
                    sp.dma_start(iota[:, :], ins["c_iota"]).then_inc(loaded, 16)
                    sp.dma_start(trib[:, :], ins["c_trib"]).then_inc(loaded, 16)
                    sp.dma_start(onesb[:, :], ins["c_onesb"]).then_inc(loaded, 16)
                    sp.wait_ge(zero_made, 1)
                    for i in range(ZN):
                        sp.dma_start(xrows.rearrange("(i p a) d -> i p (a d)", i=ZN, p=P)[i], zero[:, :]).then_inc(zeroed, 16)
                    sp.wait_ge(scattered, 16 * NT * TOPK1)

                @block.gpsimd
                def _(pool):
                    nc.gpsimd.memset(zero[:, :], 0.0).then_inc(zero_made, 1)
                    pool.wait_ge(zeroed, 16 * ZN)
                    pool.wait_ge(slots_ready, 1)
                    for i in range(NT):
                        for j in range(TOPK1):
                            nc.gpsimd.indirect_dma_start(
                                out=xrows, out_offset=bass.IndirectOffsetOnAxis(slot_i[:, i, j:j + 1], axis=0),
                                in_=k.xn_rows[:, i, :], in_offset=None, bounds_check=SLOTS - 1,
                                oob_is_err=False).then_inc(scattered, 16)
                    pool.wait_ge(scattered, 16 * NT * TOPK1)

                @block.tensor
                def _(pe):
                    pe.wait_ge(loaded, 80)
                    for i in range(NT):
                        for c in range(DC):
                            last = nc.tensor.matmul(k.ps[0][:, i // 4, (i % 4) * E1:(i % 4 + 1) * E1],
                                                    k.xnT[:, c, i * P:(i + 1) * P], gate[:, c, :], start=c == 0, stop=c == DC - 1)
                    last.then_inc(logits_ready, 1)
                    pe.wait_ge(chosen, 1)
                    for i in range(NT):
                        o = k.ps[1][:, i // 4, (i % 4) * E1:(i % 4 + 1) * E1]
                        last = nc.tensor.matmul(o, trib[:, :], m[:, i, :], start=True, stop=i == 0)
                        if i:
                            last = nc.tensor.matmul(o, onesb[:, :], mc[:, i - 1, :], start=False, stop=True)
                    last.then_inc(before_ready, 1)

                @block.scalar
                def _(act):
                    act.wait_ge(shifted, 1)
                    nc.scalar.activation(w[:, :, :], w[:, :, :], ACT.Exp).then_inc(exps_done, 1)

                @block.vector
                def _(dve):
                    ch = Chain(dve, chain, 0)
                    dve.wait_ge(loaded, 80)
                    ch.link(nc.vector.tensor_copy(o2n[:, :], o2n_i[:, :]))
                    nc.vector.tensor_scalar(neg[:, :], o2n[:, :], -1.0, NEG, ALU.is_equal, ALU.mult)
                    ch.link(nc.vector.tensor_scalar(junk[0][:, :], o2n[:, :], 0.0, FAR, ALU.is_lt, ALU.mult))
                    ch.link(nc.vector.scalar_tensor_tensor(base[:, :], o2n[:, :], float(CAP), junk[0][:, :], ALU.mult, ALU.add))
                    dve.wait_ge(logits_ready, 1)
                    ch.link(nc.vector.tensor_tensor(lg[:, :, :], k.ps[0][:, 0:NB, :].rearrange("p a (t e) -> p (a t) e", e=E1),
                                                    neg[:, :].unsqueeze(1).to_broadcast([P, NT, E1]), ALU.add))
                    for i in range(NT):
                        last = nc.vector.max(best[:, i, :], lg[:, i, :])
                    ch.link(last)
                    for i in range(NT):
                        last = nc.vector.max_index(at[:, i, :], best[:, i, :], lg[:, i, :])
                    for i in range(NT):
                        last = nc.vector.match_replace(out=left[:, i, :], in_to_replace=best[:, i, :], in_values=lg[:, i, :],
                                                       imm_value=2 * NEG)
                    ch.link(last)
                    nc.vector.tensor_tensor(w[:, :, :], best[:, :, :], best[:, :, 0:1].to_broadcast([P, NT, TOPK1]),
                                            ALU.subtract).then_inc(shifted, 1)
                    nc.vector.tensor_copy(atf[:, :, :], at[:, :, :])
                    ch.link(nc.vector.tensor_scalar(m[:, :, :], left[:, :, :], 2 * NEG, None, ALU.is_equal))
                    ch.link(nc.vector.tensor_copy(mc[:, 0, :], m[:, 0, :]))
                    for i in range(1, NT):
                        ch.link(nc.vector.tensor_tensor(mc[:, i, :], mc[:, i - 1, :], m[:, i, :], ALU.add))
                    dve.sem_inc(chosen, 1)
                    dve.wait_ge(before_ready, 1)
                    before = k.ps[1][:, 0:NB, :].rearrange("p a (t e) -> p (a t) e", e=E1)
                    nc.vector.tensor_scalar(far[:, :, :], before, CAP - 0.5, FAR, ALU.is_gt, ALU.mult)
                    ch.link(nc.vector.tensor_tensor(table[:, :, :], before,
                                                    base[:, :].unsqueeze(1).to_broadcast([P, NT, E1]), ALU.add))
                    ch.link(nc.vector.tensor_tensor(table[:, :, :], table[:, :, :], far[:, :, :], ALU.add))
                    for i in range(NT):
                        for j in range(TOPK1):
                            last = nc.vector.scalar_tensor_tensor(junk[j][:, :], iota[:, :], atf[:, i, j:j + 1], table[:, i, :],
                                                                  ALU.is_equal, ALU.mult, accum_out=slot_f[:, i, j:j + 1])
                        ch.link(last)
                    ch.link(nc.vector.tensor_copy(slot_i[:, :, :], slot_f[:, :, :]))
                    dve.sem_inc(slots_ready, 1)
                    dve.wait_ge(exps_done, 1)
                    ch.link(nc.vector.tensor_reduce(tot[:, :], w[:, :, :], AX_X, ALU.add))
                    ch.link(nc.vector.reciprocal(rtot[:, :], tot[:, :]))
                    nc.vector.tensor_scalar(ok[:, :, :], slot_f[:, :, :], SLOTS - 0.5, None, ALU.is_lt)
                    ch.link(nc.vector.tensor_tensor(w[:, :, :], w[:, :, :], rtot[:, :].unsqueeze(2).to_broadcast([P, NT, TOPK1]),
                                                    ALU.mult))
                    ch.link(nc.vector.tensor_tensor(w[:, :, :], w[:, :, :], ok[:, :, :], ALU.mult))

        xT = [sb(f"xT{h}", [P, 2, 4 * CAP]) for h in range(2)]
        sg = [sb(f"sg{h}", [I1, EU, CAP]) for h in range(2)]
        hT = [sb(f"hT{h}", [I1, EU, CAP]) for h in range(2)]
        y = [sb(f"y{h}", [CAP, EU, D]) for h in range(2)]
        UN = EK // EU // 4
        with nc.Block() as block:

            @block.sync
            def _(sp):
                def load(q, h, e):
                    s = in_loaded[q][h]
                    sp.dma_start(xs[q][h][:, :, :], xrows.rearrange("(e c) d -> e c d", c=CAP)[ds(e, EU)]
                                 .rearrange("e c d -> c e d")).then_inc(s, 16)
                    sp.dma_start(wgu[q][h][:, :, :], ins["w1gu"][ds(e, EU)].rearrange("e (c p) n -> p (e c) n", p=P))\
                        .then_inc(s, 16)
                    sp.dma_start(wd[q][h][:, :, :], ins["w1d"][ds(e, EU)].rearrange("e p n -> p e n")).then_inc(s, 16)

                for q in range(2):
                    for h in range(2):
                        load(q, h, (2 * q + h) * EU)
                with sp.Fori(1, UN) as j:
                    for q in range(2):
                        for h in range(2):
                            sp.wait_ge(down_ready[h], j * 2 + (q - 1))
                            load(q, h, j * (4 * EU) + (2 * q + h) * EU)

            @block.tensor
            def _(pe):
                with pe.Fori(0, UN) as j:
                    for q in range(2):
                        n = j * 2 + (q + 1)
                        for h in range(2):
                            pe.wait_ge(in_loaded[q][h], (j + 1) * 48)
                            if q == 1:
                                pe.wait_ge(y_kept[h], n - 1)
                            for e in range(EU):
                                for c in range(DC):
                                    last = nc.tensor.transpose(
                                        k.ps[h][:, e // 2, (e % 2 * 2 + c) * CAP:(e % 2 * 2 + c + 1) * CAP],
                                        xs[q][h][:, e, c * P:(c + 1) * P], k.ident[0:CAP, 0:CAP])
                            last.then_inc(turned[h], 1)
                        for h in range(2):
                            pe.wait_ge(x_kept[h], n)
                            for e in range(EU):
                                for gu in range(2):
                                    for c in range(DC):
                                        last = nc.tensor.matmul(
                                            k.ps[h][0:I1, 2 + e // 2, (e % 2 * 2 + gu) * CAP:(e % 2 * 2 + gu + 1) * CAP],
                                            wgu[q][h][:, e * DC + c, gu * I1:(gu + 1) * I1],
                                            xT[h][:, e // 2, (e % 2 * 2 + c) * CAP:(e % 2 * 2 + c + 1) * CAP],
                                            start=c == 0, stop=c == DC - 1)
                            last.then_inc(up_ready[h], 1)
                        for h in range(2):
                            pe.wait_ge(act_ready[h], n)
                            for e in range(EU):
                                last = nc.tensor.matmul(k.ps[h][0:CAP, e // 2, (e % 2) * D:(e % 2 + 1) * D], hT[h][:, e, :],
                                                        wd[q][h][:, e, :], start=True, stop=True)
                            last.then_inc(down_ready[h], 1)
                        if q == 1:
                            for h in range(2):
                                pe.wait_ge(y_kept[h], n)

            @block.scalar
            def _(act):
                for h in range(2):
                    act.sem_inc(y_stored[h], 16)
                with act.Fori(0, UN) as j:
                    for q in range(2):
                        n = j * 2 + (q + 1)
                        for h in range(2):
                            act.wait_ge(turned[h], n)
                            nc.scalar.copy(xT[h][:, :, :], k.ps[h][:, 0:2, 0:4 * CAP]).then_inc(x_kept[h], 1)
                        for h in range(2):
                            act.wait_ge(up_ready[h], n)
                            nc.scalar.activation(sg[h][:, :, :].rearrange("p (a b) c -> p a b c", a=2),
                                                 k.ps[h][0:I1, 2:4, 0:4 * CAP].rearrange("p a (b g c) -> p a b g c", b=2, g=2)[:, :, :, 0],
                                                 ACT.Silu).then_inc(silu_done[h], 1)
                        for h in range(2):
                            act.wait_ge(y_kept[h], n)
                            act.dma_start(yrows.rearrange("(e c) d -> e c d", c=CAP)[ds(j * (4 * EU) + (2 * q + h) * EU, EU)]
                                          .rearrange("e c d -> c e d"), y[h][:, :, :]).then_inc(y_stored[h], 16)
                for h in range(2):
                    act.wait_ge(y_stored[h], 16 * 2 * UN + 16)

            @block.vector
            def _(dve):
                with dve.Fori(0, UN) as j:
                    for q in range(2):
                        n = j * 2 + (q + 1)
                        for h in range(2):
                            dve.wait_ge(silu_done[h], n)
                            nc.vector.tensor_tensor(hT[h][:, :, :].rearrange("p (a b) c -> p a b c", a=2),
                                                    sg[h][:, :, :].rearrange("p (a b) c -> p a b c", a=2),
                                                    k.ps[h][0:I1, 2:4, 0:4 * CAP].rearrange("p a (b g c) -> p a b g c", b=2, g=2)[:, :, :, 1],
                                                    ALU.mult).then_inc(act_ready[h], 1)
                        for h in range(2):
                            dve.wait_ge(down_ready[h], n)
                            dve.wait_ge(y_stored[h], n * 16)
                            nc.vector.tensor_copy(y[h][:, :, :].rearrange("p (a b) d -> p a b d", a=2),
                                                  k.ps[h][0:CAP, 0:2, :].rearrange("p a (b d) -> p a b d", b=2))\
                                .then_inc(y_kept[h], 1)

        NG = 2
        back = [sb(f"back{i}", [P, TOPK1, D]) for i in range(NG)]
        with nc.Block() as block:

            @block.gpsimd
            def _(pool):
                for i in range(NG):
                    nc.gpsimd.memset(back[i][:, :, :], 0.0).then_inc(zero_made, 1)
                pool.wait_ge(zero_made, 1 + NG)
                for i in range(NT):
                    if i >= NG:
                        pool.wait_ge(combined, i - NG + 1)
                    for j in range(TOPK1):
                        nc.gpsimd.indirect_dma_start(
                            out=back[i % NG][:, j, :], out_offset=None, in_=yrows,
                            in_offset=bass.IndirectOffsetOnAxis(slot_i[:, i, j:j + 1], axis=0),
                            bounds_check=SLOTS - 1, oob_is_err=False).then_inc(gathered[i % NG], 16)

            @block.vector
            def _(dve):
                ch = Chain(dve, add_chain, 0)
                for i in range(NT):
                    dve.wait_ge(gathered[i % NG], 16 * TOPK1 * (i // NG + 1))
                    for j in range(TOPK1):
                        ins_ = nc.vector.scalar_tensor_tensor(k.x[:, i, :], back[i % NG][:, j, :], w[:, i, j:j + 1], k.x[:, i, :],
                                                              ALU.mult, ALU.add)
                        if j < TOPK1 - 1:
                            ch.link(ins_)
                    ins_.then_inc(combined, 1)

            @block.sync
            def _(sp):
                for i in range(NT):
                    sp.wait_ge(combined, i + 1)
                    sp.dma_start(k.out[i // TB, (i % TB) * P:(i % TB + 1) * P, :], k.x[:, i, :]).then_inc(out_stored, 16)
                sp.wait_ge(out_stored, 16 * NT)


class SelfRope:

    def __init__(self, k, stack):
        self.cos = k.sb("rope_cos", [P, TB, HD], F32, stack)
        self.sin = k.sb("rope_sin", [P, TB, HD], F32, stack)
        loaded = k.sem("rope_loaded")
        with k.nc.Block() as block:

            @block.sync
            def _(sp):
                for t, name in ((self.cos, "c_cos"), (self.sin, "c_sin")):
                    sp.dma_start(t[:, :, :], k.ins[name].rearrange("(t p) d -> p t d", p=P)).then_inc(loaded, 16)
                sp.wait_ge(loaded, 32)

    def q(self, p, h):
        return self.cos[:, :, :], self.sin[:, :, :]

    def k(self, p, h):
        return self.cos[:, :, :], self.sin[:, :, :]


def build(nc, ins, out):
    with ExitStack() as stack:
        k = Core(nc, ins, out, stack)
        load_constants(k)
        layernorm(k)
        with ExitStack() as st, k.own_semaphores("_0"):
            attention(k, ("w0q", "w0kv", "w0o"), SelfRope(k, st), None)
        layernorm(k)
        with k.own_semaphores(""):
            set_attention(k)
        layernorm(k)
        with k.own_semaphores(""):
            experts(k)
        layernorm(k)
        with k.own_semaphores(""):
            delta_attention(k)
        layernorm(k)
        with ExitStack() as st, k.own_semaphores("_1"):
            rope = CrossRope(k, st)
            attention(k, ("w1xq", "w1xkv", "w1xo"), rope, rope)
        with ExitStack() as st, k.own_semaphores(""):
            k.xn_rows = k.sb("xn_rows", [P, NT, D], F32, st)
            layernorm(k, k.xn_rows)
            sparse_experts(k)


def constants():
    c = {}
    c["c_ident"] = np.eye(P, dtype=np.float32)
    bf = mybir.dt.np(BF16)
    c["c_identb"] = np.eye(P).astype(bf)
    c["c_causb"] = np.triu(np.full((P, P), NEG), 1).astype(bf)
    inv = (np.float32(1.0) / np.float32(10000.0) ** (np.arange(0, HD, 2, dtype=np.float32) / np.float32(HD))).astype(np.float32)
    ang = (np.arange(S, dtype=np.float32)[:, None] * inv[None, :]).astype(np.float32)
    co, si = np.cos(ang), np.sin(ang)
    c["c_cos"] = np.concatenate([co, co], 1).astype(np.float32)
    c["c_sin"] = np.concatenate([-si, si], 1).astype(np.float32)
    c["c_iota"] = np.broadcast_to(np.arange(P, dtype=np.float32), (P, P))
    j, i = np.arange(P)[:, None], np.arange(P)[None, :]
    c["c_inv"] = np.broadcast_to(inv, (P, HALF))
    c["c_onesb"] = np.ones((P, P)).astype(bf)
    c["c_trib"] = (j < i).astype(bf)
    c["c_ones"] = np.ones((P, P), np.float32)
    c["c_tri"] = (j <= i).astype(np.float32)
    c["c_negstrict"] = np.where(i > j, -1.0, 0.0).astype(np.float32)
    c["c_maskadd"] = np.where(i < j, NEG, 0.0).astype(np.float32)
    lv = {n: ((i == j) | ((i // (2 * n) == j // (2 * n)) & (j // n % 2 == 1) & (i // n % 2 == 0))).astype(np.float32)
          for n in (1, 2, 4, 8, 16, 32, 64)}
    c["c_level1T"] = np.ascontiguousarray(lv[1].T)
    c["c_levels"] = np.ascontiguousarray(np.stack([lv[n] for n in (2, 4, 8, 16, 32, 64)], 1))
    return c


def heads_kv(wk, wv):
    return np.stack([wk.reshape(D, KVH, HD), wv.reshape(D, KVH, HD)], 2).reshape(D, -1)


def kernel(**inputs):
    import concourse.bacc as bacc
    from concourse.bass_utils import run_bass_kernel_spmd as run

    a = {n: np.asarray(v) for n, v in inputs.items()}
    arrays = {"x": a["x"]}
    arrays["w0q"] = a["L0_attn_Wq"]
    arrays["w0kv"] = heads_kv(a["L0_attn_Wk"], a["L0_attn_Wv"])
    arrays["w0o"] = a["L0_attn_Wo"]
    arrays["w0xq"] = a["L0_xattn_W_q"].T
    arrays["w0xb"] = a["L0_xattn_b_q"].reshape(DC, P).T
    arrays["w0xd"] = a["L0_xattn_desc_router"].T
    arrays["ctx"] = a["ctx_2048"]
    arrays["sets"] = a["itok_Sx4_0_63"]
    arrays["w0r"] = a["L0_ffn_router_w"].T
    arrays["w0rb"] = a["L0_ffn_expert_bias"]
    arrays["w0gu"] = np.concatenate([a["L0_ffn_gate_proj"], a["L0_ffn_up_proj"]], 2)
    arrays["w0d"] = a["L0_ffn_down_proj"]
    by_head = lambda m, w: np.moveaxis(m.reshape(m.shape[0], HK, w), 1, 0)
    arrays["w1kqv"] = np.concatenate([by_head(a["L1_attn_Wk"], P), by_head(a["L1_attn_Wq"], P),
                                      by_head(a["L1_attn_Wv"], VE)], 2)
    arrays["w1o"] = a["L1_attn_Wo"].reshape(HK, VE, D)
    arrays["w1ab"] = np.concatenate([a["L1_attn_Wa"], a["L1_attn_Wb"]], 1)
    feats = lambda kf, qf, vf: np.moveaxis(np.concatenate(
        [kf.reshape(HK, 1, P, -1), qf.reshape(HK, 1, P, -1), vf.reshape(HK, 2, P, -1)], 1), 2, 1)
    arrays["w1t"] = np.concatenate([feats(a["L1_attn_kcw"], a["L1_attn_qcw"], a["L1_attn_vcw"]),
                                    feats(a["L1_attn_kcb"], a["L1_attn_qcb"], a["L1_attn_vcb"])], 3)
    arrays["w1xq"] = a["L1_xattn_Wq"].T
    arrays["w1xkv"] = heads_kv(a["L1_xattn_Wk"].T, a["L1_xattn_Wv"].T)
    arrays["w1xo"] = a["L1_xattn_Wo"].T
    arrays["w1xqn"], arrays["w1xkn"] = a["L1_xattn_q_norm_w"], a["L1_xattn_k_norm_w"]
    arrays["ctxT"] = a["ctx_2048"].reshape(B * CTX, D).T
    arrays["pos"] = a["itok_BxS_4096_4607"].reshape(NT, P).T
    arrays["cpos"] = a["pos_BxS2"].T
    arrays["w1r"] = a["L1_ffn_gate_weight"].T
    arrays["w1gu"] = np.moveaxis(a["L1_ffn_gate_up_proj"], 2, 1)
    arrays["w1d"] = np.moveaxis(a["L1_ffn_down_proj"], 2, 1)
    arrays["o2n"] = a["L1_ffn_old_to_new"]
    arrays.update(constants())
    nc = bacc.Bacc("TRN2", target_bir_lowering=False, num_devices=1)
    ins = {}
    for n, v in arrays.items():
        arrays[n] = np.ascontiguousarray(v)
        ins[n] = nc.dram_tensor(f"in_{n}", v.shape, mybir.dt.from_np(v.dtype), kind="ExternalInput").ap()
    out = nc.dram_tensor("out_dram", (B, S, D), F32, kind="ExternalOutput").ap()
    build(nc, ins, out)
    r = run(nc, [{f"in_{n}": v for n, v in arrays.items()}], core_ids=[0])
    return r.results[0]["out_dram"]
```

```python
from contextlib import ExitStack, contextmanager

import numpy as np

import concourse.bass as bass
from concourse import mybir

F32 = mybir.dt.float32
BF16 = mybir.dt.bfloat16
I32 = mybir.dt.int32
U32 = mybir.dt.uint32
ALU = mybir.AluOpType
ACT = mybir.ActivationFunctionType
AX_X = mybir.AxisListType.X
ds = bass.ds

P = 128
B, S, D = 8, 256, 256
T = B * S
NT = T // P
DC = D // P
TB = S // P
NEG = -1.0e30
LN_EPS = 1e-5
LN_TILES = 4
CTX = 64
HD = 128
H, KVH = 16, 4
G = H // KVH
HALF = HD // 2


class Chain:

    def __init__(self, eng, sem, first):
        self.eng, self.sem, self.first, self.count = eng, sem, first, 0

    def link(self, ins):
        self.count += 1
        ins.then_inc(self.sem, 1)
        self.eng.wait_ge(self.sem, self.first + self.count)


class Core:

    def __init__(self, nc, ins, out, stack):
        self.nc, self.ins, self.out, self.stack = nc, ins, out, stack
        self.ln_calls = 0
        self.attn_calls = 0
        self.phase, self.suffix = None, ""

    def sb(self, name, shape, dt=F32, stack=None):
        return (stack or self.stack).enter_context(self.nc.sbuf_tensor(name, shape, dt))

    def sem(self, name):
        handle = (self.phase or self.stack).enter_context(self.nc.semaphore(name + self.suffix))
        if self.phase:
            self.phase_sems.append(handle)
        return handle

    def sems(self, name):
        return [self.sem(f"{name}{h}") for h in range(2)]

    @contextmanager
    def own_semaphores(self, suffix):
        self.phase, self.phase_sems, self.suffix = ExitStack(), [], suffix
        with self.phase:
            yield
            numbers = sorted(s.num for s in self.phase_sems)
            runs = []
            for n in numbers:
                if runs and runs[-1][-1] == n - 1:
                    runs[-1].append(n)
                else:
                    runs.append([n])
            with self.nc.Block() as block:

                @block.gpsimd
                def _(pool):
                    for r in runs:
                        pool.sem_clear(range(r[0], r[-1] + 1))
        self.phase, self.suffix = None, ""


def load_constants(k):
    nc, ins = k.nc, k.ins
    k.x = k.sb("x", [P, NT, D])
    k.xnT = k.sb("xnT", [P, DC, T])
    k.ident = k.sb("ident", [P, P])
    k.identb = k.sb("identb", [P, P], BF16)
    k.causb = k.sb("causb", [P, P], BF16)
    k.mhalf = k.sb("mhalf", [P, 16])
    k.ps = [k.stack.enter_context(nc.psum_tensor(f"ps{h}", [P, 4, 512], F32)) for h in range(2)]
    k.ln_stats = k.sb("ln_stats", [P, LN_TILES, 6])
    k.ln_mv = k.sb("ln_mv", [P, LN_TILES, 2])
    k.ln_ve = k.sb("ln_ve", [P, LN_TILES])
    k.ln_rstd = k.sb("ln_rstd", [P, LN_TILES])
    k.ln_xn = [k.sb(f"ln_xn{q}", [P, D]) for q in range(LN_TILES)]
    k.ln_chain = k.sem("ln_chain")
    k.ln_var = k.sem("ln_var")
    k.ln_pow = k.sem("ln_pow")
    k.ln_normed = k.sem("ln_normed")
    k.ln_turned = k.sem("ln_turned")
    k.ln_stored = k.sem("ln_stored")
    loaded = k.sem("const_loaded")
    made = k.sem("const_made")
    with nc.Block() as block:

        @block.sync
        def _(sp):
            for b in range(B):
                sp.dma_start(k.x[:, TB * b:TB * b + TB, :],
                             ins["x"][b].rearrange("(t p) d -> p t d", p=P)).then_inc(loaded, 16)
            sp.dma_start(k.ident[:, :], ins["c_ident"]).then_inc(loaded, 16)
            sp.dma_start(k.identb[:, :], ins["c_identb"]).then_inc(loaded, 16)
            sp.dma_start(k.causb[:, :], ins["c_causb"]).then_inc(loaded, 16)
            sp.wait_ge(loaded, 16 * (B + 3))

        @block.gpsimd
        def _(pool):
            nc.gpsimd.memset(k.mhalf[:, :], -0.5).then_inc(made, 1)
            pool.wait_ge(made, 1)


def layernorm(k, rows=None):
    nc = k.nc
    Q = LN_TILES
    turns = NT // Q

    def xn(i, q):
        return k.ln_xn[q][:, :] if rows is None else rows[:, i * Q + q, :]

    base = k.ln_calls * turns
    k.ln_calls += 1
    first = base == 0
    with nc.Block() as block:

        @block.vector
        def _(dve):
            for i in range(turns):
                for q in range(Q):
                    nc.vector.bn_stats(k.ln_stats[:, q, :], k.x[:, i * Q + q, :]).then_inc(k.ln_chain, 1)
                dve.wait_ge(k.ln_chain, (i + base) * (2 * Q) + Q)
                for q in range(Q):
                    nc.vector.bn_aggr(k.ln_mv[:, q, :], k.ln_stats[:, q, :]).then_inc(k.ln_chain, 1)
                dve.wait_ge(k.ln_chain, (i + base) * (2 * Q) + 2 * Q)
                nc.vector.tensor_scalar(k.ln_ve[:, :], k.ln_mv[:, :, 1], LN_EPS, None, ALU.add).then_inc(k.ln_var, 1)
                dve.wait_ge(k.ln_turned, i + base + 1)
                dve.wait_ge(k.ln_pow, i + base + 1)
                for q in range(Q):
                    last = nc.vector.tensor_scalar(xn(i, q), k.x[:, i * Q + q, :],
                                                   k.ln_mv[:, q, 0:1], k.ln_rstd[:, q:q + 1],
                                                   ALU.subtract, ALU.mult)
                last.then_inc(k.ln_normed, 1)

        @block.gpsimd
        def _(pool):
            for i in range(turns):
                pool.wait_ge(k.ln_var, i + base + 1)
                nc.gpsimd.tensor_tensor(k.ln_rstd[:, :], k.ln_ve[:, :], k.mhalf[:, 0:Q], ALU.pow).then_inc(k.ln_pow, 1)

        @block.tensor
        def _(pe):
            if first:
                pe.sem_inc(k.ln_turned, 1)
            for i in range(turns):
                pe.wait_ge(k.ln_normed, i + base + 1)
                pe.wait_ge(k.ln_stored, i + base + 1)
                for q in range(Q):
                    for c in range(DC):
                        last = nc.tensor.transpose(k.ps[0][:, c, q * P:(q + 1) * P],
                                                   xn(i, q)[:, c * P:(c + 1) * P], k.ident[:, :])
                last.then_inc(k.ln_turned, 1)

        @block.scalar
        def _(act):
            if first:
                act.sem_inc(k.ln_stored, 1)
            for i in range(turns):
                act.wait_ge(k.ln_turned, i + base + 2)
                nc.scalar.copy(k.xnT[:, :, i * Q * P:(i + 1) * Q * P], k.ps[0][:, 0:DC, :]).then_inc(k.ln_stored, 1)


class AttentionSemaphores:

    def __init__(self, k):
        self.xb_ready = k.sems("xb_ready")
        self.projected = k.sems("projected")
        self.v_kept = k.sems("v_kept")
        self.projected_sq = k.sems("projected_sq")
        self.rotated = k.sems("rotated")
        self.summed = k.sems("summed")
        self.sq_done = k.sems("sq_done")
        self.rms_ready = k.sems("rms_ready")
        self.turned_in = k.sems("turned_in")
        self.qk_turned = k.sems("qk_turned")
        self.qk_kept = k.sems("qk_kept")
        self.scored = k.sems("scored")
        self.max_ready = k.sems("max_ready")
        self.exp_done = k.sems("exp_done")
        self.probs_ready = k.sems("probs_ready")
        self.probs_turned = k.sems("probs_turned")
        self.probs_kept_a = k.sems("probs_kept_a")
        self.probs_kept_d = k.sems("probs_kept_d")
        self.mixed = k.sems("mixed")
        self.mix_kept = k.sems("mix_kept")
        self.out_ready = k.sems("out_ready")
        self.out_added = k.sems("out_added")


def attention(k, weights, rope, ctx):
    nc, ins = k.nc, k.ins
    cross = ctx is not None
    scale = float(HD) ** -0.5
    KT = TB + 1 if cross else TB
    NK = S + (CTX if cross else 0)
    krows = [P] * TB + [CTX]
    s = AttentionSemaphores(k)
    chains, loaded = k.sems("at_chain"), k.sem("at_loaded")
    with ExitStack() as st:
        def sb(name, shape, dt=F32):
            return k.sb(f"at{k.attn_calls}_{name}", shape, dt, st)

        wq = sb("wq", [P, DC, H * HD])
        wkv = sb("wkv", [P, DC, KVH * 2 * HD])
        wo = sb("wo", [P, H, D])
        xb = [sb(f"xb{h}", [P, DC, NK]) for h in range(2)]
        t1 = [sb(f"t1{h}", [P, KT, G + 1, HD]) for h in range(2)]
        t2 = [sb(f"t2{h}", [P, KT, G + 1, HD]) for h in range(2)]
        qT = [sb(f"qT{h}", [P, G, S]) for h in range(2)]
        kT = [sb(f"kT{h}", [P, NK]) for h in range(2)]
        v = [sb(f"v{h}", [P, KT, HD]) for h in range(2)]
        mx = [sb(f"mx{h}", [P, 4]) for h in range(2)]
        nb = [sb(f"nb{h}", [P, 4]) for h in range(2)]
        den = [sb(f"den{h}", [P, 4]) for h in range(2)]
        rden = [sb(f"rden{h}", [P, 4]) for h in range(2)]
        probs = [sb(f"probs{h}", [P, 4, NK]) for h in range(2)]
        shared = [sb(f"shared{h}", [P, max(2 * KT * S, KT * (G + 1) * HD)]) for h in range(2)]
        pT = [b[:, 0:2 * KT * S].rearrange("p (m s) -> p m s", s=S) for b in shared]
        sqs = [b[:, 0:KT * (G + 1) * HD].rearrange("p (t g d) -> p t g d", t=KT, g=G + 1) for b in shared]
        oT = [sb(f"oT{h}", [P, G, S]) for h in range(2)]
        if cross:
            ss = [sb(f"ss{h}", [P, KT, G + 1]) for h in range(2)]
            rs = [sb(f"rs{h}", [P, KT, G + 1]) for h in range(2)]
            esc = [sb(f"esc{h}", [P, TB, G]) for h in range(2)]
        loads = 3

        def q_ps(h):
            return k.ps[h][:, 0:TB, :].rearrange("p t (g d) -> p t g d", g=G)

        def kv_ps(h, part):
            return k.ps[h][:, 2, :].rearrange("p (t s d) -> p t s d", t=TB, s=2)[:, :, part, :]

        def ckv_ps(h, part):
            return k.ps[h][0:CTX, 3, part * HD:(part + 1) * HD]

        def slot(h, m):
            return k.ps[h][:, m // 2, (m % 2) * S:(m % 2) * S + S]

        with nc.Block() as block:

            @block.sync
            def _(sp):
                sp.dma_start(wq[:, :, :], ins[weights[0]].rearrange("(c p) n -> p c n", p=P)).then_inc(loaded, 16)
                sp.dma_start(wkv[:, :, :], ins[weights[1]].rearrange("(c p) n -> p c n", p=P)).then_inc(loaded, 16)
                sp.dma_start(wo[:, :, :], ins[weights[2]].rearrange("(h p) n -> p h n", p=P)).then_inc(loaded, 16)

            @block.gpsimd
            def _(pool):
                with pool.Fori(0, KVH) as g:
                    with pool.Fori(0, B // 2) as p:
                        n = g * (B // 2) + p + 1
                        for h in range(2):
                            pool.wait_ge(s.projected[h], n)
                            xc = nc.gpsimd.tensor_copy(xb[h][:, :, 0:S], k.xnT[:, :, ds(p * (2 * S) + h * S, S)])
                            if cross:
                                xc = nc.gpsimd.tensor_copy(xb[h][:, :, S:NK], ctx.ctxT[:, :, ds(p * (2 * CTX) + h * CTX, CTX)])
                            xc.then_inc(s.xb_ready[h], 1)
                        for h in range(2):
                            pool.wait_ge(s.rotated[h], n)
                            ad = nc.gpsimd.tensor_tensor(t1[h][:, 0:TB], t1[h][:, 0:TB], t2[h][:, 0:TB], ALU.add)
                            if cross:
                                ad = nc.gpsimd.tensor_tensor(t1[h][0:CTX, TB, G, :], t1[h][0:CTX, TB, G, :],
                                                             t2[h][0:CTX, TB, G, :], ALU.add)
                            ad.then_inc(s.summed[h], 1)
                            if cross:
                                pool.wait_ge(s.sq_done[h], n)
                                nc.gpsimd.tensor_tensor(rs[h][:, 0:TB, :], ss[h][:, 0:TB, :],
                                                        k.mhalf[:, 0:TB * (G + 1)].rearrange("p (t g) -> p t g", t=TB),
                                                        ALU.pow)
                                nc.gpsimd.tensor_tensor(rs[h][0:CTX, TB, G:G + 1], ss[h][0:CTX, TB, G:G + 1],
                                                        k.mhalf[0:CTX, 0:1], ALU.pow).then_inc(s.rms_ready[h], 1)

            @block.tensor
            def _(pe):
                pe.wait_ge(loaded, 16 * loads)
                for h in range(2):
                    pe.sem_inc(s.projected[h], 1)
                    pe.sem_inc(s.mixed[h], 1)
                with pe.Fori(0, KVH) as g:
                    with pe.Fori(0, B // 2) as p:
                        n = g * (B // 2) + p + 1

                        def project(h):
                            pe.wait_ge(s.xb_ready[h], n)
                            pe.wait_ge(s.out_added[h], n)
                            for t in range(TB):
                                for c in range(DC):
                                    nc.tensor.matmul(k.ps[h][:, t, :], xb[h][:, c, t * P:(t + 1) * P],
                                                     wq[:, c, ds(g * (G * HD), G * HD)], start=c == 0, stop=c == DC - 1)
                            for t in range(KT):
                                o = k.ps[h][0:krows[t], 2 + t // 2, (t % 2) * 2 * HD:(t % 2 + 1) * 2 * HD]
                                for c in range(DC):
                                    last = nc.tensor.matmul(o, xb[h][:, c, t * P:t * P + krows[t]],
                                                            wkv[:, c, ds(g * (2 * HD), 2 * HD)],
                                                            start=c == 0, stop=c == DC - 1)
                            last.then_inc(s.projected[h], 1)

                        def turn_qk(h):
                            pe.wait_ge(s.turned_in[h] if cross else s.summed[h], n)
                            pe.wait_ge(s.v_kept[h], n)
                            for hh in range(G):
                                for t in range(TB):
                                    nc.tensor.transpose(slot(h, hh)[:, t * P:(t + 1) * P], t1[h][:, t, hh, :], k.ident[:, :])
                            for t in range(KT):
                                r = krows[t]
                                last = nc.tensor.transpose(k.ps[h][:, 2, t * P:t * P + r], t1[h][0:r, t, G, :],
                                                           k.ident[0:r, 0:r])
                            last.then_inc(s.qk_turned[h], 1)

                        def score(h, r):
                            if r == 0:
                                pe.wait_ge(s.qk_kept[h], n)
                            else:
                                pe.wait_ge(s.mix_kept[h], 2 * n - 1)
                            for hh in range(2):
                                for t in range(TB):
                                    nk = NK if cross else (t + 1) * P
                                    last = nc.tensor.matmul(k.ps[h][:, hh * TB + t, 0:nk],
                                                            qT[h][:, 2 * r + hh, t * P:(t + 1) * P],
                                                            kT[h][:, 0:nk], start=True, stop=cross)
                                    if not cross:
                                        last = nc.tensor.matmul(k.ps[h][:, hh * TB + t, t * P:nk], k.identb[:, :],
                                                                k.causb[:, :], start=False, stop=True)
                            last.then_inc(s.scored[h], 1)

                        def turn_probs(h, r):
                            pe.wait_ge(s.probs_ready[h], 2 * n - 1 + r)
                            for hh in range(2):
                                for j in range(KT):
                                    w = krows[j]
                                    for t in range(TB):
                                        if cross or j <= t:
                                            last = nc.tensor.transpose(slot(h, hh * KT + j)[0:w, t * P:(t + 1) * P],
                                                                       probs[h][:, hh * TB + t, j * P:j * P + w], k.ident[:, :])
                            last.then_inc(s.probs_turned[h], 1)

                        def mix(h, r):
                            pe.wait_ge(s.probs_kept_a[h], 2 * n - 1 + r)
                            pe.wait_ge(s.probs_kept_d[h], 2 * n - 1 + r)
                            for hh in range(2):
                                for j in range(KT):
                                    w = krows[j]
                                    c0 = 0 if cross else j * P
                                    last = nc.tensor.matmul(k.ps[h][:, 3, hh * S + c0:(hh + 1) * S], v[h][0:w, j, :],
                                                            pT[h][0:w, hh * KT + j, c0:S], start=j == 0, stop=j == KT - 1)
                            last.then_inc(s.mixed[h], 1)

                        def give(h):
                            pe.wait_ge(s.mix_kept[h], 2 * n)
                            for t in range(TB):
                                for hh in range(G):
                                    last = nc.tensor.matmul(slot(h, t), oT[h][:, hh, t * P:(t + 1) * P],
                                                            wo[:, ds(g * G + hh, 1), :], start=hh == 0, stop=hh == G - 1)
                            last.then_inc(s.out_ready[h], 1)

                        for h in range(2):
                            project(h)
                        for h in range(2):
                            turn_qk(h)
                        for r in range(2):
                            for h in range(2):
                                score(h, r)
                            for h in range(2):
                                turn_probs(h, r)
                            for h in range(2):
                                mix(h, r)
                        for h in range(2):
                            give(h)

            @block.vector
            def _(dve):
                for h in range(2):
                    dve.sem_inc(s.out_added[h], 1)
                LINKS = 5 if cross else 4
                with dve.Fori(0, KVH) as g:
                    with dve.Fori(0, B // 2) as p:
                        n = g * (B // 2) + p + 1
                        chain = [Chain(dve, chains[h], (n - 1) * LINKS) for h in range(2)]

                        def rotate(h):
                            dve.wait_ge(s.projected[h], n + 1)
                            cq, sq = rope.q(p, h)
                            ck, sk = rope.k(p, h)
                            q, kk = q_ps(h), kv_ps(h, 0)

                            def each(o1, o2, x, c, sn):
                                nc.vector.tensor_tensor(o1, x, c, ALU.mult)
                                nc.vector.tensor_tensor(o2[..., 0:HALF], x[..., HALF:HD], sn[..., 0:HALF], ALU.mult)
                                return nc.vector.tensor_tensor(o2[..., HALF:HD], x[..., 0:HALF], sn[..., HALF:HD], ALU.mult)

                            for t in range(TB):
                                each(t1[h][:, t, 0:G, :], t2[h][:, t, 0:G, :], q[:, t],
                                     cq[:, t:t + 1, :].to_broadcast([P, G, HD]), sq[:, t:t + 1, :].to_broadcast([P, G, HD]))
                            last = each(t1[h][:, 0:TB, G, :], t2[h][:, 0:TB, G, :], kk, ck, sk)
                            if cross:
                                cc, sc = rope.c(p, h)
                                last = each(t1[h][0:CTX, TB, G, :], t2[h][0:CTX, TB, G, :], ckv_ps(h, 0), cc, sc)
                            last.then_inc(s.rotated[h], 1)

                        def rms(h):
                            dve.wait_ge(s.projected_sq[h], n)
                            sq = sqs[h]
                            nc.vector.tensor_reduce(ss[h][:, 0:TB, :], sq[:, 0:TB], AX_X, ALU.add)
                            chain[h].link(nc.vector.tensor_reduce(ss[h][0:CTX, TB, G:G + 1], sq[0:CTX, TB, G:G + 1, :], AX_X, ALU.add))
                            nc.vector.tensor_scalar(ss[h][:, 0:TB, :], ss[h][:, 0:TB, :], 1.0 / HD, 1e-6, ALU.mult, ALU.add)
                            nc.vector.tensor_scalar(ss[h][0:CTX, TB, G:G + 1], ss[h][0:CTX, TB, G:G + 1], 1.0 / HD, 1e-6,
                                                    ALU.mult, ALU.add).then_inc(s.sq_done[h], 1)

                        def rms_keys(h):
                            dve.wait_ge(s.rms_ready[h], n)
                            nc.vector.tensor_scalar(esc[h][:, :, :], rs[h][:, 0:TB, 0:G], scale, None, ALU.mult)
                            dve.wait_ge(s.summed[h], n)
                            for t in range(KT):
                                r = krows[t]
                                last = nc.vector.tensor_scalar(t1[h][0:r, t, G, :], t1[h][0:r, t, G, :],
                                                               rs[h][0:r, t, G:G + 1], None, ALU.mult)
                            last.then_inc(s.turned_in[h], 1)

                        def row_max(h, r):
                            dve.wait_ge(s.scored[h], 2 * n - 1 + r)
                            if cross:
                                chain[h].link(nc.vector.tensor_reduce(mx[h][:, :], k.ps[h][:, :, 0:NK], AX_X, ALU.max))
                                nc.vector.scalar_tensor_tensor(nb[h][:, :].rearrange("p (g t) -> p g t", g=2),
                                                               mx[h][:, :].rearrange("p (g t) -> p g t", g=2), -1.0,
                                                               esc[h][:, :, 2 * r:2 * r + 2].rearrange("p t g -> p g t"),
                                                               ALU.mult, ALU.mult).then_inc(s.max_ready[h], 1)
                            else:
                                for t in range(TB):
                                    last = nc.vector.tensor_reduce(mx[h][:, :].rearrange("p (g t) -> p g t", g=2)[:, :, t],
                                                                   k.ps[h][:, t:4:TB, 0:(t + 1) * P], AX_X, ALU.max)
                                chain[h].link(last)
                                nc.vector.tensor_scalar(nb[h][:, :], mx[h][:, :], -scale, None, ALU.mult).then_inc(s.max_ready[h], 1)

                        def norm_probs(h, r):
                            dve.wait_ge(s.exp_done[h], 2 * n - 1 + r)
                            chain[h].link(nc.vector.reciprocal(rden[h][:, :], den[h][:, :]))
                            for m in range(4):
                                nk = NK if cross else (m % TB + 1) * P
                                last = nc.vector.tensor_scalar(probs[h][:, m, 0:nk], probs[h][:, m, 0:nk],
                                                               rden[h][:, m:m + 1], None, ALU.mult)
                            last.then_inc(s.probs_ready[h], 1)

                        def keep_probs(h, r):
                            dve.wait_ge(s.probs_turned[h], 2 * n - 1 + r)
                            dve.wait_ge(s.mixed[h], 2 * n - 1 + r)
                            if cross:
                                nc.vector.tensor_copy(pT[h][0:CTX, 2, :], slot(h, 2)[0:CTX, :])
                                last = nc.vector.tensor_copy(pT[h][:, 3, :], slot(h, 3))
                            else:
                                nc.vector.tensor_copy(pT[h][:, 2, :], slot(h, 2))
                                last = nc.vector.tensor_copy(pT[h][:, 3, P:S], slot(h, 3)[:, P:S])
                            last.then_inc(s.probs_kept_d[h], 1)

                        def add_out(h):
                            dve.wait_ge(s.out_ready[h], n)
                            xt = k.x[:, ds(p * (2 * TB) + h * TB, TB), :]
                            nc.vector.tensor_tensor(xt, xt, k.ps[h][:, 0, :].rearrange("p (t d) -> p t d", t=TB),
                                                    ALU.add).then_inc(s.out_added[h], 1)

                        for h in range(2):
                            rotate(h)
                        if cross:
                            for h in range(2):
                                rms(h)
                            for h in range(2):
                                rms_keys(h)
                        for r in range(2):
                            for h in range(2):
                                row_max(h, r)
                            for h in range(2):
                                norm_probs(h, r)
                            for h in range(2):
                                keep_probs(h, r)
                        for h in range(2):
                            add_out(h)
                        assert chain[0].count == LINKS

            @block.scalar
            def _(act):
                with act.Fori(0, KVH) as g:
                    with act.Fori(0, B // 2) as p:
                        n = g * (B // 2) + p + 1

                        def keep_v(h):
                            act.wait_ge(s.rotated[h], n)
                            if cross:
                                nc.scalar.activation(sqs[h][:, 0:TB, 0:G, :], q_ps(h), ACT.Square)
                                nc.scalar.activation(sqs[h][:, 0:TB, G, :], kv_ps(h, 0), ACT.Square)
                                nc.scalar.activation(sqs[h][0:CTX, TB, G, :], ckv_ps(h, 0), ACT.Square)\
                                    .then_inc(s.projected_sq[h], 1)
                                nc.scalar.copy(v[h][0:CTX, TB, :], ckv_ps(h, 1))
                            nc.scalar.copy(v[h][:, 0:TB, :], kv_ps(h, 1)).then_inc(s.v_kept[h], 1)

                        def keep_qk(h):
                            act.wait_ge(s.qk_turned[h], n)
                            nc.scalar.copy(qT[h][:, :, :], k.ps[h][:, 0:2, :].rearrange("p a (b s) -> p (a b) s", b=2))
                            nc.scalar.copy(kT[h][:, :], k.ps[h][:, 2, 0:NK]).then_inc(s.qk_kept[h], 1)

                        def exps(h, r):
                            act.wait_ge(s.max_ready[h], 2 * n - 1 + r)
                            for m in range(4):
                                nk = NK if cross else (m % TB + 1) * P
                                sc = esc[h][:, m % TB, 2 * r + m // TB:2 * r + m // TB + 1] if cross else scale
                                last = nc.scalar.activation(probs[h][:, m, 0:nk], k.ps[h][:, m, 0:nk], ACT.Exp,
                                                            bias=nb[h][:, m:m + 1], scale=sc, accum_out=den[h][:, m:m + 1])
                            last.then_inc(s.exp_done[h], 1)

                        def keep_probs(h, r):
                            act.wait_ge(s.probs_turned[h], 2 * n - 1 + r)
                            act.wait_ge(s.mixed[h], 2 * n - 1 + r)
                            if cross:
                                nc.scalar.copy(pT[h][:, 0:2, :], k.ps[h][:, 0, :].rearrange("p (a s) -> p a s", a=2))
                                nc.scalar.copy(pT[h][:, 4, :], slot(h, 4))
                                last = nc.scalar.copy(pT[h][0:CTX, 5, :], slot(h, 5)[0:CTX, :])
                            else:
                                nc.scalar.copy(pT[h][:, 0, :], slot(h, 0))
                                last = nc.scalar.copy(pT[h][:, 1, P:S], slot(h, 1)[:, P:S])
                            last.then_inc(s.probs_kept_a[h], 1)

                        def keep_mix(h, r):
                            act.wait_ge(s.mixed[h], 2 * n + r)
                            nc.scalar.copy(oT[h][:, 2 * r:2 * r + 2, :], k.ps[h][:, 3, :].rearrange("p (a s) -> p a s", a=2))\
                                .then_inc(s.mix_kept[h], 1)

                        for h in range(2):
                            keep_v(h)
                        for h in range(2):
                            keep_qk(h)
                        for r in range(2):
                            for h in range(2):
                                exps(h, r)
                            for h in range(2):
                                keep_probs(h, r)
                            for h in range(2):
                                keep_mix(h, r)

    k.attn_calls += 1


TOPK_SETS = 2
E0, TOPK0, I0 = 16, 4, 224
IC = I0 // 2


def set_attention(k):
    nc, ins = k.nc, k.ins
    scale = float(D) ** -0.5
    turns = B // 2
    loaded, chain = k.sem("set_loaded"), k.sem("set_chain")
    q_ready, q_kept = k.sems("set_q_ready"), k.sems("set_q_kept")
    scored, gap_ready, gap_exp = k.sems("set_scored"), k.sems("set_gap_ready"), k.sems("set_gap_exp")
    w_ready, w_turned, w_kept = k.sems("set_w_ready"), k.sems("set_w_turned"), k.sems("set_w_kept")
    mixed, added = k.sems("set_mixed"), k.sems("set_added")
    with ExitStack() as st:
        def sb(name, shape, dt=F32):
            return k.sb(f"set_{name}", shape, dt, st)

        wq, bq, desc = sb("wq", [P, DC, D]), sb("bq", [P, DC]), sb("desc", [P, DC, CTX])
        rows = sb("rows", [CTX, B, D])
        iota = sb("iota", [P, CTX])
        tok_i, tok = sb("tok_i", [P, TB, 4], I32), sb("tok", [P, TB, 4])
        mask = sb("mask", [P, TB, CTX])
        qT = [sb(f"qT{h}", [P, DC, S]) for h in range(2)]
        sc = [sb(f"sc{h}", [P, TB, CTX]) for h in range(2)]
        best = [sb(f"best{h}", [P, TB, 8]) for h in range(2)]
        at = [sb(f"at{h}", [P, TB, 8], U32) for h in range(2)]
        atf = [sb(f"atf{h}", [P, TB, 8]) for h in range(2)]
        gap = [sb(f"gap{h}", [P, TB]) for h in range(2)]
        w2 = [sb(f"w2{h}", [P, TB]) for h in range(2)]
        w1 = [sb(f"w1{h}", [P, TB]) for h in range(2)]
        wa = [sb(f"wa{h}", [P, TB, CTX]) for h in range(2)]
        wb = [sb(f"wb{h}", [P, TB, CTX]) for h in range(2)]
        wT = [sb(f"wT{h}", [CTX, S]) for h in range(2)]
        with nc.Block() as block:

            @block.sync
            def _(sp):
                sp.dma_start(wq[:, :, :], ins["w0xq"].rearrange("(c p) n -> p c n", p=P)).then_inc(loaded, 16)
                sp.dma_start(bq[:, :], ins["w0xb"]).then_inc(loaded, 16)
                sp.dma_start(desc[:, :, :], ins["w0xd"].rearrange("(c p) n -> p c n", p=P)).then_inc(loaded, 16)
                sp.dma_start(rows[:, :, :], ins["ctx"].rearrange("b n d -> n b d")).then_inc(loaded, 16)
                sp.dma_start(iota[:, :], ins["c_iota"][:, 0:CTX]).then_inc(loaded, 16)
                sp.dma_start(tok_i[:, :, :], ins["sets"].rearrange("(t p) k -> p t k", p=P)).then_inc(loaded, 16)

            @block.tensor
            def _(pe):
                pe.wait_ge(loaded, 96)
                for n in range(1, turns + 1):
                    for h in range(2):
                        b = 2 * (n - 1) + h
                        if n > 1:
                            pe.wait_ge(added[h], n - 1)
                        for e in range(DC):
                            for c in range(DC):
                                last = nc.tensor.matmul(k.ps[h][:, 0, e * S:(e + 1) * S], wq[:, c, e * P:(e + 1) * P],
                                                        k.xnT[:, c, b * S:(b + 1) * S], start=c == 0, stop=c == DC - 1)
                        last.then_inc(q_ready[h], 1)
                    for h in range(2):
                        pe.wait_ge(q_kept[h], n)
                        for t in range(TB):
                            for e in range(DC):
                                last = nc.tensor.matmul(k.ps[h][:, 1, t * CTX:(t + 1) * CTX], qT[h][:, e, t * P:(t + 1) * P],
                                                        desc[:, e, :], start=e == 0, stop=e == DC - 1)
                        last.then_inc(scored[h], 1)
                    for h in range(2):
                        pe.wait_ge(w_ready[h], n)
                        for t in range(TB):
                            last = nc.tensor.transpose(k.ps[h][0:CTX, 2, t * P:(t + 1) * P], wa[h][:, t, :], k.ident[:, :])
                        last.then_inc(w_turned[h], 1)
                    for h in range(2):
                        b = 2 * (n - 1) + h
                        pe.wait_ge(w_kept[h], n)
                        for t in range(TB):
                            last = nc.tensor.matmul(k.ps[h][:, 3, t * D:(t + 1) * D], wT[h][:, t * P:(t + 1) * P],
                                                    rows[:, b, :], start=True, stop=True)
                        last.then_inc(mixed[h], 1)

            @block.scalar
            def _(act):
                for n in range(1, turns + 1):
                    for h in range(2):
                        act.wait_ge(q_ready[h], n)
                        for e in range(DC):
                            last = nc.scalar.activation(qT[h][:, e, :], k.ps[h][:, 0, e * S:(e + 1) * S], ACT.Identity,
                                                        bias=bq[:, e:e + 1], scale=1.0)
                        last.then_inc(q_kept[h], 1)
                    for h in range(2):
                        act.wait_ge(gap_ready[h], n)
                        nc.scalar.activation(w2[h][:, :], gap[h][:, :], ACT.Exp).then_inc(gap_exp[h], 1)
                    for h in range(2):
                        act.wait_ge(w_turned[h], n)
                        nc.scalar.copy(wT[h][:, :], k.ps[h][0:CTX, 2, 0:S]).then_inc(w_kept[h], 1)

            @block.vector
            def _(dve):
                ch = Chain(dve, chain, 0)
                dve.wait_ge(loaded, 96)
                ch.link(nc.vector.tensor_copy(tok[:, :, :], tok_i[:, :, :]))
                for t in range(TB):
                    ch.link(nc.vector.tensor_scalar(mask[:, t, :], iota[:, :], tok[:, t, 0:1], None, ALU.is_equal))
                    for j in range(1, 4):
                        ch.link(nc.vector.scalar_tensor_tensor(mask[:, t, :], iota[:, :], tok[:, t, j:j + 1], mask[:, t, :],
                                                               ALU.is_equal, ALU.add))
                ch.link(nc.vector.tensor_scalar(mask[:, :, :], mask[:, :, :], 0.5, NEG, ALU.is_lt, ALU.mult))
                for n in range(1, turns + 1):
                    for h in range(2):
                        dve.wait_ge(scored[h], n)
                        ch.link(nc.vector.scalar_tensor_tensor(
                            sc[h][:, :, :], k.ps[h][:, 1, 0:TB * CTX].rearrange("p (t n) -> p t n", t=TB), scale,
                            mask[:, :, :], ALU.mult, ALU.add))
                        for t in range(TB):
                            last = nc.vector.max(best[h][:, t, :], sc[h][:, t, :])
                        ch.link(last)
                        for t in range(TB):
                            last = nc.vector.max_index(at[h][:, t, :], best[h][:, t, :], sc[h][:, t, :])
                        ch.link(last)
                        nc.vector.tensor_copy(atf[h][:, :, :], at[h][:, :, :])
                        nc.vector.tensor_tensor(gap[h][:, :], best[h][:, :, 1], best[h][:, :, 0], ALU.subtract)\
                            .then_inc(gap_ready[h], 1)
                    for h in range(2):
                        dve.wait_ge(gap_exp[h], n)
                        ch.link(nc.vector.tensor_scalar(w1[h][:, :], w2[h][:, :], 1.0, None, ALU.add))
                        ch.link(nc.vector.reciprocal(w1[h][:, :], w1[h][:, :]))
                        ch.link(nc.vector.tensor_tensor(w2[h][:, :], w2[h][:, :], w1[h][:, :], ALU.mult))
                        for t in range(TB):
                            nc.vector.tensor_scalar(wa[h][:, t, :], iota[:, :], atf[h][:, t, 0:1], w1[h][:, t:t + 1],
                                                    ALU.is_equal, ALU.mult)
                            last = nc.vector.tensor_scalar(wb[h][:, t, :], iota[:, :], atf[h][:, t, 1:2], w2[h][:, t:t + 1],
                                                           ALU.is_equal, ALU.mult)
                        ch.link(last)
                        nc.vector.tensor_tensor(wa[h][:, :, :], wa[h][:, :, :], wb[h][:, :, :], ALU.add).then_inc(w_ready[h], 1)
                    for h in range(2):
                        b = 2 * (n - 1) + h
                        dve.wait_ge(mixed[h], n)
                        xt = k.x[:, b * TB:(b + 1) * TB, :]
                        nc.vector.tensor_tensor(xt, xt, k.ps[h][:, 3, :].rearrange("p (t d) -> p t d", t=TB),
                                                ALU.add).then_inc(added[h], 1)


def experts(k):
    nc, ins = k.nc, k.ins
    GT = 4
    groups = NT // GT
    loaded, chain = k.sem("moe_loaded"), k.sem("moe_chain")
    routed, shifted, exps_done, w_made = k.sem("moe_routed"), k.sem("moe_shifted"), k.sem("moe_exps"), k.sem("moe_w_made")
    w_loaded = [k.sem(f"moe_w_loaded{q}") for q in range(2)]
    up_ready, silu_done, act_ready = k.sems("moe_up_ready"), k.sems("moe_silu_done"), k.sems("moe_act_ready")
    down_ready, added = k.sems("moe_down_ready"), k.sems("moe_added")
    with ExitStack() as st:
        def sb(name, shape, dt=F32):
            return k.sb(f"moe_{name}", shape, dt, st)

        router, bias, iota = sb("router", [P, DC, E0]), sb("bias", [P, E0]), sb("iota", [P, E0])
        lg = sb("lg", [P, NT, E0])
        best, at, atf = sb("best", [P, NT, 8]), sb("at", [P, NT, 8], U32), sb("atf", [P, NT, 8])
        ex, tot, rtot = sb("ex", [P, NT, TOPK0]), sb("tot", [P, NT]), sb("rtot", [P, NT])
        w = sb("w", [P, NT, E0])
        eq = [sb(f"eq{j}", [P, NT, E0]) for j in range(TOPK0)]
        wgu = [[sb(f"wgu{q}{h}", [P, DC, 2 * I0]) for h in range(2)] for q in range(2)]
        wd = [[sb(f"wd{q}{h}", [IC, 2, D]) for h in range(2)] for q in range(2)]
        sg = [sb(f"sg{h}", [IC, 2, GT * P]) for h in range(2)]
        hT = [sb(f"hT{h}", [IC, 2, GT * P]) for h in range(2)]

        def load_expert(sp, q, h, e):
            sp.dma_start(wgu[q][h][:, :, :], ins["w0gu"][ds(e, 1)].rearrange("e (c p) n -> p (e c) n", p=P))\
                .then_inc(w_loaded[q], 16)
            sp.dma_start(wd[q][h][:, :, :], ins["w0d"][ds(e, 1)].rearrange("e (c p) n -> p (e c) n", p=IC))\
                .then_inc(w_loaded[q], 16)

        with nc.Block() as block:

            @block.sync
            def _(sp):
                sp.dma_start(router[:, :, :], ins["w0r"].rearrange("(c p) n -> p c n", p=P)).then_inc(loaded, 16)
                sp.dma_start(bias[:, :], ins["w0rb"].partition_broadcast(P)).then_inc(loaded, 16)
                sp.dma_start(iota[:, :], ins["c_iota"][:, 0:E0]).then_inc(loaded, 16)
                for q in range(2):
                    for h in range(2):
                        load_expert(sp, q, h, 2 * q + h)
                with sp.Fori(1, E0 // 4) as j:
                    for q in range(2):
                        for h in range(2):
                            sp.wait_ge(added[h], j * (2 * groups) + (q - 1) * groups + 1)
                            load_expert(sp, q, h, j * 4 + (2 * q + h))

            @block.tensor
            def _(pe):
                pe.wait_ge(loaded, 48)
                for i in range(NT):
                    for c in range(DC):
                        last = nc.tensor.matmul(k.ps[0][:, 0, i * E0:(i + 1) * E0], k.xnT[:, c, i * P:(i + 1) * P],
                                                router[:, c, :], start=c == 0, stop=c == DC - 1)
                last.then_inc(routed, 1)
                pe.wait_ge(shifted, 1)
                with pe.Fori(0, E0 // 4) as j:
                    for q in range(2):
                        with pe.Fori(0, groups) as g:
                            n = j * (2 * groups) + g + (q * groups + 1)
                            for h in range(2):
                                pe.wait_ge(w_loaded[q], (j + 1) * 64)
                                pe.wait_ge(added[h], n)
                                for m in range(4):
                                    for c in range(DC):
                                        last = nc.tensor.matmul(k.ps[h][0:IC, m, :], wgu[q][h][:, c, m * IC:(m + 1) * IC],
                                                                k.xnT[:, c, ds(g * (GT * P), GT * P)],
                                                                start=c == 0, stop=c == DC - 1)
                                last.then_inc(up_ready[h], 1)
                            for h in range(2):
                                pe.wait_ge(act_ready[h], n)
                                for t in range(GT):
                                    for c in range(2):
                                        last = nc.tensor.matmul(k.ps[h][:, t // 2, (t % 2) * D:(t % 2 + 1) * D],
                                                                hT[h][:, c, t * P:(t + 1) * P], wd[q][h][:, c, :],
                                                                start=c == 0, stop=c == 1)
                                last.then_inc(down_ready[h], 1)

            @block.scalar
            def _(act):
                act.wait_ge(shifted, 1)
                nc.scalar.activation(ex[:, :, :], ex[:, :, :], ACT.Exp).then_inc(exps_done, 1)
                with act.Fori(0, E0 // 4) as j:
                    for q in range(2):
                        with act.Fori(0, groups) as g:
                            n = j * (2 * groups) + g + (q * groups + 1)
                            for h in range(2):
                                act.wait_ge(up_ready[h], n)
                                nc.scalar.activation(sg[h][:, :, :], k.ps[h][0:IC, 0:2, :], ACT.Silu).then_inc(silu_done[h], 1)

            @block.vector
            def _(dve):
                for h in range(2):
                    dve.sem_inc(added[h], 1)
                ch = Chain(dve, chain, 0)
                dve.wait_ge(routed, 1)
                ch.link(nc.vector.tensor_tensor(lg[:, :, :], k.ps[0][:, 0, 0:NT * E0].rearrange("p (t e) -> p t e", e=E0),
                                                bias[:, :].unsqueeze(1).to_broadcast([P, NT, E0]), ALU.add))
                for i in range(NT):
                    last = nc.vector.max(best[:, i, :], lg[:, i, :])
                ch.link(last)
                for i in range(NT):
                    last = nc.vector.max_index(at[:, i, :], best[:, i, :], lg[:, i, :])
                ch.link(last)
                nc.vector.tensor_tensor(ex[:, :, :], best[:, :, 0:TOPK0],
                                        best[:, :, 0:1].to_broadcast([P, NT, TOPK0]), ALU.subtract).then_inc(shifted, 1)
                ch.link(nc.vector.tensor_copy(atf[:, :, :], at[:, :, :]))
                dve.wait_ge(exps_done, 1)
                ch.link(nc.vector.tensor_reduce(tot[:, :], ex[:, :, :], AX_X, ALU.add))
                ch.link(nc.vector.reciprocal(rtot[:, :], tot[:, :]))
                ch.link(nc.vector.tensor_tensor(ex[:, :, :], ex[:, :, :],
                                                rtot[:, :].unsqueeze(2).to_broadcast([P, NT, TOPK0]), ALU.mult))
                for j in range(TOPK0):
                    last = nc.vector.tensor_tensor(eq[j][:, :, :], iota[:, :].unsqueeze(1).to_broadcast([P, NT, E0]),
                                                   atf[:, :, j:j + 1].to_broadcast([P, NT, E0]), ALU.is_equal)
                ch.link(last)
                for j in range(TOPK0):
                    last = nc.vector.tensor_tensor(eq[j][:, :, :], eq[j][:, :, :],
                                                   ex[:, :, j:j + 1].to_broadcast([P, NT, E0]), ALU.mult)
                ch.link(last)
                nc.vector.tensor_tensor(eq[0][:, :, :], eq[0][:, :, :], eq[1][:, :, :], ALU.add)
                ch.link(nc.vector.tensor_tensor(eq[2][:, :, :], eq[2][:, :, :], eq[3][:, :, :], ALU.add))
                ch.link(nc.vector.tensor_tensor(w[:, :, :], eq[0][:, :, :], eq[2][:, :, :], ALU.add))
                with dve.Fori(0, E0 // 4) as j:
                    for q in range(2):
                        with dve.Fori(0, groups) as g:
                            n = j * (2 * groups) + g + (q * groups + 1)
                            for h in range(2):
                                dve.wait_ge(silu_done[h], n)
                                nc.vector.tensor_tensor(hT[h][:, :, :], sg[h][:, :, :], k.ps[h][0:IC, 2:4, :], ALU.mult)\
                                    .then_inc(act_ready[h], 1)
                            for h in range(2):
                                dve.wait_ge(down_ready[h], n)
                                if h == 1:
                                    dve.wait_ge(added[0], n + 1)
                                for t in range(GT):
                                    xt = k.x[:, ds(g * GT + t, 1), :].rearrange("p a d -> p (a d)")
                                    sc = w[:, ds(g * GT + t, 1), ds(j * 4 + (2 * q + h), 1)].rearrange("p a e -> p (a e)")
                                    last = nc.vector.scalar_tensor_tensor(xt, k.ps[h][:, t // 2, (t % 2) * D:(t % 2 + 1) * D],
                                                                          sc, xt, ALU.mult, ALU.add)
                                last.then_inc(added[h], 1)


HK, VE, KC = 16, 256, 4


def delta_attention(k):
    nc, ins = k.nc, k.ins
    loaded, made = k.sem("dl_loaded"), k.sem("dl_made")
    gates_ready, gates_abs, gates_exp, gates_log = k.sem("dl_gates"), k.sem("dl_gabs"), k.sem("dl_gexp"), k.sem("dl_glog")
    loga_ready, cum_ready, cum_kept, cum_turned = k.sem("dl_loga"), k.sem("dl_cum"), k.sem("dl_cum_kept"), k.sem("dl_cumT")
    rows_kept, rows_stored, chain0 = k.sem("dl_rows_kept"), k.sem("dl_rows_stored"), k.sem("dl_setup_chain")
    w_loaded = k.sems("dl_w_loaded")
    wo_loaded = k.sems("dl_wo_loaded")
    taps_loaded = k.sems("dl_taps_loaded")
    grow_loaded = k.sems("dl_grow_loaded")
    projected = k.sems("dl_projected")
    tapped = k.sems("dl_tapped")
    conv_part = k.sems("dl_conv_part")
    convolved = k.sems("dl_convolved")
    tanh_done = k.sems("dl_tanh_done")
    silu_done = k.sems("dl_silu_done")
    squared = k.sems("dl_squared")
    lengths = k.sems("dl_lengths")
    lengths_kept = k.sems("dl_len_kept")
    inverse_len = k.sems("dl_inv_len")
    c_part = k.sems("dl_c_part")
    scales_ready = k.sems("dl_scales")
    masked = k.sems("dl_masked")
    decayed = k.sems("dl_decayed")
    v_turned = k.sems("dl_v_turned")
    v_scaled = k.sems("dl_v_scaled")
    products = k.sems("dl_products")
    lp_ready = k.sems("dl_lp_ready")
    nt_part = k.sems("dl_nt_part")
    nt_ready = k.sems("dl_nt_ready")
    t_ready = k.sems("dl_t_ready")
    t_kept = k.sems("dl_t_kept")
    tt_ready = k.sems("dl_tt_ready")
    tt_kept = k.sems("dl_tt_kept")
    off_ready = k.sems("dl_off_ready")
    off_kept = k.sems("dl_off_kept")
    solved = k.sems("dl_solved")
    w_kept = k.sems("dl_w_kept")
    rest_kept = k.sems("dl_rest_kept")
    mixed = k.sems("dl_mixed")
    mix_kept = k.sems("dl_mix_kept")
    out_ready = k.sems("dl_out_ready")
    added = k.sems("dl_added")
    levels = [1 << i for i in range(1, 7)]
    NL = len(levels)
    scratch = nc.dram_tensor("decay_rows", (HK, T), F32, kind="Internal").ap()
    with ExitStack() as st:
        def sb(name, shape, dt=F32):
            return k.sb(f"dl_{name}", shape, dt, st)

        wab = sb("wab", [P, DC, 2 * HK])
        taps = [sb(f"taps{h}", [P, 4, KC + 1]) for h in range(2)]
        tri, ones = sb("tri", [P, P]), sb("ones", [P, P])
        negstrict, maskadd = sb("negstrict", [P, P]), sb("maskadd", [P, P])
        lvl, lvl1T = sb("lvl", [P, NL, P]), sb("lvl1T", [P, P])
        za, zabs = sb("za", [P, NT, HK]), sb("zabs", [P, NT, 2 * HK])
        loga, beta = sb("loga", [P, NT, HK]), sb("beta", [P, NT, HK])
        cum, negcum = sb("cum", [P, NT, HK]), sb("negcum", [P, NT, HK])
        rows = sb("rows", [HK, T])
        wkqv = [sb(f"wkqv{h}", [P, DC, 4 * P]) for h in range(2)]
        wo = [sb(f"wo{h}", [P, 2, D]) for h in range(2)]
        grow = [sb(f"grow{h}", [P, T]) for h in range(2)]
        y = [sb(f"y{h}", [P, 4, S]) for h in range(2)]
        e = [sb(f"e{h}", [P, 4, S]) for h in range(2)]
        z = [sb(f"z{h}", [P, 4, S]) for h in range(2)]
        sq = [sb(f"sq{h}", [P, 2, S]) for h in range(2)]
        n2 = [sb(f"n2{h}", [P, 4]) for h in range(2)]
        rn = [sb(f"rn{h}", [P, 4]) for h in range(2)]
        rq = [sb(f"rq{h}", [P, 2, TB]) for h in range(2)]
        nk = [sb(f"nk{h}", [P, TB]) for h in range(2)]
        cj = [sb(f"cj{h}", [P, TB]) for h in range(2)]
        gm = [sb(f"gm{h}", [P, 3 * P]) for h in range(2)]
        ng = [sb(f"ng{h}", [P, TB]) for h in range(2)]
        dec = [sb(f"dec{h}", [P, 3 * P]) for h in range(2)]
        vs = [sb(f"vs{h}", [P, TB, VE]) for h in range(2)]
        lp = [sb(f"lp{h}", [P, 2, 2 * S]) for h in range(2)]
        lp0 = [t[:, 0, :].rearrange("p (a s) -> p a s", a=2) for t in lp]
        lp1 = [t[:, 1, 0:S].rearrange("p (a s) -> p a s", a=2) for t in lp]
        ntm = [sb(f"ntm{h}", [P, 2, P]) for h in range(2)]
        nt = [sb(f"nt{h}", [P, 2, P]) for h in range(2)]
        tt = [sb(f"tt{h}", [P, 2, 2, P]) for h in range(2)]
        off = [sb(f"off{h}", [P, NL, 2, P]) for h in range(2)]
        wv = [sb(f"wv{h}", [P, 2, VE]) for h in range(2)]
        rest = [sb(f"rest{h}", [P, VE]) for h in range(2)]
        oT = [sb(f"oT{h}", [P, 2, S]) for h in range(2)]

        def halves(ap, b, second):
            return ap.rearrange("p (n a b) -> p n a b", a=2, b=b)[:, :, second, :]

        def load_w(sp, h, hd):
            sp.dma_start(wkqv[h][:, :, :], ins["w1kqv"][ds(hd, 1)].rearrange("e (c p) n -> p (e c) n", p=P))\
                .then_inc(w_loaded[h], 16)

        def load_taps(sp, h, hd):
            sp.dma_start(taps[h][:, :, :], ins["w1t"][ds(hd, 1)].rearrange("e p m n -> p (e m) n")).then_inc(taps_loaded[h], 16)

        def load_grow(sp, h, hd):
            sp.dma_start(grow[h][:, :], scratch[ds(hd, 1), :].rearrange("e t -> (e t)").partition_broadcast(P))\
                .then_inc(grow_loaded[h], 16)

        def load_wo(sp, h, hd):
            sp.dma_start(wo[h][:, :, :], ins["w1o"][ds(hd, 1)].rearrange("e (c p) n -> p (e c) n", p=P))\
                .then_inc(wo_loaded[h], 16)

        UNITS = HK // 2 * B

        def batch(u):
            return u % B

        def pair(u):
            return u // B

        def schedule(eng, stage):
            stage(1, None, None, 0, 0)
            stage(0, 0, None, 0, 1)
            stage(1, 0, 0, 1, 1)
            stage(0, 1, 0, 1, 2)
            with eng.Fori(1, UNITS - 2) as i:
                stage(1, i, i, i + 1, i + 1)
                stage(0, i + 1, i, i + 1, i + 2)
            stage(1, UNITS - 2, UNITS - 2, UNITS - 1, UNITS - 1)
            stage(0, UNITS - 1, UNITS - 2, UNITS - 1, None)
            stage(1, UNITS - 1, UNITS - 1, None, None)
            stage(0, None, UNITS - 1, None, None)

        def wait_before(eng, sem, u):
            if not isinstance(u, int) or u > 0:
                eng.wait_ge(sem, u)

        with nc.Block() as block:

            @block.sync
            def _(sp):
                for dst, name in ((tri[:, :], "c_tri"), (ones[:, :], "c_ones"), (negstrict[:, :], "c_negstrict"), (maskadd[:, :], "c_maskadd"),
                                  (lvl[:, :, :], "c_levels"), (lvl1T[:, :], "c_level1T")):
                    sp.dma_start(dst, ins[name]).then_inc(loaded, 16)
                sp.dma_start(wab[:, :, :], ins["w1ab"].rearrange("(c p) n -> p c n", p=P)).then_inc(loaded, 16)
                for h in range(2):
                    load_w(sp, h, h)
                    load_taps(sp, h, h)
                    load_wo(sp, h, h)
                sp.wait_ge(rows_kept, 4)
                sp.dma_start(scratch, rows[:, :]).then_inc(rows_stored, 16)
                sp.wait_ge(rows_stored, 16)
                for h in range(2):
                    load_grow(sp, h, h)
                with sp.Fori(1, HK // 2) as j:
                    for h in range(2):
                        sp.wait_ge(projected[h], j * (2 * B))
                        load_w(sp, h, j * 2 + h)
                        sp.wait_ge(convolved[h], j * (2 * B))
                        load_taps(sp, h, j * 2 + h)
                        sp.wait_ge(masked[h], j * B)
                        load_grow(sp, h, j * 2 + h)
                    for h in range(2):
                        sp.wait_ge(out_ready[h], j * B)
                        load_wo(sp, h, j * 2 + h)

            @block.gpsimd
            def _(pool):
                for h in range(2):
                    for i in range(NL):
                        nc.gpsimd.tensor_copy(off[h][:, i, :, :], k.ident[:, :].unsqueeze(1).to_broadcast([P, 2, P]))
                pool.wait_ge(loaded, 16 * 7)
                pool.wait_ge(cum_kept, 1)

                def mask_decay(h, u):
                    pool.wait_ge(grow_loaded[h], (pair(u) + 1) * 16)
                    wait_before(pool, decayed[h], u)
                    for blk, c0 in ((0, 0), (1, S)):
                        nc.gpsimd.tensor_tensor(gm[h][:, c0:c0 + P], grow[h][:, ds(batch(u) * S + blk * P, P)],
                                                maskadd[:, :], ALU.add)
                    nc.gpsimd.tensor_copy(ng[h][:, :], negcum[:, ds(batch(u) * TB, TB), ds(pair(u) * 2 + h, 1)]
                                          .rearrange("p t a -> p (t a)"))
                    nc.gpsimd.tensor_copy(gm[h][:, P:S], grow[h][:, ds(batch(u) * S + P, P)]).then_inc(masked[h], 1)

                def invert_lengths(h, u):
                    pool.wait_ge(lengths_kept[h], u + 1)
                    nc.gpsimd.tensor_tensor(rn[h][:, :], n2[h][:, :], k.mhalf[:, 0:4], ALU.pow).then_inc(inverse_len[h], 1)

                def stage(h, grown, given, prepared, project):
                    g = 1 - h
                    if prepared is not None:
                        mask_decay(g, prepared)
                        invert_lengths(g, prepared)

                schedule(pool, stage)

            @block.tensor
            def _(pe):
                pe.wait_ge(loaded, 16 * 7)
                for i in range(NT):
                    for c in range(DC):
                        last = nc.tensor.matmul(k.ps[0][:, 0, i * 2 * HK:(i + 1) * 2 * HK], k.xnT[:, c, i * P:(i + 1) * P],
                                                wab[:, c, :], start=c == 0, stop=c == DC - 1)
                last.then_inc(gates_ready, 1)
                pe.wait_ge(loga_ready, 1)
                for i in range(NT):
                    o = k.ps[0][:, 1, i * HK:(i + 1) * HK]
                    last = nc.tensor.matmul(o, tri[:, :], loga[:, i, :], start=True, stop=i % TB == 0)
                    if i % TB:
                        last = nc.tensor.matmul(o, ones[:, :], loga[:, i - 1, :], start=False, stop=True)
                last.then_inc(cum_ready, 1)
                pe.wait_ge(cum_kept, 1)
                for i in range(NT):
                    last = nc.tensor.transpose(k.ps[1][0:HK, i // 4, (i % 4) * P:(i % 4 + 1) * P], cum[:, i, :], k.ident[:, :])
                last.then_inc(cum_turned, 1)

                def project_part(h, u, m):
                    if m == 0:
                        pe.wait_ge(w_loaded[h], (pair(u) + 1) * 16)
                        wait_before(pe, lp_ready[h], u)
                    if m == 2:
                        wait_before(pe, v_scaled[h], u)
                    for c in range(DC):
                        last = nc.tensor.matmul(k.ps[h][:, m // 2, (m % 2) * S:(m % 2 + 1) * S],
                                                wkqv[h][:, c, m * P:(m + 1) * P],
                                                k.xnT[:, c, ds(batch(u) * S, S)],
                                                start=c == 0, stop=c == DC - 1)
                    if m % 2:
                        last.then_inc(projected[h], 1)

                def products_of(h, u):
                    pe.wait_ge(silu_done[h], u * 2 + 1)
                    pe.wait_ge(convolved[h], u * 2 + 2)
                    nc.tensor.matmul(k.ps[h][:, 0, :].rearrange("p (a s) -> p a s", a=2), z[h][:, 0, 0:P],
                                     z[h][:, 0:2, :], start=True, stop=True)
                    nc.tensor.matmul(k.ps[h][:, 1, 0:S].rearrange("p (a s) -> p a s", a=2), z[h][:, 0, P:S],
                                     z[h][:, 0:2, P:S], start=True, stop=True).then_inc(products[h], 1)

                def turn_v(h, u):
                    pe.wait_ge(lp_ready[h], u + 1)
                    pe.wait_ge(silu_done[h], u * 2 + 2)
                    for t in range(TB):
                        for m in range(2):
                            last = nc.tensor.transpose(k.ps[h][:, 1, (2 * t + m) * P:(2 * t + m + 1) * P],
                                                       z[h][:, 2 + m, t * P:(t + 1) * P], k.ident[:, :])
                    last.then_inc(v_turned[h], 1)

                def lengths_of(h, u):
                    pe.wait_ge(squared[h], u + 1)
                    for m in range(2):
                        for t in range(TB):
                            last = nc.tensor.matmul(k.ps[h][:, 1, S + m * TB + t:S + m * TB + t + 1],
                                                    sq[h][:, m, t * P:(t + 1) * P], ones[:, 0:1],
                                                    start=True, stop=True)
                    last.then_inc(lengths[h], 1)

                def turn_first(h, u):
                    pe.wait_ge(nt_ready[h], u + 1)
                    for blk in range(2):
                        last = nc.tensor.transpose(k.ps[h][:, 2, blk * P:(blk + 1) * P], tt[h][:, 1, blk, :],
                                                   k.ident[:, :])
                    last.then_inc(t_ready[h], 1)

                def grow_off(h, u, i):
                    pe.wait_ge(t_kept[h], u * NL + (i + 1))
                    for blk in range(2):
                        last = nc.tensor.matmul(k.ps[h][:, 2, blk * HALF:(blk + 1) * HALF], nt[h][:, blk, :],
                                                halves(tt[h][:, 0, blk, :], levels[i], 0), start=True, stop=True)
                    last.then_inc(off_ready[h], 1)

                def grow_t(h, u, i):
                    pe.wait_ge(off_kept[h], u * NL + (i + 1))
                    if i > 0:
                        pe.wait_ge(tt_kept[h], u * NL + i)
                    else:
                        wait_before(pe, added[h], u)
                    if i < NL - 1:
                        for blk in range(2):
                            last = nc.tensor.matmul(k.ps[h][:, 2, S + blk * HALF:S + (blk + 1) * HALF], tt[h][:, 1, blk, :],
                                                    halves(off[h][:, i, blk, :], levels[i], 0), start=True, stop=True)
                        last.then_inc(t_ready[h], 1)
                    for blk in range(2):
                        last = nc.tensor.matmul(k.ps[h][:, 3, blk * HALF:(blk + 1) * HALF], off[h][:, i, blk, :],
                                                halves(tt[h][:, 1, blk, :], levels[i], 1), start=True, stop=True)
                    last.then_inc(tt_ready[h], 1)

                def solve_first(h, u):
                    pe.wait_ge(tt_kept[h], u * NL + NL)
                    nc.tensor.matmul(k.ps[h][:, 2, 0:VE], tt[h][:, 1, 0, :], vs[h][:, 0, :],
                                     start=True, stop=True).then_inc(solved[h], 1)

                def solve_cross(h, u):
                    pe.wait_ge(w_kept[h], u * 2 + 1)
                    nc.tensor.matmul(k.ps[h][:, 2, VE:2 * VE], lp0[h][:, 0, P:S], wv[h][:, 0, :],
                                     start=True, stop=True).then_inc(solved[h], 1)

                def solve_second(h, u):
                    pe.wait_ge(rest_kept[h], u + 1)
                    nc.tensor.matmul(k.ps[h][:, 3, 0:VE], tt[h][:, 1, 1, :], rest[h][:, :],
                                     start=True, stop=True).then_inc(solved[h], 1)

                def mix(h, u):
                    pe.wait_ge(w_kept[h], u * 2 + 2)
                    for m in range(2):
                        nc.tensor.matmul(k.ps[h][:, 2, m * S:(m + 1) * S], wv[h][:, 0, m * P:(m + 1) * P],
                                         lp0[h][:, 1, :], start=True, stop=False)
                        last = nc.tensor.matmul(k.ps[h][:, 2, m * S + P:(m + 1) * S], wv[h][:, 1, m * P:(m + 1) * P],
                                                lp1[h][:, 1, :], start=False, stop=True)
                    last.then_inc(mixed[h], 1)

                def give(h, u, t):
                    if t == 0:
                        pe.wait_ge(wo_loaded[h], (pair(u) + 1) * 16)
                        pe.wait_ge(mix_kept[h], u + 1)
                    for m in range(2):
                        last = nc.tensor.matmul(k.ps[h][:, 3, t * D:(t + 1) * D], oT[h][:, m, t * P:(t + 1) * P],
                                                wo[h][:, m, :], start=m == 0, stop=m == 1)
                    if t:
                        last.then_inc(out_ready[h], 1)

                def stage(h, grown, given, prepared, project):
                    g = 1 - h

                    if grown is not None:
                        turn_first(h, grown)
                    if given is not None:
                        solve_first(g, given)
                    for i in range(NL):
                        if grown is not None:
                            grow_off(h, grown, i)
                        if project is not None and i < 3:
                            project_part(h, project, (0, 2, 3)[i])
                        if prepared is not None and i == 3:
                            products_of(g, prepared)
                        if given is not None and i == 4:
                            mix(g, given)
                        if given is not None and i == 5:
                            give(g, given, 1)
                        if grown is not None:
                            grow_t(h, grown, i)
                        if given is not None and i < 2:
                            (solve_cross, solve_second)[i](g, given)
                        if given is not None and i == 4:
                            give(g, given, 0)
                        if project is not None and i == 0:
                            project_part(h, project, 1)
                        if prepared is not None and i == 3:
                            lengths_of(g, prepared)
                        if prepared is not None and i == 5:
                            turn_v(g, prepared)

                pe.wait_ge(rows_kept, 4)
                for m in range(4):
                    project_part(0, 0, m)
                schedule(pe, stage)

            @block.scalar
            def _(act):
                act.wait_ge(gates_abs, 1)
                nc.scalar.activation(zabs[:, :, :], zabs[:, :, :], ACT.Exp, scale=-1.0).then_inc(gates_exp, 1)
                act.wait_ge(gates_exp, 1)
                nc.scalar.activation(loga[:, :, :], zabs[:, :, 0:HK], ACT.Ln, bias=1.0, scale=1.0).then_inc(gates_log, 1)
                act.wait_ge(cum_turned, 1)
                for i in range(4):
                    nc.scalar.copy(rows[:, i * 512:(i + 1) * 512], k.ps[1][0:HK, i, :]).then_inc(rows_kept, 1)

                def tap(h, u, part):
                    if part == 0:
                        act.wait_ge(taps_loaded[h], (pair(u) + 1) * 16)
                    act.wait_ge(projected[h], u * 2 + (part + 1))
                    for m in (2 * part, 2 * part + 1):
                        last = nc.scalar.activation(y[h][:, m, :], k.ps[h][:, m // 2, (m % 2) * S:(m % 2 + 1) * S],
                                                    ACT.Identity,
                                                    bias=taps[h][:, m, KC:KC + 1], scale=taps[h][:, m, KC - 1:KC])
                    last.then_inc(tapped[h], 1)

                def tanh_of(h, u, part):
                    act.wait_ge(convolved[h], u * 2 + (part + 1))
                    nc.scalar.activation(e[h][:, 2 * part:2 * part + 2, :], y[h][:, 2 * part:2 * part + 2, :], ACT.Tanh,
                                         scale=0.5).then_inc(tanh_done[h], 1)

                def square(h, u):
                    act.wait_ge(silu_done[h], u * 2 + 1)
                    nc.scalar.activation(sq[h][:, :, :], z[h][:, 0:2, :], ACT.Square).then_inc(squared[h], 1)

                def decay(h, u):
                    act.wait_ge(masked[h], u + 1)
                    for blk, (c0, w) in enumerate(((0, S), (S, P))):
                        last = nc.scalar.activation(dec[h][:, c0:c0 + w], gm[h][:, c0:c0 + w], ACT.Exp,
                                                    bias=ng[h][:, blk:blk + 1], scale=1.0)
                    last.then_inc(decayed[h], 1)

                def scale_v(h, u):
                    act.wait_ge(v_turned[h], u + 1)
                    act.wait_ge(scales_ready[h], u + 1)
                    for t in range(TB):
                        last = nc.scalar.activation(vs[h][:, t, :], k.ps[h][:, 1, t * VE:(t + 1) * VE], ACT.Copy,
                                                    scale=nk[h][:, t:t + 1])
                    last.then_inc(v_scaled[h], 1)

                def keep_tt(h, u, i):
                    act.wait_ge(tt_ready[h], u * NL + (i + 1))
                    nc.scalar.copy(halves(tt[h][:, 1, :, :].rearrange("p b s -> p (b s)"), levels[i], 1),
                                   k.ps[h][:, 3, 0:P].rearrange("p (n b) -> p n b", b=levels[i])).then_inc(tt_kept[h], 1)

                def keep_w(h, u, blk):
                    act.wait_ge(solved[h], u * 3 + (1 + 2 * blk))
                    nc.scalar.copy(wv[h][:, blk, :], k.ps[h][:, 2 + blk, 0:VE]).then_inc(w_kept[h], 1)

                def keep_mix(h, u):
                    act.wait_ge(mixed[h], u + 1)
                    nc.scalar.copy(oT[h][:, :, :], k.ps[h][:, 2, :].rearrange("p (m s) -> p m s", m=2))\
                        .then_inc(mix_kept[h], 1)

                def stage(h, grown, given, prepared, project):
                    g = 1 - h
                    for i in range(NL):
                        if given is not None and i == 0:
                            keep_w(g, given, 0)
                        if project is not None and i in (1, 3):
                            tap(h, project, i // 2)
                        if prepared is not None and i == 2:
                            tanh_of(g, prepared, 0)
                        if given is not None and i == 2:
                            keep_w(g, given, 1)
                        if prepared is not None and i == 2:
                            tanh_of(g, prepared, 1)
                        if prepared is not None and i == 3:
                            square(g, prepared)
                        if prepared is not None and i == 3:
                            decay(g, prepared)
                        if given is not None and i == 4:
                            keep_mix(g, given)
                        if grown is not None:
                            keep_tt(h, grown, i)
                    if prepared is not None:
                        scale_v(g, prepared)

                for part in range(2):
                    tap(0, 0, part)
                schedule(act, stage)

            @block.vector
            def _(dve):
                ch = Chain(dve, chain0, 0)
                dve.wait_ge(gates_ready, 1)
                zz = k.ps[0][:, 0, :].rearrange("p (t e) -> p t e", t=NT)
                ch.link(nc.vector.tensor_copy(za[:, :, :], zz[:, :, 0:HK]))
                nc.vector.scalar_tensor_tensor(zabs[:, :, 0:HK], zz[:, :, 0:HK], -1.0, za[:, :, :], ALU.mult, ALU.max)
                nc.vector.tensor_copy(zabs[:, :, HK:2 * HK], zz[:, :, HK:2 * HK]).then_inc(gates_abs, 1)
                dve.wait_ge(gates_exp, 1)
                ch.link(nc.vector.tensor_scalar(beta[:, :, :], zabs[:, :, HK:2 * HK], 1.0, None, ALU.add))
                ch.link(nc.vector.reciprocal(beta[:, :, :], beta[:, :, :]))
                dve.wait_ge(gates_log, 1)
                nc.vector.scalar_tensor_tensor(loga[:, :, :], za[:, :, :], 0.0, loga[:, :, :], ALU.min, ALU.subtract)\
                    .then_inc(loga_ready, 1)
                dve.wait_ge(cum_ready, 1)
                cp = k.ps[0][:, 1, 0:NT * HK].rearrange("p (t e) -> p t e", t=NT)
                nc.vector.tensor_scalar(negcum[:, :, :], cp, -1.0, None, ALU.mult)
                nc.vector.tensor_copy(cum[:, :, :], cp).then_inc(cum_kept, 1)
                dve.wait_ge(cum_kept, 1)

                def convolve(h, u, back, part):
                    if back == 1:
                        dve.wait_ge(tapped[h], u * 2 + (part + 1))
                    else:
                        dve.wait_ge(conv_part[h], u * (2 * (KC - 2)) + (2 * (back - 2) + part + 1))
                    for m in (2 * part, 2 * part + 1):
                        last = nc.vector.scalar_tensor_tensor(
                            y[h][:, m, back:S], k.ps[h][:, m // 2, (m % 2) * S:(m % 2 + 1) * S - back],
                            taps[h][:, m, KC - 1 - back:KC - back],
                            y[h][:, m, back:S], ALU.mult, ALU.add)
                    last.then_inc(conv_part[h] if back < KC - 1 else convolved[h], 1)

                def silu(h, u, part):
                    dve.wait_ge(tanh_done[h], u * 2 + (part + 1))
                    mm = slice(2 * part, 2 * part + 2)
                    nc.vector.scalar_tensor_tensor(z[h][:, mm, :], e[h][:, mm, :], 1.0, y[h][:, mm, :], ALU.add,
                                                   ALU.mult).then_inc(silu_done[h], 1)

                def keep_lengths(h, u):
                    dve.wait_ge(lengths[h], u + 1)
                    nc.vector.tensor_scalar(n2[h][:, :], k.ps[h][:, 1, S:S + 4], 4e-24, None, ALU.max)\
                        .then_inc(lengths_kept[h], 1)

                def scales(h, u):
                    dve.wait_ge(inverse_len[h], u + 1)
                    nc.vector.scalar_tensor_tensor(nk[h][:, :], n2[h][:, 0:TB], 0.5, rn[h][:, 0:TB], ALU.mult, ALU.mult)
                    nc.vector.tensor_copy(rq[h][:, ds(u % 2, 1), :].rearrange("p a t -> p (a t)"), rn[h][:, TB:2 * TB])
                    bt = beta[:, ds(batch(u) * TB, TB), ds(pair(u) * 2 + h, 1)].rearrange("p t a -> p (t a)")
                    nc.vector.tensor_tensor(cj[h][:, :], bt, rn[h][:, 0:TB], ALU.mult).then_inc(c_part[h], 1)
                    dve.wait_ge(c_part[h], u + 1)
                    nc.vector.tensor_tensor(cj[h][:, :], cj[h][:, :], rn[h][:, 0:TB], ALU.mult).then_inc(scales_ready[h], 1)

                def scale_products(h, u):
                    dve.wait_ge(scales_ready[h], u + 1)
                    dve.wait_ge(products[h], u + 1)
                    dve.wait_ge(decayed[h], u + 1)
                    nc.vector.scalar_tensor_tensor(lp0[h], k.ps[h][:, 0, :].rearrange("p (a s) -> p a s", a=2),
                                                   cj[h][:, 0:1], dec[h][:, 0:S].unsqueeze(1).to_broadcast([P, 2, S]),
                                                   ALU.mult, ALU.mult)
                    nc.vector.scalar_tensor_tensor(lp1[h], k.ps[h][:, 1, 0:S].rearrange("p (a s) -> p a s", a=2),
                                                   cj[h][:, 1:2], dec[h][:, S:S + P].unsqueeze(1).to_broadcast([P, 2, P]),
                                                   ALU.mult, ALU.mult).then_inc(lp_ready[h], 1)

                def first_inverse(h, u):
                    dve.wait_ge(lp_ready[h], u + 1)
                    nc.vector.tensor_tensor(ntm[h][:, :, :], lp[h][:, :, 0:P],
                                            negstrict[:, :].unsqueeze(1).to_broadcast([P, 2, P]), ALU.mult)\
                        .then_inc(nt_part[h], 1)
                    dve.wait_ge(nt_part[h], u * 2 + 1)
                    nc.vector.tensor_tensor(nt[h][:, :, :], ntm[h][:, :, :],
                                            k.ident[:, :].unsqueeze(1).to_broadcast([P, 2, P]), ALU.add)\
                        .then_inc(nt_part[h], 1)
                    dve.wait_ge(nt_part[h], u * 2 + 2)
                    nc.vector.tensor_tensor(tt[h][:, 1], nt[h][:, :, :],
                                            lvl1T[:, :].unsqueeze(1).to_broadcast([P, 2, P]), ALU.mult)\
                        .then_inc(nt_ready[h], 1)

                def keep_first(h, u):
                    dve.wait_ge(t_ready[h], u * NL + 1)
                    nc.vector.tensor_copy(tt[h][:, 0, :, :], k.ps[h][:, 2, 0:S].rearrange("p (b s) -> p b s", b=2))\
                        .then_inc(t_kept[h], 1)

                def keep_off(h, u, i):
                    b = levels[i]
                    dve.wait_ge(off_ready[h], u * NL + (i + 1))
                    for blk in range(2):
                        last = nc.vector.tensor_tensor(halves(off[h][:, i, blk, :], b, 0),
                                                       k.ps[h][:, 2, blk * HALF:(blk + 1) * HALF].rearrange("p (n b) -> p n b", b=b),
                                                       halves(lvl[:, i, :], b, 0), ALU.mult)
                    last.then_inc(off_kept[h], 1)

                def keep_t(h, u, i):
                    b = levels[i]
                    dve.wait_ge(t_ready[h], u * NL + (i + 2))
                    nc.vector.tensor_copy(halves(tt[h][:, 0, :, :].rearrange("p b s -> p (b s)"), b, 0),
                                          k.ps[h][:, 2, S:S + P].rearrange("p (n b) -> p n b", b=b)).then_inc(t_kept[h], 1)

                def keep_rest(h, u):
                    dve.wait_ge(solved[h], u * 3 + 2)
                    dve.wait_ge(v_scaled[h], u + 1)
                    nc.vector.tensor_tensor(rest[h][:, :], vs[h][:, 1, :], k.ps[h][:, 2, VE:2 * VE], ALU.subtract)\
                        .then_inc(rest_kept[h], 1)

                def add_out(h, u):
                    dve.wait_ge(out_ready[h], u + 1)
                    for t in range(TB):
                        xt = k.x[:, ds(batch(u) * TB + t, 1), :].rearrange("p a d -> p (a d)")
                        last = nc.vector.scalar_tensor_tensor(xt, k.ps[h][:, 3, t * D:(t + 1) * D],
                                                              rq[h][:, ds(u % 2, 1), t:t + 1].rearrange("p a t -> p (a t)"), xt, ALU.mult, ALU.add)
                    last.then_inc(added[h], 1)

                def stage(h, grown, given, prepared, project):
                    g = 1 - h
                    if grown is not None:
                        keep_first(h, grown)
                    for i in range(NL):
                        if grown is not None:
                            keep_off(h, grown, i)
                        if given is not None and i == 1:
                            keep_rest(g, given)
                        if prepared is not None and i < 2:
                            convolve(g, prepared, i + 2, 0)
                        if prepared is not None and i == 3:
                            silu(g, prepared, 1)
                        if project is not None and i == 3:
                            convolve(h, project, 1, 0)
                        if project is not None and i == 4:
                            convolve(h, project, 1, 1)
                        if prepared is not None and i == 4:
                            scales(g, prepared)
                        if prepared is not None and i == 5:
                            first_inverse(g, prepared)
                        if grown is not None and i < NL - 1:
                            keep_t(h, grown, i)
                        if prepared is not None and i < 2:
                            convolve(g, prepared, i + 2, 1)
                        if prepared is not None and i == 2:
                            silu(g, prepared, 0)
                        if prepared is not None and i == 3:
                            keep_lengths(g, prepared)
                        if prepared is not None and i == 4:
                            scale_products(g, prepared)
                        if given is not None and i == 5:
                            add_out(g, given)

                for part in range(2):
                    convolve(0, 0, 1, part)
                schedule(dve, stage)


class CrossRope:

    TWO_PI = (6.28125, 0.0019350051879882812, 3.019915981956753e-07)
    ROUND = 12582912.0

    def __init__(self, k, stack):
        nc, ins = k.nc, k.ins
        loaded, chain = k.sem("rope_loaded"), k.sem("rope_chain")
        reduced, sines = k.sem("rope_reduced"), k.sem("rope_sines")
        self.cq, self.sq_, self.ck, self.sk = [k.sb(f"rope_{n}", [P, NT, HD], F32, stack) for n in ("cq", "sq", "ck", "sk")]
        self.cc, self.sc = [k.sb(f"rope_{n}", [CTX, B, HD], F32, stack) for n in ("cc", "sc")]
        self.ctxT = k.sb("rope_ctxT", [P, DC, B * CTX], F32, stack)
        with ExitStack() as st:
            pos_i, cpos_i = k.sb("pos_i", [P, NT], I32, st), k.sb("cpos_i", [CTX, B], I32, st)
            pos, cpos = k.sb("pos", [P, NT], F32, st), k.sb("cpos", [CTX, B], F32, st)
            inv = k.sb("inv", [P, HALF], F32, st)
            wn = k.sb("wn", [P, 2, HD], F32, st)
            ang, turns, r, r2 = [k.sb(f"rope_t{i}", [P, NT, HALF], F32, st) for i in range(4)]
            cang, cturns, cr, cr2 = [k.sb(f"rope_u{i}", [CTX, B, HALF], F32, st) for i in range(4)]
            with nc.Block() as block:

                @block.sync
                def _(sp):
                    for dst, name in ((pos_i[:, :], "pos"), (cpos_i[:, :], "cpos")):
                        sp.dma_start(dst, ins[name]).then_inc(loaded, 16)
                    sp.dma_start(inv[:, :], ins["c_inv"]).then_inc(loaded, 16)
                    for i, name in enumerate(("w1xqn", "w1xkn")):
                        sp.dma_start(wn[:, i, :], ins[name].partition_broadcast(P)).then_inc(loaded, 16)
                    sp.dma_start(self.ctxT[:, :, :], ins["ctxT"].rearrange("(c p) n -> p c n", p=P)).then_inc(loaded, 16)
                    sp.wait_ge(loaded, 96)

                @block.scalar
                def _(act):
                    act.wait_ge(reduced, 1)
                    for a in (r, r2, cr, cr2):
                        last = nc.scalar.activation(a[:, :, :], a[:, :, :], ACT.Sin)
                    last.then_inc(sines, 1)

                @block.vector
                def _(dve):
                    ch = Chain(dve, chain, 0)
                    dve.wait_ge(loaded, 96)
                    for p_i, p_f, a, tu, rr, rh, m, rows in ((pos_i, pos, ang, turns, r, r2, NT, P),
                                                             (cpos_i, cpos, cang, cturns, cr, cr2, B, CTX)):
                        ch.link(nc.vector.tensor_copy(p_f[:, :], p_i[:, :]))
                        ch.link(nc.vector.tensor_tensor(a[:, :, :], inv[0:rows, :].unsqueeze(1).to_broadcast([rows, m, HALF]),
                                                        p_f[:, :].unsqueeze(2).to_broadcast([rows, m, HALF]), ALU.mult))
                        ch.link(nc.vector.tensor_scalar(tu[:, :, :], a[:, :, :], float(1 / (2 * np.pi)), self.ROUND,
                                                        ALU.mult, ALU.add))
                        ch.link(nc.vector.tensor_scalar(tu[:, :, :], tu[:, :, :], self.ROUND, None, ALU.subtract))
                        for part in self.TWO_PI:
                            ch.link(nc.vector.scalar_tensor_tensor(a[:, :, :], tu[:, :, :], -part, a[:, :, :], ALU.mult, ALU.add))
                        ch.link(nc.vector.tensor_scalar(rr[:, :, :], a[:, :, :], float(-np.float32(np.pi)),
                                                        3.1415925, ALU.max, ALU.min))
                        last = nc.vector.tensor_scalar(rh[:, :, :], rr[:, :, :], 0.5, None, ALU.mult)
                        ch.link(last)
                    dve.sem_inc(reduced, 1)
                    dve.wait_ge(sines, 1)
                    for rr, rh, m, rows, outs in ((r, r2, NT, P, ((self.cq, self.sq_, 0), (self.ck, self.sk, 1))),
                                                  (cr, cr2, B, CTX, ((self.cc, self.sc, 1),))):
                        ch.link(nc.vector.tensor_tensor(rh[:, :, :], rh[:, :, :], rh[:, :, :], ALU.mult))
                        ch.link(nc.vector.tensor_scalar(rh[:, :, :], rh[:, :, :], -2.0, 1.0, ALU.mult, ALU.add))
                        for co, si, i in outs:
                            for a0, b0, sign in ((0, HALF, -1.0), (HALF, 0, 1.0)):
                                wa = wn[0:rows, i:i + 1, a0:a0 + HALF].to_broadcast([rows, m, HALF])
                                wb = wn[0:rows, i:i + 1, b0:b0 + HALF].to_broadcast([rows, m, HALF])
                                nc.vector.tensor_tensor(co[:, :, a0:a0 + HALF], rh[:, :, :], wa, ALU.mult)
                                last = nc.vector.scalar_tensor_tensor(si[:, :, a0:a0 + HALF], rr[:, :, :], sign, wb,
                                                                      ALU.mult, ALU.mult)
                    ch.link(last)

    def q(self, p, h):
        return (t[:, ds(p * (2 * TB) + h * TB, TB), :] for t in (self.cq, self.sq_))

    def k(self, p, h):
        return (t[:, ds(p * (2 * TB) + h * TB, TB), :] for t in (self.ck, self.sk))

    def c(self, p, h):
        return (t[:, ds(p * 2 + h, 1), :].rearrange("p a d -> p (a d)") for t in (self.cc, self.sc))


E1, EK, TOPK1, I1, CAP = 128, 48, 8, 96, 96
SLOTS = EK * CAP
FAR = float(1 << 20)


def sparse_experts(k):
    nc, ins = k.nc, k.ins
    ZN = 4
    EU = 4
    loaded, chain = k.sem("sp_loaded"), k.sem("sp_chain")
    logits_ready, shifted, exps_done = k.sem("sp_logits"), k.sem("sp_shifted"), k.sem("sp_exps")
    chosen, before_ready, slots_ready = k.sem("sp_chosen"), k.sem("sp_before"), k.sem("sp_slots")
    zero_made, zeroed, scattered = k.sem("sp_zero_made"), k.sem("sp_zeroed"), k.sem("sp_scattered")
    in_loaded = [[k.sem(f"sp_in{q}{h}") for h in range(2)] for q in range(2)]
    turned, x_kept, up_ready = k.sems("sp_turned"), k.sems("sp_x_kept"), k.sems("sp_up_ready")
    silu_done, act_ready, down_ready = k.sems("sp_silu"), k.sems("sp_act"), k.sems("sp_down")
    y_kept, y_stored = k.sems("sp_y_kept"), k.sems("sp_y_stored")
    gathered = [k.sem(f"sp_gathered{h}") for h in range(2)]
    combined, out_stored = k.sem("sp_combined"), k.sem("sp_out_stored")
    add_chain = k.sem("sp_add_chain")
    xrows = nc.dram_tensor("slot_rows", (SLOTS, D), F32, kind="Internal").ap()
    yrows = nc.dram_tensor("slot_results", (SLOTS, D), F32, kind="Internal").ap()
    with ExitStack() as st:
        def sb(name, shape, dt=F32, stack=st):
            return k.sb(f"sp_{name}", shape, dt, stack)

        w = sb("w", [P, NT, TOPK1])
        slot_i = sb("slot_i", [P, NT, TOPK1], U32)
        zero = sb("zero", [P, SLOTS * D // P // ZN])
        wgu = [[sb(f"wgu{q}{h}", [P, EU * DC, 2 * I1]) for h in range(2)] for q in range(2)]
        wd = [[sb(f"wd{q}{h}", [I1, EU, D]) for h in range(2)] for q in range(2)]
        xs = [[sb(f"xs{q}{h}", [CAP, EU, D]) for h in range(2)] for q in range(2)]

        with ExitStack() as st1:
            def sb1(name, shape, dt=F32):
                return sb(name, shape, dt, st1)

            gate = sb1("gate", [P, DC, E1])
            o2n_i, o2n = sb1("o2n_i", [P, E1], I32), sb1("o2n", [P, E1])
            neg, base = sb1("neg", [P, E1]), sb1("base", [P, E1])
            iota = sb1("iota", [P, E1])
            trib, onesb = sb1("trib", [P, P], BF16), sb1("onesb", [P, P], BF16)
            lg, left = sb1("lg", [P, NT, E1]), sb1("left", [P, NT, E1])
            best, at, atf = sb1("best", [P, NT, 8]), sb1("at", [P, NT, 8], U32), sb1("atf", [P, NT, 8])
            tot, rtot = sb1("tot", [P, NT]), sb1("rtot", [P, NT])
            m = sb1("m", [P, NT, E1], BF16)
            mc = sb1("mc", [P, NT, E1], BF16)
            far = sb1("far", [P, NT, E1])
            table = sb1("table", [P, NT, E1])
            junk = [sb1(f"junk{i}", [P, E1]) for i in range(TOPK1)]
            slot_f = sb1("slot_f", [P, NT, TOPK1])
            ok = sb1("ok", [P, NT, TOPK1])
            NB = NT * E1 // 512
            with nc.Block() as block:

                @block.sync
                def _(sp):
                    sp.dma_start(gate[:, :, :], ins["w1r"].rearrange("(c p) n -> p c n", p=P)).then_inc(loaded, 16)
                    sp.dma_start(o2n_i[:, :], ins["o2n"].partition_broadcast(P)).then_inc(loaded, 16)
                    sp.dma_start(iota[:, :], ins["c_iota"]).then_inc(loaded, 16)
                    sp.dma_start(trib[:, :], ins["c_trib"]).then_inc(loaded, 16)
                    sp.dma_start(onesb[:, :], ins["c_onesb"]).then_inc(loaded, 16)
                    sp.wait_ge(zero_made, 1)
                    for i in range(ZN):
                        sp.dma_start(xrows.rearrange("(i p a) d -> i p (a d)", i=ZN, p=P)[i], zero[:, :]).then_inc(zeroed, 16)
                    sp.wait_ge(scattered, 16 * NT * TOPK1)

                @block.gpsimd
                def _(pool):
                    nc.gpsimd.memset(zero[:, :], 0.0).then_inc(zero_made, 1)
                    pool.wait_ge(zeroed, 16 * ZN)
                    pool.wait_ge(slots_ready, 1)
                    for i in range(NT):
                        for j in range(TOPK1):
                            nc.gpsimd.indirect_dma_start(
                                out=xrows, out_offset=bass.IndirectOffsetOnAxis(slot_i[:, i, j:j + 1], axis=0),
                                in_=k.xn_rows[:, i, :], in_offset=None, bounds_check=SLOTS - 1,
                                oob_is_err=False).then_inc(scattered, 16)
                    pool.wait_ge(scattered, 16 * NT * TOPK1)

                @block.tensor
                def _(pe):
                    pe.wait_ge(loaded, 80)
                    for i in range(NT):
                        for c in range(DC):
                            last = nc.tensor.matmul(k.ps[0][:, i // 4, (i % 4) * E1:(i % 4 + 1) * E1],
                                                    k.xnT[:, c, i * P:(i + 1) * P], gate[:, c, :], start=c == 0, stop=c == DC - 1)
                    last.then_inc(logits_ready, 1)
                    pe.wait_ge(chosen, 1)
                    for i in range(NT):
                        o = k.ps[1][:, i // 4, (i % 4) * E1:(i % 4 + 1) * E1]
                        last = nc.tensor.matmul(o, trib[:, :], m[:, i, :], start=True, stop=i == 0)
                        if i:
                            last = nc.tensor.matmul(o, onesb[:, :], mc[:, i - 1, :], start=False, stop=True)
                    last.then_inc(before_ready, 1)

                @block.scalar
                def _(act):
                    act.wait_ge(shifted, 1)
                    nc.scalar.activation(w[:, :, :], w[:, :, :], ACT.Exp).then_inc(exps_done, 1)

                @block.vector
                def _(dve):
                    ch = Chain(dve, chain, 0)
                    dve.wait_ge(loaded, 80)
                    ch.link(nc.vector.tensor_copy(o2n[:, :], o2n_i[:, :]))
                    nc.vector.tensor_scalar(neg[:, :], o2n[:, :], -1.0, NEG, ALU.is_equal, ALU.mult)
                    ch.link(nc.vector.tensor_scalar(junk[0][:, :], o2n[:, :], 0.0, FAR, ALU.is_lt, ALU.mult))
                    ch.link(nc.vector.scalar_tensor_tensor(base[:, :], o2n[:, :], float(CAP), junk[0][:, :], ALU.mult, ALU.add))
                    dve.wait_ge(logits_ready, 1)
                    ch.link(nc.vector.tensor_tensor(lg[:, :, :], k.ps[0][:, 0:NB, :].rearrange("p a (t e) -> p (a t) e", e=E1),
                                                    neg[:, :].unsqueeze(1).to_broadcast([P, NT, E1]), ALU.add))
                    for i in range(NT):
                        last = nc.vector.max(best[:, i, :], lg[:, i, :])
                    ch.link(last)
                    for i in range(NT):
                        last = nc.vector.max_index(at[:, i, :], best[:, i, :], lg[:, i, :])
                    for i in range(NT):
                        last = nc.vector.match_replace(out=left[:, i, :], in_to_replace=best[:, i, :], in_values=lg[:, i, :],
                                                       imm_value=2 * NEG)
                    ch.link(last)
                    nc.vector.tensor_tensor(w[:, :, :], best[:, :, :], best[:, :, 0:1].to_broadcast([P, NT, TOPK1]),
                                            ALU.subtract).then_inc(shifted, 1)
                    nc.vector.tensor_copy(atf[:, :, :], at[:, :, :])
                    ch.link(nc.vector.tensor_scalar(m[:, :, :], left[:, :, :], 2 * NEG, None, ALU.is_equal))
                    ch.link(nc.vector.tensor_copy(mc[:, 0, :], m[:, 0, :]))
                    for i in range(1, NT):
                        ch.link(nc.vector.tensor_tensor(mc[:, i, :], mc[:, i - 1, :], m[:, i, :], ALU.add))
                    dve.sem_inc(chosen, 1)
                    dve.wait_ge(before_ready, 1)
                    before = k.ps[1][:, 0:NB, :].rearrange("p a (t e) -> p (a t) e", e=E1)
                    nc.vector.tensor_scalar(far[:, :, :], before, CAP - 0.5, FAR, ALU.is_gt, ALU.mult)
                    ch.link(nc.vector.tensor_tensor(table[:, :, :], before,
                                                    base[:, :].unsqueeze(1).to_broadcast([P, NT, E1]), ALU.add))
                    ch.link(nc.vector.tensor_tensor(table[:, :, :], table[:, :, :], far[:, :, :], ALU.add))
                    for i in range(NT):
                        for j in range(TOPK1):
                            last = nc.vector.scalar_tensor_tensor(junk[j][:, :], iota[:, :], atf[:, i, j:j + 1], table[:, i, :],
                                                                  ALU.is_equal, ALU.mult, accum_out=slot_f[:, i, j:j + 1])
                        ch.link(last)
                    ch.link(nc.vector.tensor_copy(slot_i[:, :, :], slot_f[:, :, :]))
                    dve.sem_inc(slots_ready, 1)
                    dve.wait_ge(exps_done, 1)
                    ch.link(nc.vector.tensor_reduce(tot[:, :], w[:, :, :], AX_X, ALU.add))
                    ch.link(nc.vector.reciprocal(rtot[:, :], tot[:, :]))
                    nc.vector.tensor_scalar(ok[:, :, :], slot_f[:, :, :], SLOTS - 0.5, None, ALU.is_lt)
                    ch.link(nc.vector.tensor_tensor(w[:, :, :], w[:, :, :], rtot[:, :].unsqueeze(2).to_broadcast([P, NT, TOPK1]),
                                                    ALU.mult))
                    ch.link(nc.vector.tensor_tensor(w[:, :, :], w[:, :, :], ok[:, :, :], ALU.mult))

        xT = [sb(f"xT{h}", [P, 2, 4 * CAP]) for h in range(2)]
        sg = [sb(f"sg{h}", [I1, EU, CAP]) for h in range(2)]
        hT = [sb(f"hT{h}", [I1, EU, CAP]) for h in range(2)]
        y = [sb(f"y{h}", [CAP, EU, D]) for h in range(2)]
        UN = EK // EU // 4
        with nc.Block() as block:

            @block.sync
            def _(sp):
                def load(q, h, e):
                    s = in_loaded[q][h]
                    sp.dma_start(xs[q][h][:, :, :], xrows.rearrange("(e c) d -> e c d", c=CAP)[ds(e, EU)]
                                 .rearrange("e c d -> c e d")).then_inc(s, 16)
                    sp.dma_start(wgu[q][h][:, :, :], ins["w1gu"][ds(e, EU)].rearrange("e (c p) n -> p (e c) n", p=P))\
                        .then_inc(s, 16)
                    sp.dma_start(wd[q][h][:, :, :], ins["w1d"][ds(e, EU)].rearrange("e p n -> p e n")).then_inc(s, 16)

                for q in range(2):
                    for h in range(2):
                        load(q, h, (2 * q + h) * EU)
                with sp.Fori(1, UN) as j:
                    for q in range(2):
                        for h in range(2):
                            sp.wait_ge(down_ready[h], j * 2 + (q - 1))
                            load(q, h, j * (4 * EU) + (2 * q + h) * EU)

            @block.tensor
            def _(pe):
                with pe.Fori(0, UN) as j:
                    for q in range(2):
                        n = j * 2 + (q + 1)
                        for h in range(2):
                            pe.wait_ge(in_loaded[q][h], (j + 1) * 48)
                            if q == 1:
                                pe.wait_ge(y_kept[h], n - 1)
                            for e in range(EU):
                                for c in range(DC):
                                    last = nc.tensor.transpose(
                                        k.ps[h][:, e // 2, (e % 2 * 2 + c) * CAP:(e % 2 * 2 + c + 1) * CAP],
                                        xs[q][h][:, e, c * P:(c + 1) * P], k.ident[0:CAP, 0:CAP])
                            last.then_inc(turned[h], 1)
                        for h in range(2):
                            pe.wait_ge(x_kept[h], n)
                            for e in range(EU):
                                for gu in range(2):
                                    for c in range(DC):
                                        last = nc.tensor.matmul(
                                            k.ps[h][0:I1, 2 + e // 2, (e % 2 * 2 + gu) * CAP:(e % 2 * 2 + gu + 1) * CAP],
                                            wgu[q][h][:, e * DC + c, gu * I1:(gu + 1) * I1],
                                            xT[h][:, e // 2, (e % 2 * 2 + c) * CAP:(e % 2 * 2 + c + 1) * CAP],
                                            start=c == 0, stop=c == DC - 1)
                            last.then_inc(up_ready[h], 1)
                        for h in range(2):
                            pe.wait_ge(act_ready[h], n)
                            for e in range(EU):
                                last = nc.tensor.matmul(k.ps[h][0:CAP, e // 2, (e % 2) * D:(e % 2 + 1) * D], hT[h][:, e, :],
                                                        wd[q][h][:, e, :], start=True, stop=True)
                            last.then_inc(down_ready[h], 1)
                        if q == 1:
                            for h in range(2):
                                pe.wait_ge(y_kept[h], n)

            @block.scalar
            def _(act):
                for h in range(2):
                    act.sem_inc(y_stored[h], 16)
                with act.Fori(0, UN) as j:
                    for q in range(2):
                        n = j * 2 + (q + 1)
                        for h in range(2):
                            act.wait_ge(turned[h], n)
                            nc.scalar.copy(xT[h][:, :, :], k.ps[h][:, 0:2, 0:4 * CAP]).then_inc(x_kept[h], 1)
                        for h in range(2):
                            act.wait_ge(up_ready[h], n)
                            nc.scalar.activation(sg[h][:, :, :].rearrange("p (a b) c -> p a b c", a=2),
                                                 k.ps[h][0:I1, 2:4, 0:4 * CAP].rearrange("p a (b g c) -> p a b g c", b=2, g=2)[:, :, :, 0],
                                                 ACT.Silu).then_inc(silu_done[h], 1)
                        for h in range(2):
                            act.wait_ge(y_kept[h], n)
                            act.dma_start(yrows.rearrange("(e c) d -> e c d", c=CAP)[ds(j * (4 * EU) + (2 * q + h) * EU, EU)]
                                          .rearrange("e c d -> c e d"), y[h][:, :, :]).then_inc(y_stored[h], 16)
                for h in range(2):
                    act.wait_ge(y_stored[h], 16 * 2 * UN + 16)

            @block.vector
            def _(dve):
                with dve.Fori(0, UN) as j:
                    for q in range(2):
                        n = j * 2 + (q + 1)
                        for h in range(2):
                            dve.wait_ge(silu_done[h], n)
                            nc.vector.tensor_tensor(hT[h][:, :, :].rearrange("p (a b) c -> p a b c", a=2),
                                                    sg[h][:, :, :].rearrange("p (a b) c -> p a b c", a=2),
                                                    k.ps[h][0:I1, 2:4, 0:4 * CAP].rearrange("p a (b g c) -> p a b g c", b=2, g=2)[:, :, :, 1],
                                                    ALU.mult).then_inc(act_ready[h], 1)
                        for h in range(2):
                            dve.wait_ge(down_ready[h], n)
                            dve.wait_ge(y_stored[h], n * 16)
                            nc.vector.tensor_copy(y[h][:, :, :].rearrange("p (a b) d -> p a b d", a=2),
                                                  k.ps[h][0:CAP, 0:2, :].rearrange("p a (b d) -> p a b d", b=2))\
                                .then_inc(y_kept[h], 1)

        NG = 2
        back = [sb(f"back{i}", [P, TOPK1, D]) for i in range(NG)]
        with nc.Block() as block:

            @block.gpsimd
            def _(pool):
                for i in range(NG):
                    nc.gpsimd.memset(back[i][:, :, :], 0.0).then_inc(zero_made, 1)
                pool.wait_ge(zero_made, 1 + NG)
                for i in range(NT):
                    if i >= NG:
                        pool.wait_ge(combined, i - NG + 1)
                    for j in range(TOPK1):
                        nc.gpsimd.indirect_dma_start(
                            out=back[i % NG][:, j, :], out_offset=None, in_=yrows,
                            in_offset=bass.IndirectOffsetOnAxis(slot_i[:, i, j:j + 1], axis=0),
                            bounds_check=SLOTS - 1, oob_is_err=False).then_inc(gathered[i % NG], 16)

            @block.vector
            def _(dve):
                ch = Chain(dve, add_chain, 0)
                for i in range(NT):
                    dve.wait_ge(gathered[i % NG], 16 * TOPK1 * (i // NG + 1))
                    for j in range(TOPK1):
                        ins_ = nc.vector.scalar_tensor_tensor(k.x[:, i, :], back[i % NG][:, j, :], w[:, i, j:j + 1], k.x[:, i, :],
                                                              ALU.mult, ALU.add)
                        if j < TOPK1 - 1:
                            ch.link(ins_)
                    ins_.then_inc(combined, 1)

            @block.sync
            def _(sp):
                for i in range(NT):
                    sp.wait_ge(combined, i + 1)
                    sp.dma_start(k.out[i // TB, (i % TB) * P:(i % TB + 1) * P, :], k.x[:, i, :]).then_inc(out_stored, 16)
                sp.wait_ge(out_stored, 16 * NT)


class SelfRope:

    def __init__(self, k, stack):
        self.cos = k.sb("rope_cos", [P, TB, HD], F32, stack)
        self.sin = k.sb("rope_sin", [P, TB, HD], F32, stack)
        loaded = k.sem("rope_loaded")
        with k.nc.Block() as block:

            @block.sync
            def _(sp):
                for t, name in ((self.cos, "c_cos"), (self.sin, "c_sin")):
                    sp.dma_start(t[:, :, :], k.ins[name].rearrange("(t p) d -> p t d", p=P)).then_inc(loaded, 16)
                sp.wait_ge(loaded, 32)

    def q(self, p, h):
        return self.cos[:, :, :], self.sin[:, :, :]

    def k(self, p, h):
        return self.cos[:, :, :], self.sin[:, :, :]


def build(nc, ins, out):
    with ExitStack() as stack:
        k = Core(nc, ins, out, stack)
        load_constants(k)
        layernorm(k)
        with ExitStack() as st, k.own_semaphores("_0"):
            attention(k, ("w0q", "w0kv", "w0o"), SelfRope(k, st), None)
        layernorm(k)
        with k.own_semaphores(""):
            set_attention(k)
        layernorm(k)
        with k.own_semaphores(""):
            experts(k)
        layernorm(k)
        with k.own_semaphores(""):
            delta_attention(k)
        layernorm(k)
        with ExitStack() as st, k.own_semaphores("_1"):
            rope = CrossRope(k, st)
            attention(k, ("w1xq", "w1xkv", "w1xo"), rope, rope)
        with ExitStack() as st, k.own_semaphores(""):
            k.xn_rows = k.sb("xn_rows", [P, NT, D], F32, st)
            layernorm(k, k.xn_rows)
            sparse_experts(k)


def constants():
    c = {}
    c["c_ident"] = np.eye(P, dtype=np.float32)
    bf = mybir.dt.np(BF16)
    c["c_identb"] = np.eye(P).astype(bf)
    c["c_causb"] = np.triu(np.full((P, P), NEG), 1).astype(bf)
    inv = (np.float32(1.0) / np.float32(10000.0) ** (np.arange(0, HD, 2, dtype=np.float32) / np.float32(HD))).astype(np.float32)
    ang = (np.arange(S, dtype=np.float32)[:, None] * inv[None, :]).astype(np.float32)
    co, si = np.cos(ang), np.sin(ang)
    c["c_cos"] = np.concatenate([co, co], 1).astype(np.float32)
    c["c_sin"] = np.concatenate([-si, si], 1).astype(np.float32)
    c["c_iota"] = np.broadcast_to(np.arange(P, dtype=np.float32), (P, P))
    j, i = np.arange(P)[:, None], np.arange(P)[None, :]
    c["c_inv"] = np.broadcast_to(inv, (P, HALF))
    c["c_onesb"] = np.ones((P, P)).astype(bf)
    c["c_trib"] = (j < i).astype(bf)
    c["c_ones"] = np.ones((P, P), np.float32)
    c["c_tri"] = (j <= i).astype(np.float32)
    c["c_negstrict"] = np.where(i > j, -1.0, 0.0).astype(np.float32)
    c["c_maskadd"] = np.where(i < j, NEG, 0.0).astype(np.float32)
    lv = {n: ((i == j) | ((i // (2 * n) == j // (2 * n)) & (j // n % 2 == 1) & (i // n % 2 == 0))).astype(np.float32)
          for n in (1, 2, 4, 8, 16, 32, 64)}
    c["c_level1T"] = np.ascontiguousarray(lv[1].T)
    c["c_levels"] = np.ascontiguousarray(np.stack([lv[n] for n in (2, 4, 8, 16, 32, 64)], 1))
    return c


def heads_kv(wk, wv):
    return np.stack([wk.reshape(D, KVH, HD), wv.reshape(D, KVH, HD)], 2).reshape(D, -1)


def kernel(**inputs):
    import concourse.bacc as bacc
    from concourse.bass_utils import run_bass_kernel_spmd as run

    a = {n: np.asarray(v) for n, v in inputs.items()}
    arrays = {"x": a["x"]}
    arrays["w0q"] = a["L0_attn_Wq"]
    arrays["w0kv"] = heads_kv(a["L0_attn_Wk"], a["L0_attn_Wv"])
    arrays["w0o"] = a["L0_attn_Wo"]
    arrays["w0xq"] = a["L0_xattn_W_q"].T
    arrays["w0xb"] = a["L0_xattn_b_q"].reshape(DC, P).T
    arrays["w0xd"] = a["L0_xattn_desc_router"].T
    arrays["ctx"] = a["ctx_2048"]
    arrays["sets"] = a["itok_Sx4_0_63"]
    arrays["w0r"] = a["L0_ffn_router_w"].T
    arrays["w0rb"] = a["L0_ffn_expert_bias"]
    arrays["w0gu"] = np.concatenate([a["L0_ffn_gate_proj"], a["L0_ffn_up_proj"]], 2)
    arrays["w0d"] = a["L0_ffn_down_proj"]
    by_head = lambda m, w: np.moveaxis(m.reshape(m.shape[0], HK, w), 1, 0)
    arrays["w1kqv"] = np.concatenate([by_head(a["L1_attn_Wk"], P), by_head(a["L1_attn_Wq"], P),
                                      by_head(a["L1_attn_Wv"], VE)], 2)
    arrays["w1o"] = a["L1_attn_Wo"].reshape(HK, VE, D)
    arrays["w1ab"] = np.concatenate([a["L1_attn_Wa"], a["L1_attn_Wb"]], 1)
    feats = lambda kf, qf, vf: np.moveaxis(np.concatenate(
        [kf.reshape(HK, 1, P, -1), qf.reshape(HK, 1, P, -1), vf.reshape(HK, 2, P, -1)], 1), 2, 1)
    arrays["w1t"] = np.concatenate([feats(a["L1_attn_kcw"], a["L1_attn_qcw"], a["L1_attn_vcw"]),
                                    feats(a["L1_attn_kcb"], a["L1_attn_qcb"], a["L1_attn_vcb"])], 3)
    arrays["w1xq"] = a["L1_xattn_Wq"].T
    arrays["w1xkv"] = heads_kv(a["L1_xattn_Wk"].T, a["L1_xattn_Wv"].T)
    arrays["w1xo"] = a["L1_xattn_Wo"].T
    arrays["w1xqn"], arrays["w1xkn"] = a["L1_xattn_q_norm_w"], a["L1_xattn_k_norm_w"]
    arrays["ctxT"] = a["ctx_2048"].reshape(B * CTX, D).T
    arrays["pos"] = a["itok_BxS_4096_4607"].reshape(NT, P).T
    arrays["cpos"] = a["pos_BxS2"].T
    arrays["w1r"] = a["L1_ffn_gate_weight"].T
    arrays["w1gu"] = np.moveaxis(a["L1_ffn_gate_up_proj"], 2, 1)
    arrays["w1d"] = np.moveaxis(a["L1_ffn_down_proj"], 2, 1)
    arrays["o2n"] = a["L1_ffn_old_to_new"]
    arrays.update(constants())
    nc = bacc.Bacc("TRN2", target_bir_lowering=False, num_devices=1)
    ins = {}
    for n, v in arrays.items():
        arrays[n] = np.ascontiguousarray(v)
        ins[n] = nc.dram_tensor(f"in_{n}", v.shape, mybir.dt.from_np(v.dtype), kind="ExternalInput").ap()
    out = nc.dram_tensor("out_dram", (B, S, D), F32, kind="ExternalOutput").ap()
    build(nc, ins, out)
    r = run(nc, [{f"in_{n}": v for n, v in arrays.items()}], core_ids=[0])
    return r.results[0]["out_dram"]
```

```python
from contextlib import ExitStack, contextmanager

import numpy as np

import concourse.bass as bass
from concourse import mybir

F32 = mybir.dt.float32
BF16 = mybir.dt.bfloat16
I32 = mybir.dt.int32
U32 = mybir.dt.uint32
ALU = mybir.AluOpType
ACT = mybir.ActivationFunctionType
AX_X = mybir.AxisListType.X
ds = bass.ds

P = 128
B, S, D = 8, 256, 256
T = B * S
NT = T // P
DC = D // P
TB = S // P
NEG = -1.0e30
LN_EPS = 1e-5
LN_TILES = 4
CTX = 64
HD = 128
H, KVH = 16, 4
G = H // KVH
HALF = HD // 2


class Chain:

    def __init__(self, eng, sem, first):
        self.eng, self.sem, self.first, self.count = eng, sem, first, 0

    def link(self, ins):
        self.count += 1
        ins.then_inc(self.sem, 1)
        self.eng.wait_ge(self.sem, self.first + self.count)


class Core:

    def __init__(self, nc, ins, out, stack):
        self.nc, self.ins, self.out, self.stack = nc, ins, out, stack
        self.ln_calls = 0
        self.attn_calls = 0
        self.phase, self.suffix = None, ""

    def sb(self, name, shape, dt=F32, stack=None):
        return (stack or self.stack).enter_context(self.nc.sbuf_tensor(name, shape, dt))

    def sem(self, name):
        handle = (self.phase or self.stack).enter_context(self.nc.semaphore(name + self.suffix))
        if self.phase:
            self.phase_sems.append(handle)
        return handle

    def sems(self, name):
        return [self.sem(f"{name}{h}") for h in range(2)]

    @contextmanager
    def own_semaphores(self, suffix):
        self.phase, self.phase_sems, self.suffix = ExitStack(), [], suffix
        with self.phase:
            yield
            numbers = sorted(s.num for s in self.phase_sems)
            runs = []
            for n in numbers:
                if runs and runs[-1][-1] == n - 1:
                    runs[-1].append(n)
                else:
                    runs.append([n])
            with self.nc.Block() as block:

                @block.gpsimd
                def _(pool):
                    for r in runs:
                        pool.sem_clear(range(r[0], r[-1] + 1))
        self.phase, self.suffix = None, ""


def load_constants(k):
    nc, ins = k.nc, k.ins
    k.x = k.sb("x", [P, NT, D])
    k.xnT = k.sb("xnT", [P, DC, T])
    k.ident = k.sb("ident", [P, P])
    k.identb = k.sb("identb", [P, P], BF16)
    k.causb = k.sb("causb", [P, P], BF16)
    k.mhalf = k.sb("mhalf", [P, 16])
    k.ps = [k.stack.enter_context(nc.psum_tensor(f"ps{h}", [P, 4, 512], F32)) for h in range(2)]
    k.ln_stats = k.sb("ln_stats", [P, LN_TILES, 6])
    k.ln_mv = k.sb("ln_mv", [P, LN_TILES, 2])
    k.ln_ve = k.sb("ln_ve", [P, LN_TILES])
    k.ln_rstd = k.sb("ln_rstd", [P, LN_TILES])
    k.ln_xn = [k.sb(f"ln_xn{q}", [P, D]) for q in range(LN_TILES)]
    k.ln_chain = k.sem("ln_chain")
    k.ln_var = k.sem("ln_var")
    k.ln_pow = k.sem("ln_pow")
    k.ln_normed = k.sem("ln_normed")
    k.ln_turned = k.sem("ln_turned")
    k.ln_stored = k.sem("ln_stored")
    loaded = k.sem("const_loaded")
    made = k.sem("const_made")
    with nc.Block() as block:

        @block.sync
        def _(sp):
            for b in range(B):
                sp.dma_start(k.x[:, TB * b:TB * b + TB, :],
                             ins["x"][b].rearrange("(t p) d -> p t d", p=P)).then_inc(loaded, 16)
            sp.dma_start(k.ident[:, :], ins["c_ident"]).then_inc(loaded, 16)
            sp.dma_start(k.identb[:, :], ins["c_identb"]).then_inc(loaded, 16)
            sp.dma_start(k.causb[:, :], ins["c_causb"]).then_inc(loaded, 16)
            sp.wait_ge(loaded, 16 * (B + 3))

        @block.gpsimd
        def _(pool):
            nc.gpsimd.memset(k.mhalf[:, :], -0.5).then_inc(made, 1)
            pool.wait_ge(made, 1)


def layernorm(k, rows=None):
    nc = k.nc
    Q = LN_TILES
    turns = NT // Q

    def xn(i, q):
        return k.ln_xn[q][:, :] if rows is None else rows[:, i * Q + q, :]

    base = k.ln_calls * turns
    k.ln_calls += 1
    first = base == 0
    with nc.Block() as block:

        @block.vector
        def _(dve):
            for i in range(turns):
                for q in range(Q):
                    nc.vector.bn_stats(k.ln_stats[:, q, :], k.x[:, i * Q + q, :]).then_inc(k.ln_chain, 1)
                dve.wait_ge(k.ln_chain, (i + base) * (2 * Q) + Q)
                for q in range(Q):
                    nc.vector.bn_aggr(k.ln_mv[:, q, :], k.ln_stats[:, q, :]).then_inc(k.ln_chain, 1)
                dve.wait_ge(k.ln_chain, (i + base) * (2 * Q) + 2 * Q)
                nc.vector.tensor_scalar(k.ln_ve[:, :], k.ln_mv[:, :, 1], LN_EPS, None, ALU.add).then_inc(k.ln_var, 1)
                dve.wait_ge(k.ln_turned, i + base + 1)
                dve.wait_ge(k.ln_pow, i + base + 1)
                for q in range(Q):
                    last = nc.vector.tensor_scalar(xn(i, q), k.x[:, i * Q + q, :],
                                                   k.ln_mv[:, q, 0:1], k.ln_rstd[:, q:q + 1],
                                                   ALU.subtract, ALU.mult)
                last.then_inc(k.ln_normed, 1)

        @block.gpsimd
        def _(pool):
            for i in range(turns):
                pool.wait_ge(k.ln_var, i + base + 1)
                nc.gpsimd.tensor_tensor(k.ln_rstd[:, :], k.ln_ve[:, :], k.mhalf[:, 0:Q], ALU.pow).then_inc(k.ln_pow, 1)

        @block.tensor
        def _(pe):
            if first:
                pe.sem_inc(k.ln_turned, 1)
            for i in range(turns):
                pe.wait_ge(k.ln_normed, i + base + 1)
                pe.wait_ge(k.ln_stored, i + base + 1)
                for q in range(Q):
                    for c in range(DC):
                        last = nc.tensor.transpose(k.ps[0][:, c, q * P:(q + 1) * P],
                                                   xn(i, q)[:, c * P:(c + 1) * P], k.ident[:, :])
                last.then_inc(k.ln_turned, 1)

        @block.scalar
        def _(act):
            if first:
                act.sem_inc(k.ln_stored, 1)
            for i in range(turns):
                act.wait_ge(k.ln_turned, i + base + 2)
                nc.scalar.copy(k.xnT[:, :, i * Q * P:(i + 1) * Q * P], k.ps[0][:, 0:DC, :]).then_inc(k.ln_stored, 1)


class AttentionSemaphores:

    def __init__(self, k):
        self.xb_ready = k.sems("xb_ready")
        self.projected = k.sems("projected")
        self.v_kept = k.sems("v_kept")
        self.projected_sq = k.sems("projected_sq")
        self.rotated = k.sems("rotated")
        self.summed = k.sems("summed")
        self.sq_done = k.sems("sq_done")
        self.rms_ready = k.sems("rms_ready")
        self.turned_in = k.sems("turned_in")
        self.qk_turned = k.sems("qk_turned")
        self.qk_kept = k.sems("qk_kept")
        self.scored = k.sems("scored")
        self.max_ready = k.sems("max_ready")
        self.exp_done = k.sems("exp_done")
        self.probs_ready = k.sems("probs_ready")
        self.probs_turned = k.sems("probs_turned")
        self.probs_kept_a = k.sems("probs_kept_a")
        self.probs_kept_d = k.sems("probs_kept_d")
        self.mixed = k.sems("mixed")
        self.mix_kept = k.sems("mix_kept")
        self.out_ready = k.sems("out_ready")
        self.out_added = k.sems("out_added")


class AttentionWeights:

    def __init__(self, k, names, st):
        self.loaded = k.sem("at_loaded")
        self.wq = k.sb(f"at{k.attn_calls}_wq", [P, DC, H * HD], F32, st)
        self.wkv = k.sb(f"at{k.attn_calls}_wkv", [P, DC, KVH * 2 * HD], F32, st)
        self.wo = k.sb(f"at{k.attn_calls}_wo", [P, H, D], F32, st)
        self.loads = 3
        with k.nc.Block() as block:

            @block.sync
            def _(sp):
                sp.dma_start(self.wq[:, :, :], k.ins[names[0]].rearrange("(c p) n -> p c n", p=P)).then_inc(self.loaded, 16)
                sp.dma_start(self.wkv[:, :, :], k.ins[names[1]].rearrange("(c p) n -> p c n", p=P)).then_inc(self.loaded, 16)
                sp.dma_start(self.wo[:, :, :], k.ins[names[2]].rearrange("(h p) n -> p h n", p=P)).then_inc(self.loaded, 16)


def attention(k, weights, rope, ctx):
    nc = k.nc
    cross = ctx is not None
    scale = float(HD) ** -0.5
    KT = TB + 1 if cross else TB
    NK = S + (CTX if cross else 0)
    krows = [P] * TB + [CTX]
    s = AttentionSemaphores(k)
    chains = k.sems("at_chain")
    wq, wkv, wo = weights.wq, weights.wkv, weights.wo
    with ExitStack() as st:
        def sb(name, shape, dt=F32):
            return k.sb(f"at{k.attn_calls}_{name}", shape, dt, st)

        xb = [sb(f"xb{h}", [P, DC, NK]) for h in range(2)]
        t1 = [sb(f"t1{h}", [P, KT, G + 1, HD]) for h in range(2)]
        t2 = [sb(f"t2{h}", [P, KT, G + 1, HD]) for h in range(2)]
        qT = [sb(f"qT{h}", [P, G, S]) for h in range(2)]
        kT = [sb(f"kT{h}", [P, NK]) for h in range(2)]
        v = [sb(f"v{h}", [P, KT, HD]) for h in range(2)]
        mx = [sb(f"mx{h}", [P, 4]) for h in range(2)]
        nb = [sb(f"nb{h}", [P, 4]) for h in range(2)]
        den = [sb(f"den{h}", [P, 4]) for h in range(2)]
        rden = [sb(f"rden{h}", [P, 4]) for h in range(2)]
        probs = [sb(f"probs{h}", [P, 4, NK]) for h in range(2)]
        shared = [sb(f"shared{h}", [P, max(2 * KT * S, KT * (G + 1) * HD)]) for h in range(2)]
        pT = [b[:, 0:2 * KT * S].rearrange("p (a m s) -> p a m s", a=2, s=S) for b in shared]
        sqs = [b[:, 0:KT * (G + 1) * HD].rearrange("p (t g d) -> p t g d", t=KT, g=G + 1) for b in shared]
        oT = [sb(f"oT{h}", [P, G, S]) for h in range(2)]
        if cross:
            ss = [sb(f"ss{h}", [P, KT, G + 1]) for h in range(2)]
            rs = [sb(f"rs{h}", [P, KT, G + 1]) for h in range(2)]
            esc = [sb(f"esc{h}", [P, TB, G]) for h in range(2)]

        def q_ps(h):
            return k.ps[h][:, 0:TB, :].rearrange("p t (g d) -> p t g d", g=G)

        def kv_ps(h, part):
            return k.ps[h][:, 2, :].rearrange("p (t s d) -> p t s d", t=TB, s=2)[:, :, part, :]

        def ckv_ps(h, part):
            return k.ps[h][0:CTX, 3, part * HD:(part + 1) * HD]

        def slot(h, m):
            return k.ps[h][:, m // 2, (m % 2) * S:(m % 2) * S + S]

        pieces = (0, 1, 2) if cross else (0, 2)
        UNITS = KVH * B // 2
        HB = B // 2
        early = 1 if cross else 0

        def group(u):
            return u // HB

        def turn(u):
            return u % HB

        def schedule(eng, stage):
            stage(0, 0, None)
            stage(1, 0, 0)
            stage(0, 1, 0)
            stage(1, 1, 1)
            with eng.Fori(2, UNITS) as i:
                stage(0, i, i - 1)
                stage(1, i, i)
            stage(0, None, UNITS - 1)

        def wait_before(eng, sem, value):
            if not isinstance(value, int) or value > 0:
                eng.wait_ge(sem, value)

        with nc.Block() as block:

            @block.gpsimd
            def _(pool):

                def take_tokens(h, u):
                    wait_before(pool, s.projected[h], u * 3)
                    xc = nc.gpsimd.tensor_copy(xb[h][:, :, 0:S], k.xnT[:, :, ds(turn(u) * (2 * S) + h * S, S)])
                    if cross:
                        xc = nc.gpsimd.tensor_copy(xb[h][:, :, S:NK], ctx.ctxT[:, :, ds(turn(u) * (2 * CTX) + h * CTX, CTX)])
                    xc.then_inc(s.xb_ready[h], 1)

                def invert_rms(h, u):
                    pool.wait_ge(s.sq_done[h], u + 1)
                    nc.gpsimd.tensor_tensor(rs[h][:, :, :], ss[h][:, :, :],
                                            k.mhalf[:, 0:KT * (G + 1)].rearrange("p (t g) -> p t g", t=KT), ALU.pow)\
                        .then_inc(s.rms_ready[h], 1)

                def stage(h, front, back):
                    if front is not None:
                        take_tokens(h, front)
                        if cross:
                            invert_rms(h, front)

                if cross:
                    for h in range(2):
                        nc.gpsimd.memset(ss[h][:, :, :], 1.0)
                schedule(pool, stage)

            @block.tensor
            def _(pe):
                pe.wait_ge(weights.loaded, 16 * weights.loads)

                def project_q(h, u, t):
                    if t == 0:
                        pe.wait_ge(s.xb_ready[h], u + 1)
                        wait_before(pe, s.out_added[h], u)
                    for c in range(DC):
                        last = nc.tensor.matmul(k.ps[h][:, t, :], xb[h][:, c, t * P:(t + 1) * P],
                                                wq[:, c, ds(group(u) * (G * HD), G * HD)], start=c == 0, stop=c == DC - 1)
                    last.then_inc(s.projected[h], 1)

                def project_kv(h, u, tiles):
                    for t in tiles:
                        o = k.ps[h][0:krows[t], 2 + t // 2, (t % 2) * 2 * HD:(t % 2 + 1) * 2 * HD]
                        for c in range(DC):
                            last = nc.tensor.matmul(o, xb[h][:, c, t * P:t * P + krows[t]],
                                                    wkv[:, c, ds(group(u) * (2 * HD), 2 * HD)],
                                                    start=c == 0, stop=c == DC - 1)
                    if t == KT - 1:
                        last.then_inc(s.projected[h], 1)

                def turn_qk(h, u):
                    pe.wait_ge(s.turned_in[h] if cross else s.summed[h], u + 1)
                    pe.wait_ge(s.v_kept[h], u + 1)
                    for hh in range(G):
                        for t in range(TB):
                            nc.tensor.transpose(slot(h, hh)[:, t * P:(t + 1) * P], t1[h][:, t, hh, :], k.ident[:, :])
                    for t in range(KT):
                        r = krows[t]
                        last = nc.tensor.transpose(k.ps[h][:, 2, t * P:t * P + r], t1[h][0:r, t, G, :],
                                                   k.ident[0:r, 0:r])
                    last.then_inc(s.qk_turned[h], 1)

                def score(h, u, r):
                    if r == 0:
                        pe.wait_ge(s.qk_kept[h], u + 1)
                    elif r > 1:
                        pe.wait_ge(s.mix_kept[h], u * G + (r - 1))
                    for t in range(TB):
                        nk = NK if cross else (t + 1) * P
                        o = k.ps[h][:, (r % 2) * TB + t, :]
                        last = nc.tensor.matmul(o[:, 0:nk], qT[h][:, r, t * P:(t + 1) * P],
                                                kT[h][:, 0:nk], start=True, stop=cross)
                        if not cross:
                            last = nc.tensor.matmul(o[:, t * P:nk], k.identb[:, :],
                                                    k.causb[:, :], start=False, stop=True)
                    last.then_inc(s.scored[h], 1)

                def turn_probs(h, u, r):
                    pe.wait_ge(s.probs_ready[h], u * G + (r + 1))
                    for j in range(KT):
                        w = krows[j]
                        for t in range(TB):
                            if cross or j <= t:
                                last = nc.tensor.transpose(slot(h, (r % 2) * 4 + pieces[j])[0:w, t * P:(t + 1) * P],
                                                           probs[h][:, (r % 2) * TB + t, j * P:j * P + w], k.ident[:, :])
                    last.then_inc(s.probs_turned[h], 1)

                def mix(h, u, r):
                    pe.wait_ge(s.probs_kept_a[h], u * G + (r + 1))
                    pe.wait_ge(s.probs_kept_d[h], u * G + (r + 1))
                    for j in range(KT):
                        w = krows[j]
                        c0 = 0 if cross else j * P
                        last = nc.tensor.matmul(slot(h, (r % 2) * 4 + 3)[:, c0:S], v[h][0:w, j, :],
                                                pT[h][0:w, r % 2, j, c0:S], start=j == 0, stop=j == KT - 1)
                    last.then_inc(s.mixed[h], 1)

                def give(h, u):
                    pe.wait_ge(s.mix_kept[h], u * G + G)
                    for t in range(TB):
                        for hh in range(G):
                            last = nc.tensor.matmul(slot(h, t), oT[h][:, hh, t * P:(t + 1) * P],
                                                    wo[:, ds(group(u) * G + hh, 1), :], start=hh == 0, stop=hh == G - 1)
                    last.then_inc(s.out_ready[h], 1)

                def stage(h, front, back):
                    g = 1 - h
                    if front is not None and cross:
                        project_q(h, front, 0)
                    if back is not None:
                        score(g, back, 0)
                        score(g, back, 1)
                    if front is not None:
                        if not cross:
                            project_q(h, front, 0)
                        project_q(h, front, 1)
                        if early:
                            project_kv(h, front, range(early))
                    if back is not None:
                        turn_probs(g, back, 0)
                        turn_probs(g, back, 1)
                        mix(g, back, 0)
                        mix(g, back, 1)
                        score(g, back, 2)
                        score(g, back, 3)
                    if front is not None:
                        project_kv(h, front, range(early, KT))
                    if back is not None:
                        turn_probs(g, back, 2)
                        turn_probs(g, back, 3)
                        mix(g, back, 2)
                        mix(g, back, 3)
                    if back is not None and cross:
                        give(g, back)
                    if front is not None:
                        turn_qk(h, front)
                    if back is not None and not cross:
                        give(g, back)

                schedule(pe, stage)

            @block.vector
            def _(dve):
                def link(h, u, name, ins_):
                    number = names.index(name)
                    ins_.then_inc(chains[h], 1)
                    dve.wait_ge(chains[h], u * len(names) + (number + 1))

                names = ["max0", "max1", "inv0", "inv1", "max2", "max3", "inv2", "inv3"]
                if cross:
                    names = ["sums"] + names

                def rotate(h, u, part):
                    dve.wait_ge(s.projected[h], u * 3 + (part + 1))
                    cq, sq = rope.q(turn(u), h)
                    ck, sk = rope.k(turn(u), h)
                    q, kk = q_ps(h), kv_ps(h, 0)

                    def each(o1, o2, x, c, sn):
                        nc.vector.tensor_tensor(o1, x, c, ALU.mult)
                        nc.vector.tensor_tensor(o2[..., 0:HALF], x[..., HALF:HD], sn[..., 0:HALF], ALU.mult)
                        return nc.vector.tensor_tensor(o2[..., HALF:HD], x[..., 0:HALF], sn[..., HALF:HD], ALU.mult)

                    if part < TB:
                        t = part
                        each(t1[h][:, t, 0:G, :], t2[h][:, t, 0:G, :], q[:, t],
                             cq[:, t:t + 1, :].to_broadcast([P, G, HD]), sq[:, t:t + 1, :].to_broadcast([P, G, HD]))
                        return
                    last = each(t1[h][:, 0:TB, G, :], t2[h][:, 0:TB, G, :], kk, ck, sk)
                    if cross:
                        cc, sc = rope.c(turn(u), h)
                        last = each(t1[h][0:CTX, TB, G, :], t2[h][0:CTX, TB, G, :], ckv_ps(h, 0), cc, sc)
                    last.then_inc(s.rotated[h], 1)

                def add_halves(h, u):
                    dve.wait_ge(s.rotated[h], u + 1)
                    ad = nc.vector.tensor_tensor(t1[h][:, 0:TB], t1[h][:, 0:TB], t2[h][:, 0:TB], ALU.add)
                    if cross:
                        ad = nc.vector.tensor_tensor(t1[h][0:CTX, TB, G, :], t1[h][0:CTX, TB, G, :],
                                                     t2[h][0:CTX, TB, G, :], ALU.add)
                    ad.then_inc(s.summed[h], 1)

                def rms(h, u):
                    dve.wait_ge(s.projected_sq[h], u + 1)
                    sq = sqs[h]
                    nc.vector.tensor_reduce(ss[h][:, 0:TB, :], sq[:, 0:TB], AX_X, ALU.add)
                    link(h, u, "sums", nc.vector.tensor_reduce(ss[h][0:CTX, TB, G:G + 1], sq[0:CTX, TB, G:G + 1, :], AX_X, ALU.add))
                    nc.vector.tensor_scalar(ss[h][:, 0:TB, :], ss[h][:, 0:TB, :], 1.0 / HD, 1e-6, ALU.mult, ALU.add)
                    nc.vector.tensor_scalar(ss[h][0:CTX, TB, G:G + 1], ss[h][0:CTX, TB, G:G + 1], 1.0 / HD, 1e-6,
                                            ALU.mult, ALU.add).then_inc(s.sq_done[h], 1)

                def rms_keys(h, u):
                    dve.wait_ge(s.rms_ready[h], u + 1)
                    nc.vector.tensor_scalar(esc[h][:, :, :], rs[h][:, 0:TB, 0:G], scale, None, ALU.mult)
                    dve.wait_ge(s.summed[h], u + 1)
                    for t in range(KT):
                        r = krows[t]
                        last = nc.vector.tensor_scalar(t1[h][0:r, t, G, :], t1[h][0:r, t, G, :],
                                                       rs[h][0:r, t, G:G + 1], None, ALU.mult)
                    last.then_inc(s.turned_in[h], 1)

                def row_max(h, u, r):
                    dve.wait_ge(s.scored[h], u * G + (r + 1))
                    b = (r % 2) * TB
                    if cross:
                        link(h, u, f"max{r}", nc.vector.tensor_reduce(mx[h][:, b:b + TB], k.ps[h][:, b:b + TB, 0:NK], AX_X, ALU.max))
                        nc.vector.scalar_tensor_tensor(nb[h][:, b:b + TB], mx[h][:, b:b + TB], -1.0,
                                                       esc[h][:, :, r], ALU.mult, ALU.mult).then_inc(s.max_ready[h], 1)
                    else:
                        for t in range(TB):
                            last = nc.vector.tensor_reduce(mx[h][:, b + t:b + t + 1], k.ps[h][:, b + t, 0:(t + 1) * P], AX_X, ALU.max)
                        link(h, u, f"max{r}", last)
                        nc.vector.tensor_scalar(nb[h][:, b:b + TB], mx[h][:, b:b + TB], -scale, None, ALU.mult)\
                            .then_inc(s.max_ready[h], 1)

                def norm_probs(h, u, r):
                    dve.wait_ge(s.exp_done[h], u * G + (r + 1))
                    b = (r % 2) * TB
                    link(h, u, f"inv{r}", nc.vector.reciprocal(rden[h][:, b:b + TB], den[h][:, b:b + TB]))
                    for t in range(TB):
                        nk = NK if cross else (t + 1) * P
                        last = nc.vector.tensor_scalar(probs[h][:, b + t, 0:nk], probs[h][:, b + t, 0:nk],
                                                       rden[h][:, b + t:b + t + 1], None, ALU.mult)
                    last.then_inc(s.probs_ready[h], 1)

                def keep_probs(h, u, r):
                    dve.wait_ge(s.probs_turned[h], u * G + (r + 1))
                    piece = slot(h, (r % 2) * 4 + 2)
                    if cross:
                        last = nc.vector.tensor_copy(pT[h][0:CTX, r % 2, TB, :], piece[0:CTX, :])
                    else:
                        last = nc.vector.tensor_copy(pT[h][:, r % 2, 1, P:S], piece[:, P:S])
                    last.then_inc(s.probs_kept_d[h], 1)

                def add_out(h, u):
                    dve.wait_ge(s.out_ready[h], u + 1)
                    xt = k.x[:, ds(turn(u) * (2 * TB) + h * TB, TB), :]
                    nc.vector.tensor_tensor(xt, xt, k.ps[h][:, 0, :].rearrange("p (t d) -> p t d", t=TB),
                                            ALU.add).then_inc(s.out_added[h], 1)

                def stage(h, front, back):
                    g = 1 - h
                    if back is not None:
                        row_max(g, back, 0)
                        row_max(g, back, 1)
                        norm_probs(g, back, 0)
                        norm_probs(g, back, 1)
                        keep_probs(g, back, 0)
                        keep_probs(g, back, 1)
                    if front is not None:
                        rotate(h, front, 0)
                        rotate(h, front, 1)
                    if back is not None:
                        row_max(g, back, 2)
                        row_max(g, back, 3)
                        norm_probs(g, back, 2)
                    if front is not None:
                        rotate(h, front, TB)
                    if back is not None:
                        norm_probs(g, back, 3)
                        keep_probs(g, back, 2)
                        keep_probs(g, back, 3)
                    if front is not None and cross:
                        rms(h, front)
                    if front is not None:
                        add_halves(h, front)
                    if front is not None and cross:
                        rms_keys(h, front)
                    if back is not None:
                        add_out(g, back)

                schedule(dve, stage)

            @block.scalar
            def _(act):

                def keep_v(h, u):
                    act.wait_ge(s.rotated[h], u + 1)
                    if cross:
                        nc.scalar.activation(sqs[h][:, 0:TB, 0:G, :], q_ps(h), ACT.Square)
                        nc.scalar.activation(sqs[h][:, 0:TB, G, :], kv_ps(h, 0), ACT.Square)
                        nc.scalar.activation(sqs[h][0:CTX, TB, G, :], ckv_ps(h, 0), ACT.Square)\
                            .then_inc(s.projected_sq[h], 1)
                        nc.scalar.copy(v[h][0:CTX, TB, :], ckv_ps(h, 1))
                    nc.scalar.copy(v[h][:, 0:TB, :], kv_ps(h, 1)).then_inc(s.v_kept[h], 1)

                def keep_qk(h, u):
                    act.wait_ge(s.qk_turned[h], u + 1)
                    nc.scalar.copy(qT[h][:, :, :], k.ps[h][:, 0:2, :].rearrange("p a (b s) -> p (a b) s", b=2))
                    nc.scalar.copy(kT[h][:, :], k.ps[h][:, 2, 0:NK]).then_inc(s.qk_kept[h], 1)

                def exps(h, u, r):
                    act.wait_ge(s.max_ready[h], u * G + (r + 1))
                    for t in range(TB):
                        m = (r % 2) * TB + t
                        nk = NK if cross else (t + 1) * P
                        sc = esc[h][:, t, r:r + 1] if cross else scale
                        last = nc.scalar.activation(probs[h][:, m, 0:nk], k.ps[h][:, m, 0:nk], ACT.Exp,
                                                    bias=nb[h][:, m:m + 1], scale=sc, accum_out=den[h][:, m:m + 1])
                    last.then_inc(s.exp_done[h], 1)

                def keep_probs(h, u, r):
                    act.wait_ge(s.probs_turned[h], u * G + (r + 1))
                    if cross:
                        last = nc.scalar.copy(pT[h][:, r % 2, 0:TB, :],
                                              k.ps[h][:, (r % 2) * 2, :].rearrange("p (a s) -> p a s", a=TB))
                    else:
                        last = nc.scalar.copy(pT[h][:, r % 2, 0, :], slot(h, (r % 2) * 4))
                    last.then_inc(s.probs_kept_a[h], 1)

                def keep_mix(h, u, r):
                    act.wait_ge(s.mixed[h], u * G + (r + 1))
                    nc.scalar.copy(oT[h][:, r, :], slot(h, (r % 2) * 4 + 3)).then_inc(s.mix_kept[h], 1)

                def stage(h, front, back):
                    g = 1 - h
                    if back is not None:
                        exps(g, back, 0)
                        exps(g, back, 1)
                        keep_probs(g, back, 0)
                        keep_probs(g, back, 1)
                        keep_mix(g, back, 0)
                        keep_mix(g, back, 1)
                        exps(g, back, 2)
                        exps(g, back, 3)
                        keep_probs(g, back, 2)
                    if front is not None:
                        keep_v(h, front)
                    if back is not None:
                        keep_probs(g, back, 3)
                        keep_mix(g, back, 2)
                        keep_mix(g, back, 3)
                    if front is not None:
                        keep_qk(h, front)

                schedule(act, stage)

    k.attn_calls += 1




TOPK_SETS = 2
E0, TOPK0, I0 = 16, 4, 224
IC = I0 // 2


def set_attention(k):
    nc, ins = k.nc, k.ins
    scale = float(D) ** -0.5
    turns = B // 2
    loaded, chain = k.sem("set_loaded"), k.sem("set_chain")
    q_ready, q_kept = k.sems("set_q_ready"), k.sems("set_q_kept")
    scored, gap_ready, gap_exp = k.sems("set_scored"), k.sems("set_gap_ready"), k.sems("set_gap_exp")
    w_ready, w_turned, w_kept = k.sems("set_w_ready"), k.sems("set_w_turned"), k.sems("set_w_kept")
    mixed, added = k.sems("set_mixed"), k.sems("set_added")
    with ExitStack() as st:
        def sb(name, shape, dt=F32):
            return k.sb(f"set_{name}", shape, dt, st)

        wq, bq, desc = sb("wq", [P, DC, D]), sb("bq", [P, DC]), sb("desc", [P, DC, CTX])
        rows = sb("rows", [CTX, B, D])
        iota = sb("iota", [P, CTX])
        tok_i, tok = sb("tok_i", [P, TB, 4], I32), sb("tok", [P, TB, 4])
        mask = sb("mask", [P, TB, CTX])
        qT = [sb(f"qT{h}", [P, DC, S]) for h in range(2)]
        sc = [sb(f"sc{h}", [P, TB, CTX]) for h in range(2)]
        best = [sb(f"best{h}", [P, TB, 8]) for h in range(2)]
        at = [sb(f"at{h}", [P, TB, 8], U32) for h in range(2)]
        atf = [sb(f"atf{h}", [P, TB, 8]) for h in range(2)]
        gap = [sb(f"gap{h}", [P, TB]) for h in range(2)]
        w2 = [sb(f"w2{h}", [P, TB]) for h in range(2)]
        w1 = [sb(f"w1{h}", [P, TB]) for h in range(2)]
        wa = [sb(f"wa{h}", [P, TB, CTX]) for h in range(2)]
        wb = [sb(f"wb{h}", [P, TB, CTX]) for h in range(2)]
        wT = [sb(f"wT{h}", [CTX, S]) for h in range(2)]
        with nc.Block() as block:

            @block.sync
            def _(sp):
                sp.dma_start(wq[:, :, :], ins["w0xq"].rearrange("(c p) n -> p c n", p=P)).then_inc(loaded, 16)
                sp.dma_start(bq[:, :], ins["w0xb"]).then_inc(loaded, 16)
                sp.dma_start(desc[:, :, :], ins["w0xd"].rearrange("(c p) n -> p c n", p=P)).then_inc(loaded, 16)
                sp.dma_start(rows[:, :, :], ins["ctx"].rearrange("b n d -> n b d")).then_inc(loaded, 16)
                sp.dma_start(iota[:, :], ins["c_iota"][:, 0:CTX]).then_inc(loaded, 16)
                sp.dma_start(tok_i[:, :, :], ins["sets"].rearrange("(t p) k -> p t k", p=P)).then_inc(loaded, 16)

            @block.tensor
            def _(pe):
                pe.wait_ge(loaded, 96)
                for n in range(1, turns + 1):
                    for h in range(2):
                        b = 2 * (n - 1) + h
                        if n > 1:
                            pe.wait_ge(added[h], n - 1)
                        for e in range(DC):
                            for c in range(DC):
                                last = nc.tensor.matmul(k.ps[h][:, 0, e * S:(e + 1) * S], wq[:, c, e * P:(e + 1) * P],
                                                        k.xnT[:, c, b * S:(b + 1) * S], start=c == 0, stop=c == DC - 1)
                        last.then_inc(q_ready[h], 1)
                    for h in range(2):
                        pe.wait_ge(q_kept[h], n)
                        for t in range(TB):
                            for e in range(DC):
                                last = nc.tensor.matmul(k.ps[h][:, 1, t * CTX:(t + 1) * CTX], qT[h][:, e, t * P:(t + 1) * P],
                                                        desc[:, e, :], start=e == 0, stop=e == DC - 1)
                        last.then_inc(scored[h], 1)
                    for h in range(2):
                        pe.wait_ge(w_ready[h], n)
                        for t in range(TB):
                            last = nc.tensor.transpose(k.ps[h][0:CTX, 2, t * P:(t + 1) * P], wa[h][:, t, :], k.ident[:, :])
                        last.then_inc(w_turned[h], 1)
                    for h in range(2):
                        b = 2 * (n - 1) + h
                        pe.wait_ge(w_kept[h], n)
                        for t in range(TB):
                            last = nc.tensor.matmul(k.ps[h][:, 3, t * D:(t + 1) * D], wT[h][:, t * P:(t + 1) * P],
                                                    rows[:, b, :], start=True, stop=True)
                        last.then_inc(mixed[h], 1)

            @block.scalar
            def _(act):
                for n in range(1, turns + 1):
                    for h in range(2):
                        act.wait_ge(q_ready[h], n)
                        for e in range(DC):
                            last = nc.scalar.activation(qT[h][:, e, :], k.ps[h][:, 0, e * S:(e + 1) * S], ACT.Identity,
                                                        bias=bq[:, e:e + 1], scale=1.0)
                        last.then_inc(q_kept[h], 1)
                    for h in range(2):
                        act.wait_ge(gap_ready[h], n)
                        nc.scalar.activation(w2[h][:, :], gap[h][:, :], ACT.Exp).then_inc(gap_exp[h], 1)
                    for h in range(2):
                        act.wait_ge(w_turned[h], n)
                        nc.scalar.copy(wT[h][:, :], k.ps[h][0:CTX, 2, 0:S]).then_inc(w_kept[h], 1)

            @block.vector
            def _(dve):
                ch = Chain(dve, chain, 0)
                dve.wait_ge(loaded, 96)
                ch.link(nc.vector.tensor_copy(tok[:, :, :], tok_i[:, :, :]))
                for t in range(TB):
                    ch.link(nc.vector.tensor_scalar(mask[:, t, :], iota[:, :], tok[:, t, 0:1], None, ALU.is_equal))
                    for j in range(1, 4):
                        ch.link(nc.vector.scalar_tensor_tensor(mask[:, t, :], iota[:, :], tok[:, t, j:j + 1], mask[:, t, :],
                                                               ALU.is_equal, ALU.add))
                ch.link(nc.vector.tensor_scalar(mask[:, :, :], mask[:, :, :], 0.5, NEG, ALU.is_lt, ALU.mult))
                for n in range(1, turns + 1):
                    for h in range(2):
                        dve.wait_ge(scored[h], n)
                        ch.link(nc.vector.scalar_tensor_tensor(
                            sc[h][:, :, :], k.ps[h][:, 1, 0:TB * CTX].rearrange("p (t n) -> p t n", t=TB), scale,
                            mask[:, :, :], ALU.mult, ALU.add))
                        for t in range(TB):
                            last = nc.vector.max(best[h][:, t, :], sc[h][:, t, :])
                        ch.link(last)
                        for t in range(TB):
                            last = nc.vector.max_index(at[h][:, t, :], best[h][:, t, :], sc[h][:, t, :])
                        ch.link(last)
                        nc.vector.tensor_copy(atf[h][:, :, :], at[h][:, :, :])
                        nc.vector.tensor_tensor(gap[h][:, :], best[h][:, :, 1], best[h][:, :, 0], ALU.subtract)\
                            .then_inc(gap_ready[h], 1)
                    for h in range(2):
                        dve.wait_ge(gap_exp[h], n)
                        ch.link(nc.vector.tensor_scalar(w1[h][:, :], w2[h][:, :], 1.0, None, ALU.add))
                        ch.link(nc.vector.reciprocal(w1[h][:, :], w1[h][:, :]))
                        ch.link(nc.vector.tensor_tensor(w2[h][:, :], w2[h][:, :], w1[h][:, :], ALU.mult))
                        for t in range(TB):
                            nc.vector.tensor_scalar(wa[h][:, t, :], iota[:, :], atf[h][:, t, 0:1], w1[h][:, t:t + 1],
                                                    ALU.is_equal, ALU.mult)
                            last = nc.vector.tensor_scalar(wb[h][:, t, :], iota[:, :], atf[h][:, t, 1:2], w2[h][:, t:t + 1],
                                                           ALU.is_equal, ALU.mult)
                        ch.link(last)
                        nc.vector.tensor_tensor(wa[h][:, :, :], wa[h][:, :, :], wb[h][:, :, :], ALU.add).then_inc(w_ready[h], 1)
                    for h in range(2):
                        b = 2 * (n - 1) + h
                        dve.wait_ge(mixed[h], n)
                        xt = k.x[:, b * TB:(b + 1) * TB, :]
                        nc.vector.tensor_tensor(xt, xt, k.ps[h][:, 3, :].rearrange("p (t d) -> p t d", t=TB),
                                                ALU.add).then_inc(added[h], 1)


def experts(k):
    nc, ins = k.nc, k.ins
    GT = 4
    groups = NT // GT
    loaded, chain = k.sem("moe_loaded"), k.sem("moe_chain")
    routed, shifted, exps_done, w_made = k.sem("moe_routed"), k.sem("moe_shifted"), k.sem("moe_exps"), k.sem("moe_w_made")
    w_loaded = [k.sem(f"moe_w_loaded{q}") for q in range(2)]
    up_ready, silu_done, act_ready = k.sems("moe_up_ready"), k.sems("moe_silu_done"), k.sems("moe_act_ready")
    down_ready, added = k.sems("moe_down_ready"), k.sems("moe_added")
    with ExitStack() as st:
        def sb(name, shape, dt=F32):
            return k.sb(f"moe_{name}", shape, dt, st)

        router, bias, iota = sb("router", [P, DC, E0]), sb("bias", [P, E0]), sb("iota", [P, E0])
        lg = sb("lg", [P, NT, E0])
        best, at, atf = sb("best", [P, NT, 8]), sb("at", [P, NT, 8], U32), sb("atf", [P, NT, 8])
        ex, tot, rtot = sb("ex", [P, NT, TOPK0]), sb("tot", [P, NT]), sb("rtot", [P, NT])
        w = sb("w", [P, NT, E0])
        eq = [sb(f"eq{j}", [P, NT, E0]) for j in range(TOPK0)]
        wgu = [[sb(f"wgu{q}{h}", [P, DC, 2 * I0]) for h in range(2)] for q in range(2)]
        wd = [[sb(f"wd{q}{h}", [IC, 2, D]) for h in range(2)] for q in range(2)]
        sg = [sb(f"sg{h}", [IC, 2, GT * P]) for h in range(2)]
        hT = [sb(f"hT{h}", [IC, 2, GT * P]) for h in range(2)]

        def load_expert(sp, q, h, e):
            sp.dma_start(wgu[q][h][:, :, :], ins["w0gu"][ds(e, 1)].rearrange("e (c p) n -> p (e c) n", p=P))\
                .then_inc(w_loaded[q], 16)
            sp.dma_start(wd[q][h][:, :, :], ins["w0d"][ds(e, 1)].rearrange("e (c p) n -> p (e c) n", p=IC))\
                .then_inc(w_loaded[q], 16)

        with nc.Block() as block:

            @block.sync
            def _(sp):
                sp.dma_start(router[:, :, :], ins["w0r"].rearrange("(c p) n -> p c n", p=P)).then_inc(loaded, 16)
                sp.dma_start(bias[:, :], ins["w0rb"].partition_broadcast(P)).then_inc(loaded, 16)
                sp.dma_start(iota[:, :], ins["c_iota"][:, 0:E0]).then_inc(loaded, 16)
                for q in range(2):
                    for h in range(2):
                        load_expert(sp, q, h, 2 * q + h)
                with sp.Fori(1, E0 // 4) as j:
                    for q in range(2):
                        for h in range(2):
                            sp.wait_ge(added[h], j * (2 * groups) + (q - 1) * groups + 1)
                            load_expert(sp, q, h, j * 4 + (2 * q + h))

            @block.tensor
            def _(pe):
                pe.wait_ge(loaded, 48)
                for i in range(NT):
                    for c in range(DC):
                        last = nc.tensor.matmul(k.ps[0][:, 0, i * E0:(i + 1) * E0], k.xnT[:, c, i * P:(i + 1) * P],
                                                router[:, c, :], start=c == 0, stop=c == DC - 1)
                last.then_inc(routed, 1)
                pe.wait_ge(shifted, 1)
                with pe.Fori(0, E0 // 4) as j:
                    for q in range(2):
                        with pe.Fori(0, groups) as g:
                            n = j * (2 * groups) + g + (q * groups + 1)
                            for h in range(2):
                                pe.wait_ge(w_loaded[q], (j + 1) * 64)
                                pe.wait_ge(added[h], n)
                                for m in range(4):
                                    for c in range(DC):
                                        last = nc.tensor.matmul(k.ps[h][0:IC, m, :], wgu[q][h][:, c, m * IC:(m + 1) * IC],
                                                                k.xnT[:, c, ds(g * (GT * P), GT * P)],
                                                                start=c == 0, stop=c == DC - 1)
                                last.then_inc(up_ready[h], 1)
                            for h in range(2):
                                pe.wait_ge(act_ready[h], n)
                                for t in range(GT):
                                    for c in range(2):
                                        last = nc.tensor.matmul(k.ps[h][:, t // 2, (t % 2) * D:(t % 2 + 1) * D],
                                                                hT[h][:, c, t * P:(t + 1) * P], wd[q][h][:, c, :],
                                                                start=c == 0, stop=c == 1)
                                last.then_inc(down_ready[h], 1)

            @block.scalar
            def _(act):
                act.wait_ge(shifted, 1)
                nc.scalar.activation(ex[:, :, :], ex[:, :, :], ACT.Exp).then_inc(exps_done, 1)
                with act.Fori(0, E0 // 4) as j:
                    for q in range(2):
                        with act.Fori(0, groups) as g:
                            n = j * (2 * groups) + g + (q * groups + 1)
                            for h in range(2):
                                act.wait_ge(up_ready[h], n)
                                nc.scalar.activation(sg[h][:, :, :], k.ps[h][0:IC, 0:2, :], ACT.Silu).then_inc(silu_done[h], 1)

            @block.vector
            def _(dve):
                for h in range(2):
                    dve.sem_inc(added[h], 1)
                ch = Chain(dve, chain, 0)
                dve.wait_ge(routed, 1)
                ch.link(nc.vector.tensor_tensor(lg[:, :, :], k.ps[0][:, 0, 0:NT * E0].rearrange("p (t e) -> p t e", e=E0),
                                                bias[:, :].unsqueeze(1).to_broadcast([P, NT, E0]), ALU.add))
                for i in range(NT):
                    last = nc.vector.max(best[:, i, :], lg[:, i, :])
                ch.link(last)
                for i in range(NT):
                    last = nc.vector.max_index(at[:, i, :], best[:, i, :], lg[:, i, :])
                ch.link(last)
                nc.vector.tensor_tensor(ex[:, :, :], best[:, :, 0:TOPK0],
                                        best[:, :, 0:1].to_broadcast([P, NT, TOPK0]), ALU.subtract).then_inc(shifted, 1)
                ch.link(nc.vector.tensor_copy(atf[:, :, :], at[:, :, :]))
                dve.wait_ge(exps_done, 1)
                ch.link(nc.vector.tensor_reduce(tot[:, :], ex[:, :, :], AX_X, ALU.add))
                ch.link(nc.vector.reciprocal(rtot[:, :], tot[:, :]))
                ch.link(nc.vector.tensor_tensor(ex[:, :, :], ex[:, :, :],
                                                rtot[:, :].unsqueeze(2).to_broadcast([P, NT, TOPK0]), ALU.mult))
                for j in range(TOPK0):
                    last = nc.vector.tensor_tensor(eq[j][:, :, :], iota[:, :].unsqueeze(1).to_broadcast([P, NT, E0]),
                                                   atf[:, :, j:j + 1].to_broadcast([P, NT, E0]), ALU.is_equal)
                ch.link(last)
                for j in range(TOPK0):
                    last = nc.vector.tensor_tensor(eq[j][:, :, :], eq[j][:, :, :],
                                                   ex[:, :, j:j + 1].to_broadcast([P, NT, E0]), ALU.mult)
                ch.link(last)
                nc.vector.tensor_tensor(eq[0][:, :, :], eq[0][:, :, :], eq[1][:, :, :], ALU.add)
                ch.link(nc.vector.tensor_tensor(eq[2][:, :, :], eq[2][:, :, :], eq[3][:, :, :], ALU.add))
                ch.link(nc.vector.tensor_tensor(w[:, :, :], eq[0][:, :, :], eq[2][:, :, :], ALU.add))
                with dve.Fori(0, E0 // 4) as j:
                    for q in range(2):
                        with dve.Fori(0, groups) as g:
                            n = j * (2 * groups) + g + (q * groups + 1)
                            for h in range(2):
                                dve.wait_ge(silu_done[h], n)
                                nc.vector.tensor_tensor(hT[h][:, :, :], sg[h][:, :, :], k.ps[h][0:IC, 2:4, :], ALU.mult)\
                                    .then_inc(act_ready[h], 1)
                            for h in range(2):
                                dve.wait_ge(down_ready[h], n)
                                if h == 1:
                                    dve.wait_ge(added[0], n + 1)
                                for t in range(GT):
                                    xt = k.x[:, ds(g * GT + t, 1), :].rearrange("p a d -> p (a d)")
                                    sc = w[:, ds(g * GT + t, 1), ds(j * 4 + (2 * q + h), 1)].rearrange("p a e -> p (a e)")
                                    last = nc.vector.scalar_tensor_tensor(xt, k.ps[h][:, t // 2, (t % 2) * D:(t % 2 + 1) * D],
                                                                          sc, xt, ALU.mult, ALU.add)
                                last.then_inc(added[h], 1)


HK, VE, KC = 16, 256, 4


def delta_attention(k):
    nc, ins = k.nc, k.ins
    loaded, made = k.sem("dl_loaded"), k.sem("dl_made")
    gates_ready, gates_abs, gates_exp, gates_log = k.sem("dl_gates"), k.sem("dl_gabs"), k.sem("dl_gexp"), k.sem("dl_glog")
    loga_ready, cum_ready, cum_kept, cum_turned = k.sem("dl_loga"), k.sem("dl_cum"), k.sem("dl_cum_kept"), k.sem("dl_cumT")
    rows_kept, rows_stored, chain0 = k.sem("dl_rows_kept"), k.sem("dl_rows_stored"), k.sem("dl_setup_chain")
    w_loaded = k.sems("dl_w_loaded")
    wo_loaded = k.sems("dl_wo_loaded")
    taps_loaded = k.sems("dl_taps_loaded")
    grow_loaded = k.sems("dl_grow_loaded")
    projected = k.sems("dl_projected")
    tapped = k.sems("dl_tapped")
    conv_part = k.sems("dl_conv_part")
    convolved = k.sems("dl_convolved")
    tanh_done = k.sems("dl_tanh_done")
    silu_done = k.sems("dl_silu_done")
    squared = k.sems("dl_squared")
    lengths = k.sems("dl_lengths")
    lengths_kept = k.sems("dl_len_kept")
    inverse_len = k.sems("dl_inv_len")
    c_part = k.sems("dl_c_part")
    scales_ready = k.sems("dl_scales")
    masked = k.sems("dl_masked")
    decayed = k.sems("dl_decayed")
    v_turned = k.sems("dl_v_turned")
    v_scaled = k.sems("dl_v_scaled")
    products = k.sems("dl_products")
    lp_ready = k.sems("dl_lp_ready")
    nt_part = k.sems("dl_nt_part")
    nt_ready = k.sems("dl_nt_ready")
    t_ready = k.sems("dl_t_ready")
    t_kept = k.sems("dl_t_kept")
    tt_ready = k.sems("dl_tt_ready")
    tt_kept = k.sems("dl_tt_kept")
    off_ready = k.sems("dl_off_ready")
    off_kept = k.sems("dl_off_kept")
    solved = k.sems("dl_solved")
    w_kept = k.sems("dl_w_kept")
    rest_kept = k.sems("dl_rest_kept")
    mixed = k.sems("dl_mixed")
    mix_kept = k.sems("dl_mix_kept")
    out_ready = k.sems("dl_out_ready")
    added = k.sems("dl_added")
    levels = [1 << i for i in range(1, 7)]
    NL = len(levels)
    scratch = nc.dram_tensor("decay_rows", (HK, T), F32, kind="Internal").ap()
    with ExitStack() as st:
        def sb(name, shape, dt=F32):
            return k.sb(f"dl_{name}", shape, dt, st)

        wab = sb("wab", [P, DC, 2 * HK])
        taps = [sb(f"taps{h}", [P, 4, KC + 1]) for h in range(2)]
        tri, ones = sb("tri", [P, P]), sb("ones", [P, P])
        negstrict, maskadd = sb("negstrict", [P, P]), sb("maskadd", [P, P])
        lvl, lvl1T = sb("lvl", [P, NL, P]), sb("lvl1T", [P, P])
        za, zabs = sb("za", [P, NT, HK]), sb("zabs", [P, NT, 2 * HK])
        loga, beta = sb("loga", [P, NT, HK]), sb("beta", [P, NT, HK])
        cum, negcum = sb("cum", [P, NT, HK]), sb("negcum", [P, NT, HK])
        rows = sb("rows", [HK, T])
        wkqv = [sb(f"wkqv{h}", [P, DC, 4 * P]) for h in range(2)]
        wo = [sb(f"wo{h}", [P, 2, D]) for h in range(2)]
        grow = [sb(f"grow{h}", [P, T]) for h in range(2)]
        y = [sb(f"y{h}", [P, 4, S]) for h in range(2)]
        e = [sb(f"e{h}", [P, 4, S]) for h in range(2)]
        z = [sb(f"z{h}", [P, 4, S]) for h in range(2)]
        sq = [sb(f"sq{h}", [P, 2, S]) for h in range(2)]
        n2 = [sb(f"n2{h}", [P, 4]) for h in range(2)]
        rn = [sb(f"rn{h}", [P, 4]) for h in range(2)]
        rq = [sb(f"rq{h}", [P, 2, TB]) for h in range(2)]
        nk = [sb(f"nk{h}", [P, TB]) for h in range(2)]
        cj = [sb(f"cj{h}", [P, TB]) for h in range(2)]
        gm = [sb(f"gm{h}", [P, 3 * P]) for h in range(2)]
        ng = [sb(f"ng{h}", [P, TB]) for h in range(2)]
        dec = [sb(f"dec{h}", [P, 3 * P]) for h in range(2)]
        vs = [sb(f"vs{h}", [P, TB, VE]) for h in range(2)]
        lp = [sb(f"lp{h}", [P, 2, 2 * S]) for h in range(2)]
        lp0 = [t[:, 0, :].rearrange("p (a s) -> p a s", a=2) for t in lp]
        lp1 = [t[:, 1, 0:S].rearrange("p (a s) -> p a s", a=2) for t in lp]
        ntm = [sb(f"ntm{h}", [P, 2, P]) for h in range(2)]
        nt = [sb(f"nt{h}", [P, 2, P]) for h in range(2)]
        tt = [sb(f"tt{h}", [P, 2, 2, P]) for h in range(2)]
        off = [sb(f"off{h}", [P, NL, 2, P]) for h in range(2)]
        wv = [sb(f"wv{h}", [P, 2, VE]) for h in range(2)]
        rest = [sb(f"rest{h}", [P, VE]) for h in range(2)]
        oT = [sb(f"oT{h}", [P, 2, S]) for h in range(2)]

        def halves(ap, b, second):
            return ap.rearrange("p (n a b) -> p n a b", a=2, b=b)[:, :, second, :]

        def load_w(sp, h, hd):
            sp.dma_start(wkqv[h][:, :, :], ins["w1kqv"][ds(hd, 1)].rearrange("e (c p) n -> p (e c) n", p=P))\
                .then_inc(w_loaded[h], 16)

        def load_taps(sp, h, hd):
            sp.dma_start(taps[h][:, :, :], ins["w1t"][ds(hd, 1)].rearrange("e p m n -> p (e m) n")).then_inc(taps_loaded[h], 16)

        def load_grow(sp, h, hd):
            sp.dma_start(grow[h][:, :], scratch[ds(hd, 1), :].rearrange("e t -> (e t)").partition_broadcast(P))\
                .then_inc(grow_loaded[h], 16)

        def load_wo(sp, h, hd):
            sp.dma_start(wo[h][:, :, :], ins["w1o"][ds(hd, 1)].rearrange("e (c p) n -> p (e c) n", p=P))\
                .then_inc(wo_loaded[h], 16)

        UNITS = HK // 2 * B

        def batch(u):
            return u % B

        def pair(u):
            return u // B

        def schedule(eng, stage):
            stage(1, None, None, 0, 0)
            stage(0, 0, None, 0, 1)
            stage(1, 0, 0, 1, 1)
            stage(0, 1, 0, 1, 2)
            with eng.Fori(1, UNITS - 2) as i:
                stage(1, i, i, i + 1, i + 1)
                stage(0, i + 1, i, i + 1, i + 2)
            stage(1, UNITS - 2, UNITS - 2, UNITS - 1, UNITS - 1)
            stage(0, UNITS - 1, UNITS - 2, UNITS - 1, None)
            stage(1, UNITS - 1, UNITS - 1, None, None)
            stage(0, None, UNITS - 1, None, None)

        def wait_before(eng, sem, u):
            if not isinstance(u, int) or u > 0:
                eng.wait_ge(sem, u)

        with nc.Block() as block:

            @block.sync
            def _(sp):
                for dst, name in ((tri[:, :], "c_tri"), (ones[:, :], "c_ones"), (negstrict[:, :], "c_negstrict"), (maskadd[:, :], "c_maskadd"),
                                  (lvl[:, :, :], "c_levels"), (lvl1T[:, :], "c_level1T")):
                    sp.dma_start(dst, ins[name]).then_inc(loaded, 16)
                sp.dma_start(wab[:, :, :], ins["w1ab"].rearrange("(c p) n -> p c n", p=P)).then_inc(loaded, 16)
                for h in range(2):
                    load_w(sp, h, h)
                    load_taps(sp, h, h)
                    load_wo(sp, h, h)
                sp.wait_ge(rows_kept, 4)
                sp.dma_start(scratch, rows[:, :]).then_inc(rows_stored, 16)
                sp.wait_ge(rows_stored, 16)
                for h in range(2):
                    load_grow(sp, h, h)
                with sp.Fori(1, HK // 2) as j:
                    for h in range(2):
                        sp.wait_ge(projected[h], j * (2 * B))
                        load_w(sp, h, j * 2 + h)
                        sp.wait_ge(convolved[h], j * (2 * B))
                        load_taps(sp, h, j * 2 + h)
                        sp.wait_ge(masked[h], j * B)
                        load_grow(sp, h, j * 2 + h)
                    for h in range(2):
                        sp.wait_ge(out_ready[h], j * B)
                        load_wo(sp, h, j * 2 + h)

            @block.gpsimd
            def _(pool):
                for h in range(2):
                    for i in range(NL):
                        nc.gpsimd.tensor_copy(off[h][:, i, :, :], k.ident[:, :].unsqueeze(1).to_broadcast([P, 2, P]))
                pool.wait_ge(loaded, 16 * 7)
                pool.wait_ge(cum_kept, 1)

                def mask_decay(h, u):
                    pool.wait_ge(grow_loaded[h], (pair(u) + 1) * 16)
                    wait_before(pool, decayed[h], u)
                    for blk, c0 in ((0, 0), (1, S)):
                        nc.gpsimd.tensor_tensor(gm[h][:, c0:c0 + P], grow[h][:, ds(batch(u) * S + blk * P, P)],
                                                maskadd[:, :], ALU.add)
                    nc.gpsimd.tensor_copy(ng[h][:, :], negcum[:, ds(batch(u) * TB, TB), ds(pair(u) * 2 + h, 1)]
                                          .rearrange("p t a -> p (t a)"))
                    nc.gpsimd.tensor_copy(gm[h][:, P:S], grow[h][:, ds(batch(u) * S + P, P)]).then_inc(masked[h], 1)

                def invert_lengths(h, u):
                    pool.wait_ge(lengths_kept[h], u + 1)
                    nc.gpsimd.tensor_tensor(rn[h][:, :], n2[h][:, :], k.mhalf[:, 0:4], ALU.pow).then_inc(inverse_len[h], 1)

                def stage(h, grown, given, prepared, project):
                    g = 1 - h
                    if prepared is not None:
                        mask_decay(g, prepared)
                        invert_lengths(g, prepared)

                schedule(pool, stage)

            @block.tensor
            def _(pe):
                pe.wait_ge(loaded, 16 * 7)
                for i in range(NT):
                    for c in range(DC):
                        last = nc.tensor.matmul(k.ps[0][:, 0, i * 2 * HK:(i + 1) * 2 * HK], k.xnT[:, c, i * P:(i + 1) * P],
                                                wab[:, c, :], start=c == 0, stop=c == DC - 1)
                last.then_inc(gates_ready, 1)
                pe.wait_ge(loga_ready, 1)
                for i in range(NT):
                    o = k.ps[0][:, 1, i * HK:(i + 1) * HK]
                    last = nc.tensor.matmul(o, tri[:, :], loga[:, i, :], start=True, stop=i % TB == 0)
                    if i % TB:
                        last = nc.tensor.matmul(o, ones[:, :], loga[:, i - 1, :], start=False, stop=True)
                last.then_inc(cum_ready, 1)
                pe.wait_ge(cum_kept, 1)
                for i in range(NT):
                    last = nc.tensor.transpose(k.ps[1][0:HK, i // 4, (i % 4) * P:(i % 4 + 1) * P], cum[:, i, :], k.ident[:, :])
                last.then_inc(cum_turned, 1)

                def project_part(h, u, m):
                    if m == 0:
                        pe.wait_ge(w_loaded[h], (pair(u) + 1) * 16)
                        wait_before(pe, lp_ready[h], u)
                    if m == 2:
                        wait_before(pe, v_scaled[h], u)
                    for c in range(DC):
                        last = nc.tensor.matmul(k.ps[h][:, m // 2, (m % 2) * S:(m % 2 + 1) * S],
                                                wkqv[h][:, c, m * P:(m + 1) * P],
                                                k.xnT[:, c, ds(batch(u) * S, S)],
                                                start=c == 0, stop=c == DC - 1)
                    if m % 2:
                        last.then_inc(projected[h], 1)

                def products_of(h, u, blk):
                    if blk == 0:
                        pe.wait_ge(silu_done[h], u * 2 + 1)
                        pe.wait_ge(convolved[h], u * 2 + 2)
                    else:
                        pe.wait_ge(lengths_kept[h], u + 1)
                    last = nc.tensor.matmul(k.ps[h][:, blk, 0:2 * (S - blk * P)].rearrange("p (a s) -> p a s", a=2),
                                            z[h][:, 0, blk * P:(blk + 1) * P], z[h][:, 0:2, blk * P:S],
                                            start=True, stop=True)
                    if blk:
                        last.then_inc(products[h], 1)

                def turn_v(h, u):
                    pe.wait_ge(lp_ready[h], u + 1)
                    pe.wait_ge(silu_done[h], u * 2 + 2)
                    for t in range(TB):
                        for m in range(2):
                            last = nc.tensor.transpose(k.ps[h][:, 1, (2 * t + m) * P:(2 * t + m + 1) * P],
                                                       z[h][:, 2 + m, t * P:(t + 1) * P], k.ident[:, :])
                    last.then_inc(v_turned[h], 1)

                def lengths_of(h, u):
                    pe.wait_ge(squared[h], u + 1)
                    pe.wait_ge(convolved[h], u * 2 + 2)
                    for m in range(2):
                        for t in range(TB):
                            last = nc.tensor.matmul(k.ps[h][:, 1, S + m * TB + t:S + m * TB + t + 1],
                                                    sq[h][:, m, t * P:(t + 1) * P], ones[:, 0:1],
                                                    start=True, stop=True)
                    last.then_inc(lengths[h], 1)

                def turn_first(h, u):
                    pe.wait_ge(nt_ready[h], u + 1)
                    for blk in range(2):
                        last = nc.tensor.transpose(k.ps[h][:, 2, blk * P:(blk + 1) * P], tt[h][:, 1, blk, :],
                                                   k.ident[:, :])
                    last.then_inc(t_ready[h], 1)

                def grow_off(h, u, i):
                    pe.wait_ge(t_kept[h], u * NL + (i + 1))
                    for blk in range(2):
                        last = nc.tensor.matmul(k.ps[h][:, 2, blk * HALF:(blk + 1) * HALF], nt[h][:, blk, :],
                                                halves(tt[h][:, 0, blk, :], levels[i], 0), start=True, stop=True)
                    last.then_inc(off_ready[h], 1)

                def turn_t(h, u):
                    for blk in range(2):
                        last = nc.tensor.transpose(k.ps[h][:, 3, blk * P:(blk + 1) * P], tt[h][:, 0, blk, :], k.ident[:, :])
                    last.then_inc(tt_ready[h], 1)

                def grow_t(h, u, i):
                    pe.wait_ge(off_kept[h], u * NL + (i + 1))
                    if i > 0:
                        pe.wait_ge(tt_kept[h], u * NL + i)
                    if i < NL - 1:
                        for blk in range(2):
                            last = nc.tensor.matmul(k.ps[h][:, 2, S + blk * HALF:S + (blk + 1) * HALF], tt[h][:, 1, blk, :],
                                                    halves(off[h][:, i, blk, :], levels[i], 0), start=True, stop=True)
                        last.then_inc(t_ready[h], 1)
                    else:
                        for blk in range(2):
                            last = nc.tensor.matmul(k.ps[h][:, 3, blk * HALF:(blk + 1) * HALF], off[h][:, i, blk, :],
                                                    halves(tt[h][:, 1, blk, :], levels[i], 1), start=True, stop=True)
                        last.then_inc(tt_ready[h], 1)

                def solve_first(h, u):
                    pe.wait_ge(tt_kept[h], u * NL + NL)
                    nc.tensor.matmul(k.ps[h][:, 2, 0:VE], tt[h][:, 1, 0, :], vs[h][:, 0, :],
                                     start=True, stop=True).then_inc(solved[h], 1)

                def solve_cross(h, u):
                    pe.wait_ge(w_kept[h], u * 2 + 1)
                    nc.tensor.matmul(k.ps[h][:, 2, VE:2 * VE], lp0[h][:, 0, P:S], wv[h][:, 0, :],
                                     start=True, stop=True).then_inc(solved[h], 1)

                def solve_second(h, u):
                    pe.wait_ge(rest_kept[h], u + 1)
                    nc.tensor.matmul(k.ps[h][:, 3, 0:VE], tt[h][:, 1, 1, :], rest[h][:, :],
                                     start=True, stop=True).then_inc(solved[h], 1)

                def mix(h, u, m):
                    if m == 0:
                        pe.wait_ge(w_kept[h], u * 2 + 2)
                    nc.tensor.matmul(k.ps[h][:, 2, m * S:(m + 1) * S], wv[h][:, 0, m * P:(m + 1) * P],
                                     lp0[h][:, 1, :], start=True, stop=False)
                    last = nc.tensor.matmul(k.ps[h][:, 2, m * S + P:(m + 1) * S], wv[h][:, 1, m * P:(m + 1) * P],
                                            lp1[h][:, 1, :], start=False, stop=True)
                    if m:
                        last.then_inc(mixed[h], 1)

                def give(h, u, t):
                    if t == 0:
                        pe.wait_ge(wo_loaded[h], (pair(u) + 1) * 16)
                        pe.wait_ge(mix_kept[h], u + 1)
                    for m in range(2):
                        last = nc.tensor.matmul(k.ps[h][:, 3, t * D:(t + 1) * D], oT[h][:, m, t * P:(t + 1) * P],
                                                wo[h][:, m, :], start=m == 0, stop=m == 1)
                    if t:
                        last.then_inc(out_ready[h], 1)

                def stage(h, grown, given, prepared, project):
                    g = 1 - h
                    if grown is not None:
                        turn_first(h, grown)
                    if given is not None:
                        solve_first(g, given)
                    if project is not None:
                        project_part(h, project, 0)
                    for i in range(NL):
                        if grown is not None:
                            grow_off(h, grown, i)
                            if i == 1:
                                wait_before(pe, added[h], grown)
                            if i > 0:
                                turn_t(h, grown)
                        if project is not None and i < 3:
                            project_part(h, project, i + 1)
                        if prepared is not None and i == 3:
                            products_of(g, prepared, 0)
                        if given is not None and i == 4:
                            mix(g, given, 1)
                        if given is not None and i == 5:
                            give(g, given, 1)
                        if grown is not None:
                            grow_t(h, grown, i)
                        if given is not None and i < 2:
                            (solve_cross, solve_second)[i](g, given)
                        if given is not None and i == 2:
                            mix(g, given, 0)
                        if prepared is not None and i == 3:
                            lengths_of(g, prepared)
                        if prepared is not None and i == 4:
                            products_of(g, prepared, 1)
                        if given is not None and i == 4:
                            give(g, given, 0)
                        if prepared is not None and i == 5:
                            turn_v(g, prepared)

                pe.wait_ge(rows_kept, 4)
                for m in range(4):
                    project_part(0, 0, m)
                schedule(pe, stage)

            @block.scalar
            def _(act):
                act.wait_ge(gates_abs, 1)
                nc.scalar.activation(zabs[:, :, :], zabs[:, :, :], ACT.Exp, scale=-1.0).then_inc(gates_exp, 1)
                act.wait_ge(gates_exp, 1)
                nc.scalar.activation(loga[:, :, :], zabs[:, :, 0:HK], ACT.Ln, bias=1.0, scale=1.0).then_inc(gates_log, 1)
                act.wait_ge(cum_turned, 1)
                for i in range(4):
                    nc.scalar.copy(rows[:, i * 512:(i + 1) * 512], k.ps[1][0:HK, i, :]).then_inc(rows_kept, 1)

                def tap(h, u, part):
                    if part == 0:
                        act.wait_ge(taps_loaded[h], (pair(u) + 1) * 16)
                    act.wait_ge(projected[h], u * 2 + (part + 1))
                    for m in (2 * part, 2 * part + 1):
                        last = nc.scalar.activation(y[h][:, m, :], k.ps[h][:, m // 2, (m % 2) * S:(m % 2 + 1) * S],
                                                    ACT.Identity,
                                                    bias=taps[h][:, m, KC:KC + 1], scale=taps[h][:, m, KC - 1:KC])
                    last.then_inc(tapped[h], 1)

                def tanh_of(h, u, part):
                    act.wait_ge(convolved[h], u * 2 + (part + 1))
                    nc.scalar.activation(e[h][:, 2 * part:2 * part + 2, :], y[h][:, 2 * part:2 * part + 2, :], ACT.Tanh,
                                         scale=0.5).then_inc(tanh_done[h], 1)

                def square(h, u):
                    act.wait_ge(silu_done[h], u * 2 + 1)
                    nc.scalar.activation(sq[h][:, :, :], z[h][:, 0:2, :], ACT.Square).then_inc(squared[h], 1)

                def decay(h, u):
                    act.wait_ge(masked[h], u + 1)
                    for blk, (c0, w) in enumerate(((0, S), (S, P))):
                        last = nc.scalar.activation(dec[h][:, c0:c0 + w], gm[h][:, c0:c0 + w], ACT.Exp,
                                                    bias=ng[h][:, blk:blk + 1], scale=1.0)
                    last.then_inc(decayed[h], 1)

                def scale_v(h, u):
                    act.wait_ge(v_turned[h], u + 1)
                    act.wait_ge(scales_ready[h], u + 1)
                    for t in range(TB):
                        last = nc.scalar.activation(vs[h][:, t, :], k.ps[h][:, 1, t * VE:(t + 1) * VE], ACT.Copy,
                                                    scale=nk[h][:, t:t + 1])
                    last.then_inc(v_scaled[h], 1)

                def keep_tt(h, u, i):
                    act.wait_ge(tt_ready[h], u * NL + (i + 1))
                    if i < NL - 1:
                        nc.scalar.copy(tt[h][:, 1, :, :], k.ps[h][:, 3, 0:2 * P].rearrange("p (b s) -> p b s", b=2))\
                            .then_inc(tt_kept[h], 1)
                        return
                    nc.scalar.copy(halves(tt[h][:, 1, :, :].rearrange("p b s -> p (b s)"), levels[i], 1),
                                   k.ps[h][:, 3, 0:P].rearrange("p (n b) -> p n b", b=levels[i])).then_inc(tt_kept[h], 1)

                def keep_w(h, u, blk):
                    act.wait_ge(solved[h], u * 3 + (1 + 2 * blk))
                    nc.scalar.copy(wv[h][:, blk, :], k.ps[h][:, 2 + blk, 0:VE]).then_inc(w_kept[h], 1)

                def keep_mix(h, u):
                    act.wait_ge(mixed[h], u + 1)
                    nc.scalar.copy(oT[h][:, :, :], k.ps[h][:, 2, :].rearrange("p (m s) -> p m s", m=2))\
                        .then_inc(mix_kept[h], 1)

                def stage(h, grown, given, prepared, project):
                    g = 1 - h
                    for i in range(NL):
                        if given is not None and i == 0:
                            keep_w(g, given, 0)
                        if grown is not None and i > 0:
                            keep_tt(h, grown, i - 1)
                        if given is not None and i == 2:
                            keep_w(g, given, 1)
                        if prepared is not None and i == 2:
                            tanh_of(g, prepared, 0)
                            tanh_of(g, prepared, 1)
                        if prepared is not None and i == 3:
                            square(g, prepared)
                        if project is not None and i in (1, 3):
                            tap(h, project, i // 2)
                        if prepared is not None and i == 3:
                            decay(g, prepared)
                        if given is not None and i == 4:
                            keep_mix(g, given)
                    if grown is not None:
                        keep_tt(h, grown, NL - 1)
                    if prepared is not None:
                        scale_v(g, prepared)

                for part in range(2):
                    tap(0, 0, part)
                schedule(act, stage)

            @block.vector
            def _(dve):
                ch = Chain(dve, chain0, 0)
                dve.wait_ge(gates_ready, 1)
                zz = k.ps[0][:, 0, :].rearrange("p (t e) -> p t e", t=NT)
                ch.link(nc.vector.tensor_copy(za[:, :, :], zz[:, :, 0:HK]))
                nc.vector.scalar_tensor_tensor(zabs[:, :, 0:HK], zz[:, :, 0:HK], -1.0, za[:, :, :], ALU.mult, ALU.max)
                nc.vector.tensor_copy(zabs[:, :, HK:2 * HK], zz[:, :, HK:2 * HK]).then_inc(gates_abs, 1)
                dve.wait_ge(gates_exp, 1)
                ch.link(nc.vector.tensor_scalar(beta[:, :, :], zabs[:, :, HK:2 * HK], 1.0, None, ALU.add))
                ch.link(nc.vector.reciprocal(beta[:, :, :], beta[:, :, :]))
                dve.wait_ge(gates_log, 1)
                nc.vector.scalar_tensor_tensor(loga[:, :, :], za[:, :, :], 0.0, loga[:, :, :], ALU.min, ALU.subtract)\
                    .then_inc(loga_ready, 1)
                dve.wait_ge(cum_ready, 1)
                cp = k.ps[0][:, 1, 0:NT * HK].rearrange("p (t e) -> p t e", t=NT)
                nc.vector.tensor_scalar(negcum[:, :, :], cp, -1.0, None, ALU.mult)
                nc.vector.tensor_copy(cum[:, :, :], cp).then_inc(cum_kept, 1)
                dve.wait_ge(cum_kept, 1)

                def convolve(h, u, back, part):
                    if back == 1:
                        dve.wait_ge(tapped[h], u * 2 + (part + 1))
                    else:
                        dve.wait_ge(conv_part[h], u * (2 * (KC - 2)) + (2 * (back - 2) + part + 1))
                    for m in (2 * part, 2 * part + 1):
                        last = nc.vector.scalar_tensor_tensor(
                            y[h][:, m, back:S], k.ps[h][:, m // 2, (m % 2) * S:(m % 2 + 1) * S - back],
                            taps[h][:, m, KC - 1 - back:KC - back],
                            y[h][:, m, back:S], ALU.mult, ALU.add)
                    last.then_inc(conv_part[h] if back < KC - 1 else convolved[h], 1)

                def silu(h, u, part):
                    dve.wait_ge(tanh_done[h], u * 2 + (part + 1))
                    mm = slice(2 * part, 2 * part + 2)
                    nc.vector.scalar_tensor_tensor(z[h][:, mm, :], e[h][:, mm, :], 1.0, y[h][:, mm, :], ALU.add,
                                                   ALU.mult).then_inc(silu_done[h], 1)

                def keep_lengths(h, u):
                    dve.wait_ge(lengths[h], u + 1)
                    nc.vector.tensor_scalar(n2[h][:, :], k.ps[h][:, 1, S:S + 4], 4e-24, None, ALU.max)\
                        .then_inc(lengths_kept[h], 1)

                def scales(h, u):
                    dve.wait_ge(inverse_len[h], u + 1)
                    nc.vector.scalar_tensor_tensor(nk[h][:, :], n2[h][:, 0:TB], 0.5, rn[h][:, 0:TB], ALU.mult, ALU.mult)
                    nc.vector.tensor_copy(rq[h][:, ds(u % 2, 1), :].rearrange("p a t -> p (a t)"), rn[h][:, TB:2 * TB])
                    bt = beta[:, ds(batch(u) * TB, TB), ds(pair(u) * 2 + h, 1)].rearrange("p t a -> p (t a)")
                    nc.vector.tensor_tensor(cj[h][:, :], bt, rn[h][:, 0:TB], ALU.mult).then_inc(c_part[h], 1)
                    dve.wait_ge(c_part[h], u + 1)
                    nc.vector.tensor_tensor(cj[h][:, :], cj[h][:, :], rn[h][:, 0:TB], ALU.mult).then_inc(scales_ready[h], 1)

                def scale_products(h, u):
                    dve.wait_ge(scales_ready[h], u + 1)
                    dve.wait_ge(products[h], u + 1)
                    dve.wait_ge(decayed[h], u + 1)
                    nc.vector.scalar_tensor_tensor(lp0[h], k.ps[h][:, 0, :].rearrange("p (a s) -> p a s", a=2),
                                                   cj[h][:, 0:1], dec[h][:, 0:S].unsqueeze(1).to_broadcast([P, 2, S]),
                                                   ALU.mult, ALU.mult)
                    nc.vector.scalar_tensor_tensor(lp1[h], k.ps[h][:, 1, 0:S].rearrange("p (a s) -> p a s", a=2),
                                                   cj[h][:, 1:2], dec[h][:, S:S + P].unsqueeze(1).to_broadcast([P, 2, P]),
                                                   ALU.mult, ALU.mult).then_inc(lp_ready[h], 1)

                def first_inverse(h, u):
                    dve.wait_ge(lp_ready[h], u + 1)
                    nc.vector.tensor_tensor(ntm[h][:, :, :], lp[h][:, :, 0:P],
                                            negstrict[:, :].unsqueeze(1).to_broadcast([P, 2, P]), ALU.mult)\
                        .then_inc(nt_part[h], 1)
                    dve.wait_ge(nt_part[h], u * 2 + 1)
                    nc.vector.tensor_tensor(nt[h][:, :, :], ntm[h][:, :, :],
                                            k.ident[:, :].unsqueeze(1).to_broadcast([P, 2, P]), ALU.add)\
                        .then_inc(nt_part[h], 1)
                    dve.wait_ge(nt_part[h], u * 2 + 2)
                    nc.vector.tensor_tensor(tt[h][:, 1], nt[h][:, :, :],
                                            lvl1T[:, :].unsqueeze(1).to_broadcast([P, 2, P]), ALU.mult)\
                        .then_inc(nt_ready[h], 1)

                def keep_first(h, u):
                    dve.wait_ge(t_ready[h], u * NL + 1)
                    nc.vector.tensor_copy(tt[h][:, 0, :, :], k.ps[h][:, 2, 0:S].rearrange("p (b s) -> p b s", b=2))\
                        .then_inc(t_kept[h], 1)

                def keep_off(h, u, i):
                    b = levels[i]
                    dve.wait_ge(off_ready[h], u * NL + (i + 1))
                    for blk in range(2):
                        last = nc.vector.tensor_tensor(halves(off[h][:, i, blk, :], b, 0),
                                                       k.ps[h][:, 2, blk * HALF:(blk + 1) * HALF].rearrange("p (n b) -> p n b", b=b),
                                                       halves(lvl[:, i, :], b, 0), ALU.mult)
                    last.then_inc(off_kept[h], 1)

                def keep_t(h, u, i):
                    b = levels[i]
                    dve.wait_ge(t_ready[h], u * NL + (i + 2))
                    nc.vector.tensor_copy(halves(tt[h][:, 0, :, :].rearrange("p b s -> p (b s)"), b, 0),
                                          k.ps[h][:, 2, S:S + P].rearrange("p (n b) -> p n b", b=b)).then_inc(t_kept[h], 1)

                def keep_rest(h, u):
                    dve.wait_ge(solved[h], u * 3 + 2)
                    dve.wait_ge(v_scaled[h], u + 1)
                    nc.vector.tensor_tensor(rest[h][:, :], vs[h][:, 1, :], k.ps[h][:, 2, VE:2 * VE], ALU.subtract)\
                        .then_inc(rest_kept[h], 1)

                def add_out(h, u):
                    dve.wait_ge(out_ready[h], u + 1)
                    for t in range(TB):
                        xt = k.x[:, ds(batch(u) * TB + t, 1), :].rearrange("p a d -> p (a d)")
                        last = nc.vector.scalar_tensor_tensor(xt, k.ps[h][:, 3, t * D:(t + 1) * D],
                                                              rq[h][:, ds(u % 2, 1), t:t + 1].rearrange("p a t -> p (a t)"), xt, ALU.mult, ALU.add)
                    last.then_inc(added[h], 1)

                def stage(h, grown, given, prepared, project):
                    g = 1 - h
                    if grown is not None:
                        keep_first(h, grown)
                    for i in range(NL):
                        if grown is not None:
                            keep_off(h, grown, i)
                        if given is not None and i == 1:
                            keep_rest(g, given)
                        if prepared is not None and i < 2:
                            convolve(g, prepared, i + 2, 0)
                        if prepared is not None and i == 3:
                            silu(g, prepared, 1)
                        if project is not None and i == 3:
                            convolve(h, project, 1, 0)
                        if project is not None and i == 4:
                            convolve(h, project, 1, 1)
                        if prepared is not None and i == 4:
                            scales(g, prepared)
                        if prepared is not None and i == 5:
                            first_inverse(g, prepared)
                        if grown is not None and i < NL - 1:
                            keep_t(h, grown, i)
                        if prepared is not None and i < 2:
                            convolve(g, prepared, i + 2, 1)
                        if prepared is not None and i == 2:
                            silu(g, prepared, 0)
                        if prepared is not None and i == 3:
                            keep_lengths(g, prepared)
                        if prepared is not None and i == 4:
                            scale_products(g, prepared)
                        if given is not None and i == 5:
                            add_out(g, given)

                for part in range(2):
                    convolve(0, 0, 1, part)
                schedule(dve, stage)


class CrossRope:

    TWO_PI = (6.28125, 0.0019350051879882812, 3.019915981956753e-07)
    ROUND = 12582912.0

    def __init__(self, k, stack):
        nc, ins = k.nc, k.ins
        loaded, chain = k.sem("rope_loaded"), k.sem("rope_chain")
        reduced, sines = k.sem("rope_reduced"), k.sem("rope_sines")
        self.cq, self.sq_, self.ck, self.sk = [k.sb(f"rope_{n}", [P, NT, HD], F32, stack) for n in ("cq", "sq", "ck", "sk")]
        self.cc, self.sc = [k.sb(f"rope_{n}", [CTX, B, HD], F32, stack) for n in ("cc", "sc")]
        self.ctxT = k.sb("rope_ctxT", [P, DC, B * CTX], F32, stack)
        with ExitStack() as st:
            pos_i, cpos_i = k.sb("pos_i", [P, NT], I32, st), k.sb("cpos_i", [CTX, B], I32, st)
            pos, cpos = k.sb("pos", [P, NT], F32, st), k.sb("cpos", [CTX, B], F32, st)
            inv = k.sb("inv", [P, HALF], F32, st)
            wn = k.sb("wn", [P, 2, HD], F32, st)
            ang, turns, r, r2 = [k.sb(f"rope_t{i}", [P, NT, HALF], F32, st) for i in range(4)]
            cang, cturns, cr, cr2 = [k.sb(f"rope_u{i}", [CTX, B, HALF], F32, st) for i in range(4)]
            with nc.Block() as block:

                @block.sync
                def _(sp):
                    for dst, name in ((pos_i[:, :], "pos"), (cpos_i[:, :], "cpos")):
                        sp.dma_start(dst, ins[name]).then_inc(loaded, 16)
                    sp.dma_start(inv[:, :], ins["c_inv"]).then_inc(loaded, 16)
                    for i, name in enumerate(("w1xqn", "w1xkn")):
                        sp.dma_start(wn[:, i, :], ins[name].partition_broadcast(P)).then_inc(loaded, 16)
                    sp.dma_start(self.ctxT[:, :, :], ins["ctxT"].rearrange("(c p) n -> p c n", p=P)).then_inc(loaded, 16)
                    sp.wait_ge(loaded, 96)

                @block.scalar
                def _(act):
                    act.wait_ge(reduced, 1)
                    for a in (r, r2, cr, cr2):
                        last = nc.scalar.activation(a[:, :, :], a[:, :, :], ACT.Sin)
                    last.then_inc(sines, 1)

                @block.vector
                def _(dve):
                    ch = Chain(dve, chain, 0)
                    dve.wait_ge(loaded, 96)
                    for p_i, p_f, a, tu, rr, rh, m, rows in ((pos_i, pos, ang, turns, r, r2, NT, P),
                                                             (cpos_i, cpos, cang, cturns, cr, cr2, B, CTX)):
                        ch.link(nc.vector.tensor_copy(p_f[:, :], p_i[:, :]))
                        ch.link(nc.vector.tensor_tensor(a[:, :, :], inv[0:rows, :].unsqueeze(1).to_broadcast([rows, m, HALF]),
                                                        p_f[:, :].unsqueeze(2).to_broadcast([rows, m, HALF]), ALU.mult))
                        ch.link(nc.vector.tensor_scalar(tu[:, :, :], a[:, :, :], float(1 / (2 * np.pi)), self.ROUND,
                                                        ALU.mult, ALU.add))
                        ch.link(nc.vector.tensor_scalar(tu[:, :, :], tu[:, :, :], self.ROUND, None, ALU.subtract))
                        for part in self.TWO_PI:
                            ch.link(nc.vector.scalar_tensor_tensor(a[:, :, :], tu[:, :, :], -part, a[:, :, :], ALU.mult, ALU.add))
                        ch.link(nc.vector.tensor_scalar(rr[:, :, :], a[:, :, :], float(-np.float32(np.pi)),
                                                        3.1415925, ALU.max, ALU.min))
                        last = nc.vector.tensor_scalar(rh[:, :, :], rr[:, :, :], 0.5, None, ALU.mult)
                        ch.link(last)
                    dve.sem_inc(reduced, 1)
                    dve.wait_ge(sines, 1)
                    for rr, rh, m, rows, outs in ((r, r2, NT, P, ((self.cq, self.sq_, 0), (self.ck, self.sk, 1))),
                                                  (cr, cr2, B, CTX, ((self.cc, self.sc, 1),))):
                        ch.link(nc.vector.tensor_tensor(rh[:, :, :], rh[:, :, :], rh[:, :, :], ALU.mult))
                        ch.link(nc.vector.tensor_scalar(rh[:, :, :], rh[:, :, :], -2.0, 1.0, ALU.mult, ALU.add))
                        for co, si, i in outs:
                            for a0, b0, sign in ((0, HALF, -1.0), (HALF, 0, 1.0)):
                                wa = wn[0:rows, i:i + 1, a0:a0 + HALF].to_broadcast([rows, m, HALF])
                                wb = wn[0:rows, i:i + 1, b0:b0 + HALF].to_broadcast([rows, m, HALF])
                                nc.vector.tensor_tensor(co[:, :, a0:a0 + HALF], rh[:, :, :], wa, ALU.mult)
                                last = nc.vector.scalar_tensor_tensor(si[:, :, a0:a0 + HALF], rr[:, :, :], sign, wb,
                                                                      ALU.mult, ALU.mult)
                    ch.link(last)

    def q(self, p, h):
        return (t[:, ds(p * (2 * TB) + h * TB, TB), :] for t in (self.cq, self.sq_))

    def k(self, p, h):
        return (t[:, ds(p * (2 * TB) + h * TB, TB), :] for t in (self.ck, self.sk))

    def c(self, p, h):
        return (t[:, ds(p * 2 + h, 1), :].rearrange("p a d -> p (a d)") for t in (self.cc, self.sc))


E1, EK, TOPK1, I1, CAP = 128, 48, 8, 96, 96
SLOTS = EK * CAP
FAR = float(1 << 20)


def sparse_experts(k):
    nc, ins = k.nc, k.ins
    ZN = 4
    EU = 4
    loaded, chain = k.sem("sp_loaded"), k.sem("sp_chain")
    logits_ready, shifted, exps_done = k.sem("sp_logits"), k.sem("sp_shifted"), k.sem("sp_exps")
    chosen, before_ready, slots_ready = k.sem("sp_chosen"), k.sem("sp_before"), k.sem("sp_slots")
    zero_made, zeroed, scattered = k.sem("sp_zero_made"), k.sem("sp_zeroed"), k.sem("sp_scattered")
    in_loaded = [[k.sem(f"sp_in{q}{h}") for h in range(2)] for q in range(2)]
    turned, x_kept, up_ready = k.sems("sp_turned"), k.sems("sp_x_kept"), k.sems("sp_up_ready")
    silu_done, act_ready, down_ready = k.sems("sp_silu"), k.sems("sp_act"), k.sems("sp_down")
    y_kept, y_stored = k.sems("sp_y_kept"), k.sems("sp_y_stored")
    gathered = [k.sem(f"sp_gathered{h}") for h in range(2)]
    combined, out_stored = k.sem("sp_combined"), k.sem("sp_out_stored")
    add_chain = k.sem("sp_add_chain")
    xrows = nc.dram_tensor("slot_rows", (SLOTS, D), F32, kind="Internal").ap()
    yrows = nc.dram_tensor("slot_results", (SLOTS, D), F32, kind="Internal").ap()
    with ExitStack() as st:
        def sb(name, shape, dt=F32, stack=st):
            return k.sb(f"sp_{name}", shape, dt, stack)

        w = sb("w", [P, NT, TOPK1])
        slot_i = sb("slot_i", [P, NT, TOPK1], U32)
        zero = sb("zero", [P, SLOTS * D // P // ZN])
        wgu = [[sb(f"wgu{q}{h}", [P, EU * DC, 2 * I1]) for h in range(2)] for q in range(2)]
        wd = [[sb(f"wd{q}{h}", [I1, EU, D]) for h in range(2)] for q in range(2)]
        xs = [[sb(f"xs{q}{h}", [CAP, EU, D]) for h in range(2)] for q in range(2)]

        def load_weights(sp, q, h, e):
            sp.dma_start(wgu[q][h][:, :, :], ins["w1gu"][ds(e, EU)].rearrange("e (c p) n -> p (e c) n", p=P))\
                .then_inc(in_loaded[q][h], 16)
            sp.dma_start(wd[q][h][:, :, :], ins["w1d"][ds(e, EU)].rearrange("e p n -> p e n")).then_inc(in_loaded[q][h], 16)

        def load_slots(sp, q, h, e):
            sp.dma_start(xs[q][h][:, :, :], xrows.rearrange("(e c) d -> e c d", c=CAP)[ds(e, EU)]
                         .rearrange("e c d -> c e d")).then_inc(in_loaded[q][h], 16)

        with ExitStack() as st1:
            def sb1(name, shape, dt=F32):
                return sb(name, shape, dt, st1)

            gate = sb1("gate", [P, DC, E1])
            o2n_i, o2n = sb1("o2n_i", [P, E1], I32), sb1("o2n", [P, E1])
            neg, base = sb1("neg", [P, E1]), sb1("base", [P, E1])
            iota = sb1("iota", [P, E1])
            trib, onesb = sb1("trib", [P, P], BF16), sb1("onesb", [P, P], BF16)
            lg, left = sb1("lg", [P, NT, E1]), sb1("left", [P, NT, E1])
            best, at, atf = sb1("best", [P, NT, 8]), sb1("at", [P, NT, 8], U32), sb1("atf", [P, NT, 8])
            tot, rtot = sb1("tot", [P, NT]), sb1("rtot", [P, NT])
            m = sb1("m", [P, NT, E1], BF16)
            mc = sb1("mc", [P, NT, E1], BF16)
            far = sb1("far", [P, NT, E1])
            table = sb1("table", [P, NT, E1])
            junk = [sb1(f"junk{i}", [P, E1]) for i in range(TOPK1)]
            slot_f = sb1("slot_f", [P, NT, TOPK1])
            ok = sb1("ok", [P, NT, TOPK1])
            NB = NT * E1 // 512
            with nc.Block() as block:

                @block.sync
                def _(sp):
                    sp.dma_start(gate[:, :, :], ins["w1r"].rearrange("(c p) n -> p c n", p=P)).then_inc(loaded, 16)
                    sp.dma_start(o2n_i[:, :], ins["o2n"].partition_broadcast(P)).then_inc(loaded, 16)
                    sp.dma_start(iota[:, :], ins["c_iota"]).then_inc(loaded, 16)
                    sp.dma_start(trib[:, :], ins["c_trib"]).then_inc(loaded, 16)
                    sp.dma_start(onesb[:, :], ins["c_onesb"]).then_inc(loaded, 16)
                    sp.wait_ge(zero_made, 1)
                    for i in range(ZN):
                        sp.dma_start(xrows.rearrange("(i p a) d -> i p (a d)", i=ZN, p=P)[i], zero[:, :]).then_inc(zeroed, 16)
                    for q in range(2):
                        for h in range(2):
                            load_weights(sp, q, h, (2 * q + h) * EU)
                    sp.wait_ge(scattered, 16 * NT * TOPK1)

                @block.gpsimd
                def _(pool):
                    nc.gpsimd.memset(zero[:, :], 0.0).then_inc(zero_made, 1)
                    pool.wait_ge(zeroed, 16 * ZN)
                    for i in range(NT):
                        pool.wait_ge(slots_ready, i + 1)
                        for j in range(TOPK1):
                            nc.gpsimd.indirect_dma_start(
                                out=xrows, out_offset=bass.IndirectOffsetOnAxis(slot_i[:, i, j:j + 1], axis=0),
                                in_=k.xn_rows[:, i, :], in_offset=None, bounds_check=SLOTS - 1,
                                oob_is_err=False).then_inc(scattered, 16)
                    pool.wait_ge(scattered, 16 * NT * TOPK1)

                @block.tensor
                def _(pe):
                    pe.wait_ge(loaded, 80)
                    for i in range(NT):
                        for c in range(DC):
                            last = nc.tensor.matmul(k.ps[0][:, i // 4, (i % 4) * E1:(i % 4 + 1) * E1],
                                                    k.xnT[:, c, i * P:(i + 1) * P], gate[:, c, :], start=c == 0, stop=c == DC - 1)
                    last.then_inc(logits_ready, 1)
                    pe.wait_ge(chosen, 1)
                    for i in range(NT):
                        o = k.ps[1][:, i // 4, (i % 4) * E1:(i % 4 + 1) * E1]
                        last = nc.tensor.matmul(o, trib[:, :], m[:, i, :], start=True, stop=i == 0)
                        if i:
                            last = nc.tensor.matmul(o, onesb[:, :], mc[:, i - 1, :], start=False, stop=True)
                    last.then_inc(before_ready, 1)

                @block.scalar
                def _(act):
                    act.wait_ge(shifted, 1)
                    nc.scalar.activation(w[:, :, :], w[:, :, :], ACT.Exp).then_inc(exps_done, 1)

                @block.vector
                def _(dve):
                    ch = Chain(dve, chain, 0)
                    dve.wait_ge(loaded, 80)
                    ch.link(nc.vector.tensor_copy(o2n[:, :], o2n_i[:, :]))
                    nc.vector.tensor_scalar(neg[:, :], o2n[:, :], -1.0, NEG, ALU.is_equal, ALU.mult)
                    ch.link(nc.vector.tensor_scalar(junk[0][:, :], o2n[:, :], 0.0, FAR, ALU.is_lt, ALU.mult))
                    ch.link(nc.vector.scalar_tensor_tensor(base[:, :], o2n[:, :], float(CAP), junk[0][:, :], ALU.mult, ALU.add))
                    dve.wait_ge(logits_ready, 1)
                    ch.link(nc.vector.tensor_tensor(lg[:, :, :], k.ps[0][:, 0:NB, :].rearrange("p a (t e) -> p (a t) e", e=E1),
                                                    neg[:, :].unsqueeze(1).to_broadcast([P, NT, E1]), ALU.add))
                    for i in range(NT):
                        last = nc.vector.max(best[:, i, :], lg[:, i, :])
                    ch.link(last)
                    for i in range(NT):
                        last = nc.vector.max_index(at[:, i, :], best[:, i, :], lg[:, i, :])
                    for i in range(NT):
                        last = nc.vector.match_replace(out=left[:, i, :], in_to_replace=best[:, i, :], in_values=lg[:, i, :],
                                                       imm_value=2 * NEG)
                    ch.link(last)
                    nc.vector.tensor_tensor(w[:, :, :], best[:, :, :], best[:, :, 0:1].to_broadcast([P, NT, TOPK1]),
                                            ALU.subtract).then_inc(shifted, 1)
                    nc.vector.tensor_copy(atf[:, :, :], at[:, :, :])
                    ch.link(nc.vector.tensor_scalar(m[:, :, :], left[:, :, :], 2 * NEG, None, ALU.is_equal))
                    ch.link(nc.vector.tensor_copy(mc[:, 0, :], m[:, 0, :]))
                    for i in range(1, NT):
                        ch.link(nc.vector.tensor_tensor(mc[:, i, :], mc[:, i - 1, :], m[:, i, :], ALU.add))
                    dve.sem_inc(chosen, 1)
                    dve.wait_ge(before_ready, 1)
                    before = k.ps[1][:, 0:NB, :].rearrange("p a (t e) -> p (a t) e", e=E1)
                    nc.vector.tensor_scalar(far[:, :, :], before, CAP - 0.5, FAR, ALU.is_gt, ALU.mult)
                    ch.link(nc.vector.tensor_tensor(table[:, :, :], before,
                                                    base[:, :].unsqueeze(1).to_broadcast([P, NT, E1]), ALU.add))
                    ch.link(nc.vector.tensor_tensor(table[:, :, :], table[:, :, :], far[:, :, :], ALU.add))
                    for i in range(NT):
                        for j in range(TOPK1):
                            last = nc.vector.scalar_tensor_tensor(junk[j][:, :], iota[:, :], atf[:, i, j:j + 1], table[:, i, :],
                                                                  ALU.is_equal, ALU.mult, accum_out=slot_f[:, i, j:j + 1])
                        ch.link(last)
                        nc.vector.tensor_copy(slot_i[:, i, :], slot_f[:, i, :]).then_inc(slots_ready, 1)
                    dve.wait_ge(exps_done, 1)
                    ch.link(nc.vector.tensor_reduce(tot[:, :], w[:, :, :], AX_X, ALU.add))
                    ch.link(nc.vector.reciprocal(rtot[:, :], tot[:, :]))
                    nc.vector.tensor_scalar(ok[:, :, :], slot_f[:, :, :], SLOTS - 0.5, None, ALU.is_lt)
                    ch.link(nc.vector.tensor_tensor(w[:, :, :], w[:, :, :], rtot[:, :].unsqueeze(2).to_broadcast([P, NT, TOPK1]),
                                                    ALU.mult))
                    ch.link(nc.vector.tensor_tensor(w[:, :, :], w[:, :, :], ok[:, :, :], ALU.mult))

        xT = [sb(f"xT{h}", [P, 2, 4 * CAP]) for h in range(2)]
        sg = [sb(f"sg{h}", [I1, EU, CAP]) for h in range(2)]
        hT = [sb(f"hT{h}", [I1, EU, CAP]) for h in range(2)]
        y = [sb(f"y{h}", [CAP, EU, D]) for h in range(2)]
        UN = EK // EU // 4
        with nc.Block() as block:

            @block.sync
            def _(sp):
                for q in range(2):
                    for h in range(2):
                        load_slots(sp, q, h, (2 * q + h) * EU)
                with sp.Fori(1, UN) as j:
                    for q in range(2):
                        for h in range(2):
                            sp.wait_ge(down_ready[h], j * 2 + (q - 1))
                            load_slots(sp, q, h, j * (4 * EU) + (2 * q + h) * EU)
                            load_weights(sp, q, h, j * (4 * EU) + (2 * q + h) * EU)

            @block.tensor
            def _(pe):
                with pe.Fori(0, UN) as j:
                    for q in range(2):
                        n = j * 2 + (q + 1)
                        for h in range(2):
                            pe.wait_ge(in_loaded[q][h], (j + 1) * 48)
                            if q == 1:
                                pe.wait_ge(y_kept[h], n - 1)
                            for e in range(EU):
                                for c in range(DC):
                                    last = nc.tensor.transpose(
                                        k.ps[h][:, e // 2, (e % 2 * 2 + c) * CAP:(e % 2 * 2 + c + 1) * CAP],
                                        xs[q][h][:, e, c * P:(c + 1) * P], k.ident[0:CAP, 0:CAP])
                            last.then_inc(turned[h], 1)
                        for h in range(2):
                            pe.wait_ge(x_kept[h], n)
                            for e in range(EU):
                                for gu in range(2):
                                    for c in range(DC):
                                        last = nc.tensor.matmul(
                                            k.ps[h][0:I1, 2 + e // 2, (e % 2 * 2 + gu) * CAP:(e % 2 * 2 + gu + 1) * CAP],
                                            wgu[q][h][:, e * DC + c, gu * I1:(gu + 1) * I1],
                                            xT[h][:, e // 2, (e % 2 * 2 + c) * CAP:(e % 2 * 2 + c + 1) * CAP],
                                            start=c == 0, stop=c == DC - 1)
                            last.then_inc(up_ready[h], 1)
                        for h in range(2):
                            pe.wait_ge(act_ready[h], n)
                            for e in range(EU):
                                last = nc.tensor.matmul(k.ps[h][0:CAP, e // 2, (e % 2) * D:(e % 2 + 1) * D], hT[h][:, e, :],
                                                        wd[q][h][:, e, :], start=True, stop=True)
                            last.then_inc(down_ready[h], 1)
                        if q == 1:
                            for h in range(2):
                                pe.wait_ge(y_kept[h], n)

            @block.scalar
            def _(act):
                for h in range(2):
                    act.sem_inc(y_stored[h], 16)
                with act.Fori(0, UN) as j:
                    for q in range(2):
                        n = j * 2 + (q + 1)
                        for h in range(2):
                            act.wait_ge(turned[h], n)
                            nc.scalar.copy(xT[h][:, :, :], k.ps[h][:, 0:2, 0:4 * CAP]).then_inc(x_kept[h], 1)
                        for h in range(2):
                            act.wait_ge(up_ready[h], n)
                            nc.scalar.activation(sg[h][:, :, :].rearrange("p (a b) c -> p a b c", a=2),
                                                 k.ps[h][0:I1, 2:4, 0:4 * CAP].rearrange("p a (b g c) -> p a b g c", b=2, g=2)[:, :, :, 0],
                                                 ACT.Silu).then_inc(silu_done[h], 1)
                        for h in range(2):
                            act.wait_ge(y_kept[h], n)
                            act.dma_start(yrows.rearrange("(e c) d -> e c d", c=CAP)[ds(j * (4 * EU) + (2 * q + h) * EU, EU)]
                                          .rearrange("e c d -> c e d"), y[h][:, :, :]).then_inc(y_stored[h], 16)
                for h in range(2):
                    act.wait_ge(y_stored[h], 16 * 2 * UN + 16)

            @block.vector
            def _(dve):
                with dve.Fori(0, UN) as j:
                    for q in range(2):
                        n = j * 2 + (q + 1)
                        for h in range(2):
                            dve.wait_ge(silu_done[h], n)
                            nc.vector.tensor_tensor(hT[h][:, :, :].rearrange("p (a b) c -> p a b c", a=2),
                                                    sg[h][:, :, :].rearrange("p (a b) c -> p a b c", a=2),
                                                    k.ps[h][0:I1, 2:4, 0:4 * CAP].rearrange("p a (b g c) -> p a b g c", b=2, g=2)[:, :, :, 1],
                                                    ALU.mult).then_inc(act_ready[h], 1)
                        for h in range(2):
                            dve.wait_ge(down_ready[h], n)
                            dve.wait_ge(y_stored[h], n * 16)
                            nc.vector.tensor_copy(y[h][:, :, :].rearrange("p (a b) d -> p a b d", a=2),
                                                  k.ps[h][0:CAP, 0:2, :].rearrange("p a (b d) -> p a b d", b=2))\
                                .then_inc(y_kept[h], 1)

        NG = 2
        back = [sb(f"back{i}", [P, TOPK1, D]) for i in range(NG)]
        with nc.Block() as block:

            @block.gpsimd
            def _(pool):
                for i in range(NG):
                    nc.gpsimd.memset(back[i][:, :, :], 0.0).then_inc(zero_made, 1)
                pool.wait_ge(zero_made, 1 + NG)
                for i in range(NT):
                    if i >= NG:
                        pool.wait_ge(combined, i - NG + 1)
                    for j in range(TOPK1):
                        nc.gpsimd.indirect_dma_start(
                            out=back[i % NG][:, j, :], out_offset=None, in_=yrows,
                            in_offset=bass.IndirectOffsetOnAxis(slot_i[:, i, j:j + 1], axis=0),
                            bounds_check=SLOTS - 1, oob_is_err=False).then_inc(gathered[i % NG], 16)

            @block.vector
            def _(dve):
                ch = Chain(dve, add_chain, 0)
                for i in range(NT):
                    dve.wait_ge(gathered[i % NG], 16 * TOPK1 * (i // NG + 1))
                    for j in range(TOPK1):
                        ins_ = nc.vector.scalar_tensor_tensor(k.x[:, i, :], back[i % NG][:, j, :], w[:, i, j:j + 1], k.x[:, i, :],
                                                              ALU.mult, ALU.add)
                        if j < TOPK1 - 1:
                            ch.link(ins_)
                    ins_.then_inc(combined, 1)

            @block.sync
            def _(sp):
                for i in range(NT):
                    sp.wait_ge(combined, i + 1)
                    sp.dma_start(k.out[i // TB, (i % TB) * P:(i % TB + 1) * P, :], k.x[:, i, :]).then_inc(out_stored, 16)
                sp.wait_ge(out_stored, 16 * NT)


class SelfRope:

    def __init__(self, k, stack):
        self.cos = k.sb("rope_cos", [P, TB, HD], F32, stack)
        self.sin = k.sb("rope_sin", [P, TB, HD], F32, stack)
        loaded = k.sem("rope_loaded")
        with k.nc.Block() as block:

            @block.sync
            def _(sp):
                for t, name in ((self.cos, "c_cos"), (self.sin, "c_sin")):
                    sp.dma_start(t[:, :, :], k.ins[name].rearrange("(t p) d -> p t d", p=P)).then_inc(loaded, 16)
                sp.wait_ge(loaded, 32)

    def q(self, p, h):
        return self.cos[:, :, :], self.sin[:, :, :]

    def k(self, p, h):
        return self.cos[:, :, :], self.sin[:, :, :]


def build(nc, ins, out):
    with ExitStack() as stack:
        k = Core(nc, ins, out, stack)
        load_constants(k)
        with ExitStack() as st, k.own_semaphores("_0"):
            rope = SelfRope(k, st)
            weights = AttentionWeights(k, ("w0q", "w0kv", "w0o"), st)
            layernorm(k)
            attention(k, weights, rope, None)
        layernorm(k)
        with k.own_semaphores(""):
            set_attention(k)
        layernorm(k)
        with k.own_semaphores(""):
            experts(k)
        layernorm(k)
        with k.own_semaphores(""):
            delta_attention(k)
        with ExitStack() as st, k.own_semaphores("_1"):
            weights = AttentionWeights(k, ("w1xq", "w1xkv", "w1xo"), st)
            rope = CrossRope(k, st)
            layernorm(k)
            attention(k, weights, rope, rope)
        with ExitStack() as st, k.own_semaphores(""):
            k.xn_rows = k.sb("xn_rows", [P, NT, D], F32, st)
            layernorm(k, k.xn_rows)
            sparse_experts(k)


def constants():
    c = {}
    c["c_ident"] = np.eye(P, dtype=np.float32)
    bf = mybir.dt.np(BF16)
    c["c_identb"] = np.eye(P).astype(bf)
    c["c_causb"] = np.triu(np.full((P, P), NEG), 1).astype(bf)
    inv = (np.float32(1.0) / np.float32(10000.0) ** (np.arange(0, HD, 2, dtype=np.float32) / np.float32(HD))).astype(np.float32)
    ang = (np.arange(S, dtype=np.float32)[:, None] * inv[None, :]).astype(np.float32)
    co, si = np.cos(ang), np.sin(ang)
    c["c_cos"] = np.concatenate([co, co], 1).astype(np.float32)
    c["c_sin"] = np.concatenate([-si, si], 1).astype(np.float32)
    c["c_iota"] = np.broadcast_to(np.arange(P, dtype=np.float32), (P, P))
    j, i = np.arange(P)[:, None], np.arange(P)[None, :]
    c["c_inv"] = np.broadcast_to(inv, (P, HALF))
    c["c_onesb"] = np.ones((P, P)).astype(bf)
    c["c_trib"] = (j < i).astype(bf)
    c["c_ones"] = np.ones((P, P), np.float32)
    c["c_tri"] = (j <= i).astype(np.float32)
    c["c_negstrict"] = np.where(i > j, -1.0, 0.0).astype(np.float32)
    c["c_maskadd"] = np.where(i < j, NEG, 0.0).astype(np.float32)
    lv = {n: ((i == j) | ((i // (2 * n) == j // (2 * n)) & (j // n % 2 == 1) & (i // n % 2 == 0))).astype(np.float32)
          for n in (1, 2, 4, 8, 16, 32, 64)}
    c["c_level1T"] = np.ascontiguousarray(lv[1].T)
    c["c_levels"] = np.ascontiguousarray(np.stack([lv[n] for n in (2, 4, 8, 16, 32, 64)], 1))
    return c


def heads_kv(wk, wv):
    return np.stack([wk.reshape(D, KVH, HD), wv.reshape(D, KVH, HD)], 2).reshape(D, -1)


def kernel(**inputs):
    import concourse.bacc as bacc
    from concourse.bass_utils import run_bass_kernel_spmd as run

    a = {n: np.asarray(v) for n, v in inputs.items()}
    arrays = {"x": a["x"]}
    arrays["w0q"] = a["L0_attn_Wq"]
    arrays["w0kv"] = heads_kv(a["L0_attn_Wk"], a["L0_attn_Wv"])
    arrays["w0o"] = a["L0_attn_Wo"]
    arrays["w0xq"] = a["L0_xattn_W_q"].T
    arrays["w0xb"] = a["L0_xattn_b_q"].reshape(DC, P).T
    arrays["w0xd"] = a["L0_xattn_desc_router"].T
    arrays["ctx"] = a["ctx_2048"]
    arrays["sets"] = a["itok_Sx4_0_63"]
    arrays["w0r"] = a["L0_ffn_router_w"].T
    arrays["w0rb"] = a["L0_ffn_expert_bias"]
    arrays["w0gu"] = np.concatenate([a["L0_ffn_gate_proj"], a["L0_ffn_up_proj"]], 2)
    arrays["w0d"] = a["L0_ffn_down_proj"]
    by_head = lambda m, w: np.moveaxis(m.reshape(m.shape[0], HK, w), 1, 0)
    arrays["w1kqv"] = np.concatenate([by_head(a["L1_attn_Wk"], P), by_head(a["L1_attn_Wq"], P),
                                      by_head(a["L1_attn_Wv"], VE)], 2)
    arrays["w1o"] = a["L1_attn_Wo"].reshape(HK, VE, D)
    arrays["w1ab"] = np.concatenate([a["L1_attn_Wa"], a["L1_attn_Wb"]], 1)
    feats = lambda kf, qf, vf: np.moveaxis(np.concatenate(
        [kf.reshape(HK, 1, P, -1), qf.reshape(HK, 1, P, -1), vf.reshape(HK, 2, P, -1)], 1), 2, 1)
    arrays["w1t"] = np.concatenate([feats(a["L1_attn_kcw"], a["L1_attn_qcw"], a["L1_attn_vcw"]),
                                    feats(a["L1_attn_kcb"], a["L1_attn_qcb"], a["L1_attn_vcb"])], 3)
    arrays["w1xq"] = a["L1_xattn_Wq"].T
    arrays["w1xkv"] = heads_kv(a["L1_xattn_Wk"].T, a["L1_xattn_Wv"].T)
    arrays["w1xo"] = a["L1_xattn_Wo"].T
    arrays["w1xqn"], arrays["w1xkn"] = a["L1_xattn_q_norm_w"], a["L1_xattn_k_norm_w"]
    arrays["ctxT"] = a["ctx_2048"].reshape(B * CTX, D).T
    arrays["pos"] = a["itok_BxS_4096_4607"].reshape(NT, P).T
    arrays["cpos"] = a["pos_BxS2"].T
    arrays["w1r"] = a["L1_ffn_gate_weight"].T
    arrays["w1gu"] = np.moveaxis(a["L1_ffn_gate_up_proj"], 2, 1)
    arrays["w1d"] = np.moveaxis(a["L1_ffn_down_proj"], 2, 1)
    arrays["o2n"] = a["L1_ffn_old_to_new"]
    arrays.update(constants())
    nc = bacc.Bacc("TRN2", target_bir_lowering=False, num_devices=1)
    ins = {}
    for n, v in arrays.items():
        arrays[n] = np.ascontiguousarray(v)
        ins[n] = nc.dram_tensor(f"in_{n}", v.shape, mybir.dt.from_np(v.dtype), kind="ExternalInput").ap()
    out = nc.dram_tensor("out_dram", (B, S, D), F32, kind="ExternalOutput").ap()
    build(nc, ins, out)
    r = run(nc, [{f"in_{n}": v for n, v in arrays.items()}], core_ids=[0])
    return r.results[0]["out_dram"]
```
